# Optimizing a Trainium2 kernel written in Bass

```python
import numpy as np
import jax
import jax.numpy as jnp

def _softmax(x, axis=-1):
    return jax.nn.softmax(x, axis=axis)

def _gelu(x):
    return jax.nn.gelu(x, approximate=True)

def _silu(x):
    return jax.nn.silu(x)

def _sigmoid(x):
    return jax.nn.sigmoid(x)

def _layernorm(x, axis=-1, eps=1e-05):
    m = jnp.mean(x, axis=axis, keepdims=True)
    v = jnp.var(x, axis=axis, keepdims=True)
    return (x - m) / jnp.sqrt(v + eps)

def _scatter_add(tgt, idx, src, axis=0):
    return tgt.at[idx].add(src)

def _segment_sum(src, seg, n):
    return jax.ops.segment_sum(src, seg, n)
kernel_name = 'mk_xattn_ffn_d2_seqx_r4_91e8bc'

def setup_inputs(seed: int=0):
    np.random.seed(seed)
    _w = jnp.asarray

    def _rec_inputs():
        import jax
        import jax.numpy as jnp
        _rk = jax.random.key(seed)
        x = 2.818e-05 + 1 * jax.random.normal(jax.random.fold_in(_rk, 1), (4, 512, 512), jnp.float32)
        _lenS = 512 - jax.random.randint(jax.random.fold_in(_rk, 7), (4,), 0, max(1, 512 // 4) + 1, jnp.int32)
        _lenS2 = 512 - jax.random.randint(jax.random.fold_in(_rk, 8), (4,), 0, max(1, 512 // 4) + 1, jnp.int32)
        _ctx_1024P = jax.random.normal(jax.random.fold_in(_rk, 11), (4, 16, 256), jnp.float32)
        _ctx_1024c = jax.random.dirichlet(jax.random.fold_in(_rk, 511), 0.3 * jnp.ones((16,), jnp.float32), (4, 512))
        _ctx_1024t = jnp.einsum('bsk,bkd->bsd', _ctx_1024c, _ctx_1024P)
        _ctx_1024t = _ctx_1024t * jax.lax.rsqrt(jnp.mean(jnp.square(_ctx_1024t)) + 1e-12) * 0.953939
        ctx_1024 = 7.22013e-05 + 1.00017 * (_ctx_1024t + 0.3 * jax.random.normal(jax.random.fold_in(_rk, 611), (4, 512, 256), jnp.float32))
        return (x, ctx_1024)
    x, ctx_1024 = _rec_inputs()

    def _L0_xattn_setup():
        import jax, jax.numpy as jnp
        import numpy as np
        B_, L_, D_MODEL = (4, 512, 256)
        D_STATE, D_CONV, EXPAND = (16, 4, 2)
        D_INNER = EXPAND * D_MODEL
        DT_RANK = (D_MODEL + 15) // 16

        def silu(x):
            return x * jax.nn.sigmoid(x)
        key = jax.random.key(seed)
        ks = jax.random.split(key, 10)
        f32 = jnp.float32
        hidden_states = jax.random.normal(ks[0], (B_, L_, D_MODEL), dtype=f32)
        z = jax.random.normal(ks[1], (B_, D_INNER, L_), dtype=f32)
        in_proj_w = jax.random.normal(ks[2], (D_INNER, D_MODEL), dtype=f32) * 0.02
        conv_w = jax.random.normal(ks[3], (D_INNER, 1, D_CONV), dtype=f32) * 0.1
        conv_b = jax.random.normal(ks[4], (D_INNER,), dtype=f32) * 0.02
        x_proj_w = jax.random.normal(ks[5], (DT_RANK + 2 * D_STATE, D_INNER), dtype=f32) * 0.02
        dt_proj_w = jax.random.uniform(ks[6], (D_INNER, DT_RANK), dtype=f32, minval=-DT_RANK ** (-0.5), maxval=DT_RANK ** (-0.5))
        dt = jnp.exp(jax.random.uniform(ks[7], (D_INNER,), dtype=f32, minval=np.log(0.001), maxval=np.log(0.1)))
        dt_proj_b = jnp.log(jnp.expm1(dt))
        A_log = jnp.log(jnp.broadcast_to(jnp.arange(1, D_STATE + 1, dtype=f32), (D_INNER, D_STATE)))
        D = jnp.ones((D_INNER,), f32)
        return {'hidden_states': hidden_states, 'z': z, 'in_proj_w': in_proj_w, 'conv_w': conv_w, 'conv_b': conv_b, 'x_proj_w': x_proj_w, 'dt_proj_w': dt_proj_w, 'dt_proj_b': dt_proj_b, 'A_log': A_log, 'D': D}
    _L0_xattn_all = _L0_xattn_setup()
    _L0_xattn_in = {k: v for k, v in _L0_xattn_all.items() if k in ('in_proj_w', 'conv_w', 'conv_b', 'x_proj_w', 'dt_proj_w', 'dt_proj_b', 'A_log', 'D')}
    del _L0_xattn_all

    def _L0_ffn_setup():
        import jax, jax.numpy as jnp
        import numpy as np
        B, S, H = (1, 256, 512)
        E, K = (32, 4)
        F, FS = (352, 1408)
        CAP = 64

        def silu(x):
            return x * jax.nn.sigmoid(x)
        key = jax.random.key(seed)
        ks = jax.random.split(key, 9)
        sc = 0.02
        return {'hidden_states': jax.random.normal(ks[0], (B, S, H), jnp.float32), 'Wr': jax.random.normal(ks[1], (H, E), jnp.float32) * sc, 'Wg': jax.random.normal(ks[2], (E, H, F), jnp.float32) * sc, 'Wu': jax.random.normal(ks[3], (E, H, F), jnp.float32) * sc, 'Wd': jax.random.normal(ks[4], (E, F, H), jnp.float32) * sc, 'Wsg': jax.random.normal(ks[5], (H, FS), jnp.float32) * sc, 'Wsu': jax.random.normal(ks[6], (H, FS), jnp.float32) * sc, 'Wsd': jax.random.normal(ks[7], (FS, H), jnp.float32) * sc, 'Wse': jax.random.normal(ks[8], (H, 1), jnp.float32) * sc}
    _L0_ffn_all = _L0_ffn_setup()
    _L0_ffn_in = {k: v for k, v in _L0_ffn_all.items() if k in ('Wr', 'Wg', 'Wu', 'Wd', 'Wsg', 'Wsu', 'Wsd', 'Wse')}
    del _L0_ffn_all

    def _L1_xattn_setup():
        import jax, jax.numpy as jnp
        import numpy as np
        B, S1, S2, DCA = (2, 512, 256, 16)
        QDIM, KDIM, H = (512, 256, 16)
        HD = QDIM // H
        SCALE = HD ** (-0.5)
        EPS = 1e-06
        DCA_WEIGHT = 1.0

        def _ln(t, w, b):
            m = jnp.mean(t, axis=-1, keepdims=True)
            v = jnp.var(t, axis=-1, keepdims=True)
            return (t - m) * jax.lax.rsqrt(v + EPS) * w + b

        def _attn(q, k, v):
            s = jnp.einsum('bhqd,bhkd->bhqk', q, k) * SCALE
            p = jax.nn.softmax(s, axis=-1)
            return jnp.einsum('bhqk,bhkd->bhqd', p, v)
        key = jax.random.key(seed)
        ks = jax.random.split(key, 8)
        w = lambda k, shape: jax.random.normal(k, shape, jnp.float32) * 0.02
        return {'x': jax.random.normal(ks[0], (B, S1, QDIM), jnp.float32), 'y': jax.random.normal(ks[1], (B, S2 + DCA, KDIM), jnp.float32), 'Wq': w(ks[2], (QDIM, QDIM)), 'bq': jnp.zeros((QDIM,), jnp.float32), 'Wk': w(ks[3], (KDIM, QDIM)), 'bk': jnp.zeros((QDIM,), jnp.float32), 'Wv': w(ks[4], (KDIM, QDIM)), 'bv': jnp.zeros((QDIM,), jnp.float32), 'Wkv_dca': w(ks[5], (KDIM, 2 * QDIM)), 'bkv_dca': jnp.zeros((2 * QDIM,), jnp.float32), 'qn_w': jnp.ones((HD,), jnp.float32), 'qn_b': jnp.zeros((HD,), jnp.float32), 'kn_w': jnp.ones((HD,), jnp.float32), 'kn_b': jnp.zeros((HD,), jnp.float32), 'kn_dca_w': jnp.ones((HD,), jnp.float32), 'kn_dca_b': jnp.zeros((HD,), jnp.float32), 'Wo': w(ks[6], (QDIM, QDIM)), 'bo': jnp.zeros((QDIM,), jnp.float32)}
    _L1_xattn_all = _L1_xattn_setup()
    _L1_xattn_in = {k: v for k, v in _L1_xattn_all.items() if k in ('Wq', 'bq', 'Wk', 'bk', 'Wv', 'bv', 'Wkv_dca', 'bkv_dca', 'qn_w', 'qn_b', 'kn_w', 'kn_b', 'kn_dca_w', 'kn_dca_b', 'Wo', 'bo')}
    del _L1_xattn_all

    def _L1_ffn_setup():
        import jax, jax.numpy as jnp
        import numpy as np
        B, S, H = (2, 512, 512)
        E, G, TKG, K = (32, 8, 4, 8)
        I, SI = (256, 512)
        ROUTED_SCALE = 2.5

        def _moe_forward(hidden_states, router_w, router_bias, w_gate, w_up, w_down, sw_gate, sw_up, sw_down):
            x = hidden_states.reshape(-1, H)
            T = x.shape[0]
            logits = x.astype(jnp.float32) @ router_w.astype(jnp.float32)
            scores = jax.nn.sigmoid(logits)
            scores_grouped = (scores + router_bias).reshape(T, G, E // G)
            top2, _ = jax.lax.top_k(scores_grouped, 2)
            group_scores = top2.sum(-1)
            _, top_groups = jax.lax.top_k(group_scores, TKG)
            mask = jnp.ones((T, G), bool).at[jnp.arange(T)[:, None], top_groups].set(False)
            masked = jnp.where(mask[:, :, None], 0.0, scores_grouped).reshape(T, E)
            _, top_k_index = jax.lax.top_k(masked, K)
            tkw = jnp.take_along_axis(scores, top_k_index, axis=-1)
            tkw = tkw / tkw.sum(-1, keepdims=True)
            tkw = (tkw * ROUTED_SCALE).astype(hidden_states.dtype)
            flat_idx = top_k_index.reshape(-1)
            sort_idx = jnp.argsort(flat_idx)
            xs = jnp.repeat(x, K, axis=0)[sort_idx]
            group_sizes = jnp.bincount(flat_idx, length=E).astype(jnp.int32)
            gate = jax.lax.ragged_dot(xs, w_gate, group_sizes)
            up = jax.lax.ragged_dot(xs, w_up, group_sizes)
            down = jax.lax.ragged_dot(jax.nn.silu(gate) * up, w_down, group_sizes)
            unsort = jnp.argsort(sort_idx)
            routed = (down[unsort].reshape(T, K, H) * tkw[..., None]).sum(axis=1)
            shared = jax.nn.silu(x @ sw_gate) * (x @ sw_up) @ sw_down
            return (routed + shared).reshape(hidden_states.shape)
        key = jax.random.key(seed)
        ks = jax.random.split(key, 9)

        def w(k, shape, fan_in):
            return jax.random.normal(k, shape, jnp.float32) / np.float32(np.sqrt(fan_in))
        return dict(hidden_states=jax.random.normal(ks[0], (B, S, H), jnp.float32), router_w=w(ks[1], (H, E), H), router_bias=jnp.zeros((E,), jnp.float32), w_gate=w(ks[2], (E, H, I), H), w_up=w(ks[3], (E, H, I), H), w_down=w(ks[4], (E, I, H), I), sw_gate=w(ks[5], (H, SI), H), sw_up=w(ks[6], (H, SI), H), sw_down=w(ks[7], (SI, H), SI))
    _L1_ffn_all = _L1_ffn_setup()
    _L1_ffn_in = {k: v for k, v in _L1_ffn_all.items() if k in ('router_w', 'router_bias', 'w_gate', 'w_up', 'w_down', 'sw_gate', 'sw_up', 'sw_down')}
    del _L1_ffn_all
    return {'x': x, 'ctx_1024': ctx_1024, 'L0_xattn_in_proj_w': _L0_xattn_in['in_proj_w'], 'L0_xattn_conv_w': _L0_xattn_in['conv_w'], 'L0_xattn_conv_b': _L0_xattn_in['conv_b'], 'L0_xattn_x_proj_w': _L0_xattn_in['x_proj_w'], 'L0_xattn_dt_proj_w': _L0_xattn_in['dt_proj_w'], 'L0_xattn_dt_proj_b': _L0_xattn_in['dt_proj_b'], 'L0_xattn_A_log': _L0_xattn_in['A_log'], 'L0_xattn_D': _L0_xattn_in['D'], 'L0_ffn_Wr': _L0_ffn_in['Wr'], 'L0_ffn_Wg': _L0_ffn_in['Wg'], 'L0_ffn_Wu': _L0_ffn_in['Wu'], 'L0_ffn_Wd': _L0_ffn_in['Wd'], 'L0_ffn_Wsg': _L0_ffn_in['Wsg'], 'L0_ffn_Wsu': _L0_ffn_in['Wsu'], 'L0_ffn_Wsd': _L0_ffn_in['Wsd'], 'L0_ffn_Wse': _L0_ffn_in['Wse'], 'L1_xattn_Wq': _L1_xattn_in['Wq'], 'L1_xattn_bq': _L1_xattn_in['bq'], 'L1_xattn_Wk': _L1_xattn_in['Wk'], 'L1_xattn_bk': _L1_xattn_in['bk'], 'L1_xattn_Wv': _L1_xattn_in['Wv'], 'L1_xattn_bv': _L1_xattn_in['bv'], 'L1_xattn_Wkv_dca': _L1_xattn_in['Wkv_dca'], 'L1_xattn_bkv_dca': _L1_xattn_in['bkv_dca'], 'L1_xattn_qn_w': _L1_xattn_in['qn_w'], 'L1_xattn_qn_b': _L1_xattn_in['qn_b'], 'L1_xattn_kn_w': _L1_xattn_in['kn_w'], 'L1_xattn_kn_b': _L1_xattn_in['kn_b'], 'L1_xattn_kn_dca_w': _L1_xattn_in['kn_dca_w'], 'L1_xattn_kn_dca_b': _L1_xattn_in['kn_dca_b'], 'L1_xattn_Wo': _L1_xattn_in['Wo'], 'L1_xattn_bo': _L1_xattn_in['bo'], 'L1_ffn_router_w': _L1_ffn_in['router_w'], 'L1_ffn_router_bias': _L1_ffn_in['router_bias'], 'L1_ffn_w_gate': _L1_ffn_in['w_gate'], 'L1_ffn_w_up': _L1_ffn_in['w_up'], 'L1_ffn_w_down': _L1_ffn_in['w_down'], 'L1_ffn_sw_gate': _L1_ffn_in['sw_gate'], 'L1_ffn_sw_up': _L1_ffn_in['sw_up'], 'L1_ffn_sw_down': _L1_ffn_in['sw_down']}

def reference(x, ctx_1024, L0_xattn_in_proj_w, L0_xattn_conv_w, L0_xattn_conv_b, L0_xattn_x_proj_w, L0_xattn_dt_proj_w, L0_xattn_dt_proj_b, L0_xattn_A_log, L0_xattn_D, L0_ffn_Wr, L0_ffn_Wg, L0_ffn_Wu, L0_ffn_Wd, L0_ffn_Wsg, L0_ffn_Wsu, L0_ffn_Wsd, L0_ffn_Wse, L1_xattn_Wq, L1_xattn_bq, L1_xattn_Wk, L1_xattn_bk, L1_xattn_Wv, L1_xattn_bv, L1_xattn_Wkv_dca, L1_xattn_bkv_dca, L1_xattn_qn_w, L1_xattn_qn_b, L1_xattn_kn_w, L1_xattn_kn_b, L1_xattn_kn_dca_w, L1_xattn_kn_dca_b, L1_xattn_Wo, L1_xattn_bo, L1_ffn_router_w, L1_ffn_router_bias, L1_ffn_w_gate, L1_ffn_w_up, L1_ffn_w_down, L1_ffn_sw_gate, L1_ffn_sw_up, L1_ffn_sw_down):
    import jax
    import jax.numpy as jnp

    def _L0_xattn_ref(hidden_states, z, in_proj_w, conv_w, conv_b, x_proj_w, dt_proj_w, dt_proj_b, A_log, D):
        import jax, jax.numpy as jnp
        import numpy as np
        B_, L_, D_MODEL = (4, 512, 256)
        D_STATE, D_CONV, EXPAND = (16, 4, 2)
        D_INNER = EXPAND * D_MODEL
        DT_RANK = (D_MODEL + 15) // 16

        def silu(x):
            return x * jax.nn.sigmoid(x)
        Bsz, L, _ = hidden_states.shape
        d_inner, _, d_conv = conv_w.shape
        dt_rank = dt_proj_w.shape[1]
        d_state = A_log.shape[1]
        x = jnp.einsum('bld,ed->bel', hidden_states, in_proj_w)
        xc = jax.lax.conv_general_dilated(x, conv_w, window_strides=(1,), padding=[(d_conv - 1, 0)], feature_group_count=d_inner, dimension_numbers=('NCH', 'OIH', 'NCH'))
        x = silu(xc + conv_b[None, :, None])
        x_dbl = jnp.einsum('bdl,ed->bel', x, x_proj_w)
        dt_low, Bm, Cm = jnp.split(x_dbl, [dt_rank, dt_rank + d_state], axis=1)
        dt = jnp.einsum('brl,dr->bdl', dt_low, dt_proj_w)
        dt = jax.nn.softplus(dt + dt_proj_b[None, :, None])
        A = -jnp.exp(A_log)
        dt_t = jnp.moveaxis(dt, -1, 0)
        B_t = jnp.moveaxis(Bm, -1, 0)
        C_t = jnp.moveaxis(Cm, -1, 0)
        u_t = jnp.moveaxis(x, -1, 0)

        def step(state, inp):
            d, b, c, u = inp
            dA = jnp.exp(d[..., None] * A)
            state = state * dA + (d * u)[..., None] * b[:, None, :]
            y = jnp.einsum('bdn,bn->bd', state, c)
            return (state, y)
        state0 = jnp.zeros((Bsz, d_inner, d_state), x.dtype)
        _, ys = jax.lax.scan(step, state0, (dt_t, B_t, C_t, u_t))
        y = jnp.moveaxis(ys, 0, 2)
        y = y + D[None, :, None] * x
        y = y * silu(z)
        return jnp.swapaxes(y, 1, 2)

    def _L0_ffn_ref(hidden_states, Wr, Wg, Wu, Wd, Wsg, Wsu, Wsd, Wse):
        import jax, jax.numpy as jnp
        import numpy as np
        B, S, H = (1, 256, 512)
        E, K = (32, 4)
        F, FS = (352, 1408)
        CAP = 64

        def silu(x):
            return x * jax.nn.sigmoid(x)
        b, s_len, h = hidden_states.shape
        x = hidden_states.reshape(-1, h)
        T = x.shape[0]
        probs = jax.nn.softmax(x @ Wr, axis=-1)
        topw, topi = jax.lax.top_k(probs, K)
        topw = topw / jnp.sum(topw, axis=-1, keepdims=True)
        shared = silu(x @ Wsg) * (x @ Wsu) @ Wsd
        shared = shared * jax.nn.sigmoid(x @ Wse)
        sel = topi.reshape(-1)
        w = topw.reshape(-1)
        tok = jnp.repeat(jnp.arange(T), K)
        oh = jax.nn.one_hot(sel, E, dtype=jnp.int32)
        pos = (jnp.cumsum(oh, axis=0) * oh).sum(-1) - 1
        valid = (pos < CAP).astype(x.dtype)
        posc = jnp.clip(pos, 0, CAP - 1)
        xe = jnp.zeros((E, CAP, h), x.dtype).at[sel, posc].add(x[tok] * valid[:, None])
        g = silu(jnp.einsum('ech,ehf->ecf', xe, Wg))
        u = jnp.einsum('ech,ehf->ecf', xe, Wu)
        ye = jnp.einsum('ecf,efh->ech', g * u, Wd)
        y_pair = ye[sel, posc] * (w * valid)[:, None]
        out = shared.at[tok].add(y_pair)
        return out.reshape(b, s_len, h)

    def _L1_xattn_ref(x, y, Wq, bq, Wk, bk, Wv, bv, Wkv_dca, bkv_dca, qn_w, qn_b, kn_w, kn_b, kn_dca_w, kn_dca_b, Wo, bo):
        import jax, jax.numpy as jnp
        import numpy as np
        B, S1, S2, DCA = (2, 512, 256, 16)
        QDIM, KDIM, H = (512, 256, 16)
        HD = QDIM // H
        SCALE = HD ** (-0.5)
        EPS = 1e-06
        DCA_WEIGHT = 1.0

        def _ln(t, w, b):
            m = jnp.mean(t, axis=-1, keepdims=True)
            v = jnp.var(t, axis=-1, keepdims=True)
            return (t - m) * jax.lax.rsqrt(v + EPS) * w + b

        def _attn(q, k, v):
            s = jnp.einsum('bhqd,bhkd->bhqk', q, k) * SCALE
            p = jax.nn.softmax(s, axis=-1)
            return jnp.einsum('bhqk,bhkd->bhqd', p, v)
        b, s1, _ = x.shape
        y_dca = y[:, -DCA:, :]
        y_main = y[:, :-DCA, :]
        kv_dca = (y_dca @ Wkv_dca + bkv_dca).reshape(b, DCA, 2, H, HD)
        k_dca = _ln(kv_dca[:, :, 0], kn_dca_w, kn_dca_b)
        v_dca = kv_dca[:, :, 1]
        s2 = y_main.shape[1]
        q = _ln((x @ Wq + bq).reshape(b, s1, H, HD), qn_w, qn_b)
        kv = jnp.concatenate([y_main @ Wk + bk, y_main @ Wv + bv], axis=-1)
        kv = kv.reshape(b, s2, H, 2 * HD)
        k = _ln(kv[..., :HD], kn_w, kn_b)
        v = kv[..., HD:]
        qT = q.transpose(0, 2, 1, 3)
        ctx = _attn(qT, k.transpose(0, 2, 1, 3), v.transpose(0, 2, 1, 3))
        ctx = ctx.transpose(0, 2, 1, 3).reshape(b, s1, QDIM)
        ctx_dca = _attn(qT, k_dca.transpose(0, 2, 1, 3), v_dca.transpose(0, 2, 1, 3))
        ctx_dca = ctx_dca.transpose(0, 2, 1, 3).reshape(b, s1, QDIM)
        ctx = ctx + DCA_WEIGHT * ctx_dca
        return ctx @ Wo + bo

    def _L1_ffn_ref(hidden_states, router_w, router_bias, w_gate, w_up, w_down, sw_gate, sw_up, sw_down):
        import jax, jax.numpy as jnp
        import numpy as np
        B, S, H = (2, 512, 512)
        E, G, TKG, K = (32, 8, 4, 8)
        I, SI = (256, 512)
        ROUTED_SCALE = 2.5

        def _moe_forward(hidden_states, router_w, router_bias, w_gate, w_up, w_down, sw_gate, sw_up, sw_down):
            x = hidden_states.reshape(-1, H)
            T = x.shape[0]
            logits = x.astype(jnp.float32) @ router_w.astype(jnp.float32)
            scores = jax.nn.sigmoid(logits)
            scores_grouped = (scores + router_bias).reshape(T, G, E // G)
            top2, _ = jax.lax.top_k(scores_grouped, 2)
            group_scores = top2.sum(-1)
            _, top_groups = jax.lax.top_k(group_scores, TKG)
            mask = jnp.ones((T, G), bool).at[jnp.arange(T)[:, None], top_groups].set(False)
            masked = jnp.where(mask[:, :, None], 0.0, scores_grouped).reshape(T, E)
            _, top_k_index = jax.lax.top_k(masked, K)
            tkw = jnp.take_along_axis(scores, top_k_index, axis=-1)
            tkw = tkw / tkw.sum(-1, keepdims=True)
            tkw = (tkw * ROUTED_SCALE).astype(hidden_states.dtype)
            flat_idx = top_k_index.reshape(-1)
            sort_idx = jnp.argsort(flat_idx)
            xs = jnp.repeat(x, K, axis=0)[sort_idx]
            group_sizes = jnp.bincount(flat_idx, length=E).astype(jnp.int32)
            gate = jax.lax.ragged_dot(xs, w_gate, group_sizes)
            up = jax.lax.ragged_dot(xs, w_up, group_sizes)
            down = jax.lax.ragged_dot(jax.nn.silu(gate) * up, w_down, group_sizes)
            unsort = jnp.argsort(sort_idx)
            routed = (down[unsort].reshape(T, K, H) * tkw[..., None]).sum(axis=1)
            shared = jax.nn.silu(x @ sw_gate) * (x @ sw_up) @ sw_down
            return (routed + shared).reshape(hidden_states.shape)
        return _moe_forward(hidden_states, router_w, router_bias, w_gate, w_up, w_down, sw_gate, sw_up, sw_down)
    x = x + _L0_xattn_ref(ctx_1024, _layernorm(x, axis=-1), L0_xattn_in_proj_w, L0_xattn_conv_w, L0_xattn_conv_b, L0_xattn_x_proj_w, L0_xattn_dt_proj_w, L0_xattn_dt_proj_b, L0_xattn_A_log, L0_xattn_D)
    x = x + _L0_ffn_ref(_layernorm(x, axis=-1), L0_ffn_Wr, L0_ffn_Wg, L0_ffn_Wu, L0_ffn_Wd, L0_ffn_Wsg, L0_ffn_Wsu, L0_ffn_Wsd, L0_ffn_Wse)
    x = x + _L1_xattn_ref(_layernorm(x, axis=-1), ctx_1024, L1_xattn_Wq, L1_xattn_bq, L1_xattn_Wk, L1_xattn_bk, L1_xattn_Wv, L1_xattn_bv, L1_xattn_Wkv_dca, L1_xattn_bkv_dca, L1_xattn_qn_w, L1_xattn_qn_b, L1_xattn_kn_w, L1_xattn_kn_b, L1_xattn_kn_dca_w, L1_xattn_kn_dca_b, L1_xattn_Wo, L1_xattn_bo)
    x = x + _L1_ffn_ref(_layernorm(x, axis=-1), L1_ffn_router_w, L1_ffn_router_bias, L1_ffn_w_gate, L1_ffn_w_up, L1_ffn_w_down, L1_ffn_sw_gate, L1_ffn_sw_up, L1_ffn_sw_down)
    return x

_drawn_inputs = setup_inputs


def setup_inputs(seed=0):
    import zlib

    import numpy as np

    out = dict(_drawn_inputs(seed))
    spreads = {'L0_xattn_D': (1.0, 0.6),
     'L1_xattn_bq': (0.0, 0.1),
     'L1_xattn_bk': (0.0, 0.1),
     'L1_xattn_bv': (0.0, 0.1),
     'L1_xattn_bkv_dca': (0.0, 0.1),
     'L1_xattn_qn_w': (1.0, 0.2),
     'L1_xattn_qn_b': (0.0, 0.289),
     'L1_xattn_kn_w': (1.0, 0.2),
     'L1_xattn_kn_b': (0.0, 0.8),
     'L1_xattn_kn_dca_w': (1.0, 0.2),
     'L1_xattn_kn_dca_b': (0.0, 0.8),
     'L1_xattn_bo': (0.0, 0.1),
     'L1_ffn_router_bias': (0.0, 0.1)}
    factors = {'L0_xattn_x_proj_w': 8.0,
     'L0_xattn_dt_proj_w': 8.0,
     'L0_xattn_dt_proj_b': 8.0,
     'L0_xattn_A_log': 8.0}
    for name, (base, spread) in spreads.items():
        noise = np.random.default_rng([zlib.crc32(name.encode()), seed]).standard_normal(out[name].shape)
        drawn = base * np.exp(spread * noise) if base else spread * noise
        out[name] = jnp.asarray(drawn.astype(out[name].dtype))
    for name, factor in factors.items():
        out[name] = (out[name] * factor).astype(out[name].dtype)
    return out
```

```python
from contextlib import ExitStack

import numpy as np

import concourse.bass as bass
from concourse import mybir

F32 = mybir.dt.float32
BF16 = mybir.dt.bfloat16
I32 = mybir.dt.int32
ALU = mybir.AluOpType
ACT = mybir.ActivationFunctionType
AX_X = mybir.AxisListType.X

P = 128
B, S, H = 4, 512, 512
T = B * S
NT = T // P
TB = S // P
KH = H // P
DM = 256
KC = DM // P
LN_EPS = 1e-5

NST, RK, CONV = 16, 16, 4
XD = RK + 2 * NST

E = 32
F0, FS0, CAP, K0 = 352, 1408, 64, 4
F1, FS1, K1 = 256, 512, 8
GR, GSEL = 8, 4
ROUTED = 2.5
NSLOT0 = E * CAP
NTILE1 = T * K1 // P + E
NSLOT1 = NTILE1 * P
SKIP = 1 << 20

NH, HD = 16, 32
DCA = 16
S2 = S - DCA
HG = 4
NG = NH // HG
GW = HG * HD
SCALE = float(HD) ** -0.5
HEAD_EPS = 1e-6


def bc(ap, axis, n):
    u = ap.unsqueeze(axis)
    shape = list(u.shape)
    shape[axis] = n
    return u.to_broadcast(shape)


def hold(eng, sem, value, held):
    eng.wait_ge(sem, value)
    eng.sem_inc(held, 1)


class Pools:

    def __init__(self, nc, ctx):
        self.nc, self.ctx, self.sems, self.from0 = nc, ctx, [], []

    def sb(self, name, shape, dt=F32):
        return self.ctx.enter_context(self.nc.sbuf_tensor(name, shape, dt))

    def ps(self, name, shape):
        return self.ctx.enter_context(self.nc.psum_tensor(name, shape, F32))

    def sem(self, name):
        self.sems.append(self.nc.alloc_semaphore(name))
        return self.sems[-1]

    def sem0(self, name):
        self.from0.append(self.sem(name))
        return self.from0[-1]

    def start_at_one(self):
        for i, s in enumerate(s for s in self.sems if s not in self.from0):
            (self.nc.gpsimd, self.nc.vector, self.nc.scalar, self.nc.sync)[i % 4].sem_inc(s, 1)
        self.nc.all_engine_barrier()

    def clear(self):
        self.nc.clear_and_free_semaphores(self.sems)
        self.nc.all_engine_barrier()


def constants(nc, pl, c):
    c["ident"] = pl.sb("ident", [P, P])
    c["zeros"] = pl.sb("zeros", [P, 2 * H])
    c["ones_bf"] = pl.sb("ones_bf", [P, P], BF16)
    c["before_bf"] = pl.sb("before_bf", [P, P], BF16)
    c["ones_row"] = pl.sb("ones_row", [1, P])
    c["seg"] = pl.sb("seg", [P, TB * E])
    c["slot0"] = pl.sb("slot0", [P, E])
    c["tile_no"] = pl.sb("tile_no", [P, 2])
    c["minus_half"] = pl.sb("minus_half", [P, E])
    c["half_seg8"] = pl.sb("half_seg8", [P, TB * GR])
    tri_all = pl.sb("tri_all", [P, P])
    idx_i = pl.sb("idx_i", [P, E], I32)
    tile_i = pl.sb("tile_i", [P, 2], I32)
    made, filled, cast = pl.sem("const_made"), pl.sem("const_filled"), pl.sem("const_cast")
    c["held"] = pl.sem("held")
    with nc.Block() as block:

        @block.gpsimd
        def _(pool):
            pool.memset(c["ident"][:, :], 0.0).then_inc(filled, 1)
            pool.memset(tri_all[:, :], 1.0).then_inc(filled, 1)
            pool.memset(c["seg"][:, :], 1.0).then_inc(filled, 1)
            pool.memset(c["half_seg8"][:, :], 1.0).then_inc(filled, 1)
            pool.memset(c["zeros"][:, :], 0.0).then_inc(filled, 1)
            pool.memset(c["ones_bf"][:, :], 1.0).then_inc(filled, 1)
            pool.memset(c["ones_row"][:, :], 1.0).then_inc(filled, 1)
            pool.memset(c["minus_half"][:, :], -0.5).then_inc(filled, 1)
            pool.iota(idx_i[:, :], [[CAP, E]], base=1, channel_multiplier=0).then_inc(filled, 1)
            pool.iota(tile_i[:, :], [[1, 2]], base=0, channel_multiplier=2).then_inc(filled, 1)
            pool.wait_ge(filled, 10)
            pool.affine_select(out=c["ident"][:, :], in_=c["ident"][:, :], compare_op=ALU.not_equal, fill=1.0,
                               base=0, pattern=[[-1, P]], channel_multiplier=1).then_inc(made, 1)
            pool.affine_select(out=tri_all[:, :], in_=tri_all[:, :], compare_op=ALU.is_gt, fill=0.0,
                               base=0, pattern=[[1, P]], channel_multiplier=-1).then_inc(made, 1)
            seg = c["seg"][:, :].rearrange("p (t e) -> p t e", e=E)
            pool.memset(seg[:, :, 0], 0.0).then_inc(made, 1)
            seg8 = c["half_seg8"][:, :].rearrange("p (t e) -> p t e", e=GR)
            pool.memset(seg8[:, :, 0], 0.0).then_inc(made, 1)

        @block.vector
        def _(dve):
            dve.wait_ge(made, 4)
            dve.wait_ge(filled, 10)
            dve.tensor_copy(c["before_bf"][:, :], tri_all[:, :]).then_inc(cast, 1)
            dve.tensor_copy(c["slot0"][:, :], idx_i[:, :]).then_inc(cast, 1)
            dve.tensor_copy(c["tile_no"][:, :], tile_i[:, :]).then_inc(cast, 1)


def mamba_stage(nc, pl0, c, I, D, x):
    with ExitStack() as ctx:
        pl = Pools(nc, ctx)
        ctx.callback(pl.clear)
        w_in = pl.sb("w_in", [P, KC, H])
        w_xp = pl.sb("w_xp", [P, KH, XD])
        w_dt = pl.sb("w_dt", [RK, H])
        conv_w = pl.sb("conv_w", [P, TB, CONV])
        conv_b = pl.sb("conv_b", [P, TB])
        dt_b = pl.sb("dt_b", [P, TB])
        a_log = pl.sb("a_log", [P, NST, TB])
        a_neg = pl.sb("a_neg", [P, NST, TB])
        d_col = pl.sb("d_col", [P, TB])
        d_diag = pl.sb("d_diag", [P, TB, P])
        ctxT = pl.sb("ctxT", [P, KC, S])
        xpad = pl.sb("xpad", [P, TB, S + CONV - 1])
        conv = pl.sb("conv", [P, TB, S])
        u = pl.sb("u", [P, TB, S])
        xd = pl.sb("xd", [XD, S])
        dt = pl.sb("dt", [P, TB, S])
        du = pl.sb("du", [P, TB, S])
        tmp = pl.sb("tmp", [P, TB, S])
        gate = pl.sb("gate", [P, TB, S])
        dA = pl.sb("dA", [P, 2, TB, S])
        dBu = pl.sb("dBu", [P, TB, S])
        hs = pl.sb("hs", [P, 2, TB, S])
        hc = pl.sb("hc", [P, 2, TB, S])
        bcst = pl.sb("bcst", [P, 2, 2, S])
        st = pl.sb("st", [P, TB, 6])
        mv = pl.sb("mv", [P, TB, 2])
        ve = pl.sb("ve", [P, TB])
        rs = pl.sb("rs", [P, TB])
        nb = pl.sb("nb", [P, TB])
        ps_y = pl.ps("ps_y", [P, TB, S])
        ps_w = pl.ps("ps_w", [P, TB, S])

        sem = {n: pl.sem("m_" + n) for n in (
            "weights", "xin", "ctxin", "pad", "aexp", "aneg", "diag", "inproj", "xpadc", "conv", "u", "xproj", "xdc",
            "bcout", "bcin0", "bcin1", "bfree", "cfree", "dtmm", "spa", "spb", "spc", "spd", "spe", "spm", "dt", "du",
            "dA", "dAfree", "dBu", "scan", "hsfree", "hc", "hcfree", "seed",
            "stats", "ve", "rs", "nb", "gate", "yz", "tr", "xadd")}
        sem["zfill"] = pl.sem0("m_zfill")
        bcin = (sem["bcin0"], sem["bcin1"])
        n_weights = 8
        n_zero = (NSLOT0 + NSLOT1) // (2 * P)

        pl.start_at_one()
        with nc.Block() as block:

            @block.sync
            def _(sp):
                for dst, src in ((w_in[:, :, :], I["in_projT"].rearrange("(k p) n -> p k n", p=P)),
                                 (w_xp[:, :, :], I["x_projT"].rearrange("(k p) n -> p k n", p=P)),
                                 (w_dt[:, :], I["dt_projT"]),
                                 (conv_w[:, :, :], I["conv_w"].rearrange("(t p) j -> p t j", p=P)),
                                 (conv_b[:, :], I["conv_b"]), (dt_b[:, :], I["dt_b"]),
                                 (a_log[:, :, :], I["a_log"].rearrange("p (n t) -> p n t", t=TB)),
                                 (d_col[:, :], I["d_col"])):
                    sp.dma_start(dst, src).then_inc(sem["weights"], 16)
                sp.dma_start(x[:, :, :], I["x"].rearrange("(t p) h -> p t h", p=P)).then_inc(sem["xin"], 16)
                with sp.Fori(0, B) as b:
                    hold(sp, sem["inproj"], 1 + TB * b, c["held"])
                    sp.dma_start(ctxT[:, :, :], I["ctxT"][:, bass.ds(b * S, S)].rearrange("(k p) n -> p k n", p=P))\
                      .then_inc(sem["ctxin"], 16)
                    hold(sp, sem["xdc"], 1 + b + 1, c["held"])
                    sp.dma_start(D["bc"][bass.ds(b * 2 * NST, 2 * NST), :], xd[RK:XD, :]).then_inc(sem["bcout"], 16)
                    with sp.Fori(0, NST // 2) as n2:
                        for q in range(2):
                            hold(sp, sem["bcout"], 1 + 16 * (b + 1), c["held"])
                            hold(sp, sem["bfree"], 1 + b * NST + n2 * 2 + q + 1, c["held"])
                            hold(sp, sem["cfree"], 1 + b * NST + n2 * 2 + q + 1, c["held"])
                            for w in range(2):
                                row = D["bc"][bass.ds(b * 2 * NST + w * NST + n2 * 2 + q, 1), :]
                                sp.dma_start(bcst[:, q, w, :], row.to_broadcast([P, S])).then_inc(bcin[q], 16)

            @block.gpsimd
            def _(pool):
                pool.sem_inc(sem["cfree"], 2)
                for buf, rows in ((D["xs1"], NSLOT1), (D["xs0"], NSLOT0)):
                    with pool.Fori(0, rows // (2 * P)) as i:
                        pool.dma_start(buf[bass.ds(i * 2 * P, 2 * P), :].rearrange("(p a) h -> p (a h)", a=2),
                                       c["zeros"][:, :]).then_inc(sem["zfill"], 16)
                with pool.Fori(0, B) as b:
                    pool.wait_ge(sem["ve"], 1 + b + 1)
                    pool.tensor_tensor(rs[:, :], ve[:, :], c["minus_half"][:, 0:TB], ALU.pow).then_inc(sem["rs"], 1)
                    with pool.Fori(0, NST // 2) as n2:
                        for q in range(2):
                            it = b * NST + n2 * 2 + q
                            pool.wait_ge(bcin[q], 1 + 32 * (b * (NST // 2) + n2 + 1))
                            pool.wait_ge(sem["scan"], 1 + it + 1)
                            pool.wait_ge(sem["hcfree"], 1 + it + 1)
                            pool.tensor_tensor(hc[:, q, :, :], hs[:, q, :, :], bc(bcst[:, q, 1, :], 1, TB), ALU.mult)\
                                .then_inc(sem["hc"], 1)
                            pool.wait_ge(sem["hc"], 1 + it + 1)
                            pool.sem_inc(sem["cfree"], 1)
                            pool.sem_inc(sem["hsfree"], 1)
                pool.wait_ge(sem["zfill"], 16 * n_zero)

            @block.scalar
            def _(act):
                act.wait_ge(sem["weights"], 1 + 16 * n_weights)
                act.activation(a_neg[:, :, :], a_log[:, :, :], ACT.Exp).then_inc(sem["aexp"], 1)
                with act.Fori(0, B) as b:
                    for t in range(TB):
                        act.wait_ge(sem["inproj"], 1 + TB * b + t + 1)
                        act.wait_ge(sem["conv"], 1 + TB * b)
                        act.wait_ge(sem["pad"], 1 + 1)
                        act.activation(xpad[:, t, CONV - 1:], ps_w[:, t, :], ACT.Copy).then_inc(sem["xpadc"], 1)
                    act.wait_ge(sem["yz"], 1 + b)
                    for t in range(TB):
                        act.wait_ge(sem["conv"], 1 + TB * b + t + 1)
                        act.activation(u[:, t, :], conv[:, t, :], ACT.Silu, bias=conv_b[:, t:t + 1]).then_inc(sem["u"], 1)
                    for t in range(TB):
                        act.wait_ge(sem["dtmm"], 1 + TB * b + t + 1)
                        act.activation(tmp[:, t, :], ps_w[:, t, :], ACT.Abs, bias=dt_b[:, t:t + 1]).then_inc(sem["spa"], 1)
                    act.wait_ge(sem["spa"], 1 + TB * (b + 1))
                    act.activation(tmp[:, :, :], tmp[:, :, :], ACT.Exp, scale=-1.0).then_inc(sem["spb"], 1)
                    act.wait_ge(sem["spc"], 1 + b + 1)
                    act.activation(gate[:, :, :], conv[:, :, :], ACT.Ln).then_inc(sem["spd"], 1)
                    act.wait_ge(sem["dt"], 1 + b + 1)
                    act.wait_ge(sem["nb"], 1 + b + 1)
                    for t in range(TB):
                        act.activation(gate[:, t, :], x[:, b * TB + t, :], ACT.Silu, scale=rs[:, t:t + 1],
                                       bias=nb[:, t:t + 1]).then_inc(sem["gate"], 1)
                    act.wait_ge(sem["aneg"], 1 + 1)
                    with act.Fori(0, NST // 2) as n2:
                        for q in range(2):
                            act.wait_ge(sem["dAfree"], 1 + b * NST + n2 * 2 + q + 1)
                            for t in range(TB):
                                i = act.activation(dA[:, q, t, 1:], dt[:, t, 1:], ACT.Exp,
                                                   scale=a_neg[:, n2 * 2 + q, t:t + 1])
                            i.then_inc(sem["dA"], 1)

            @block.vector
            def _(dve):
                dve.sem_inc(sem["bfree"], 2)
                dve.sem_inc(sem["dAfree"], 2)
                dve.sem_inc(sem["hsfree"], 2)
                dve.memset(xpad[:, :, 0:CONV - 1], 0.0).then_inc(sem["pad"], 1)
                dve.memset(dA[:, :, :, 0:1], 0.0).then_inc(sem["diag"], 1)
                dve.wait_ge(sem["aexp"], 1 + 1)
                dve.tensor_scalar(a_neg[:, :, :], a_neg[:, :, :], -1.0, None, ALU.mult).then_inc(sem["aneg"], 1)
                for t in range(TB):
                    dve.tensor_scalar(d_diag[:, t, :], c["ident"][:, :], d_col[:, t:t + 1], None, ALU.mult)\
                       .then_inc(sem["diag"], 1)
                dve.wait_ge(sem["xin"], 1 + 16)
                dve.wait_ge(sem["diag"], 1 + 1)
                with dve.Fori(0, B) as b:
                    for t in range(TB):
                        dve.wait_ge(sem["xpadc"], 1 + TB * b + t + 1)
                        dve.tensor_scalar(conv[:, t, :], xpad[:, t, 0:S], conv_w[:, t, 0:1], None, ALU.mult)\
                           .then_inc(sem["spe"], 1)
                        for j in range(1, CONV):
                            dve.wait_ge(sem["spe"], 1 + (TB * b + t) * (CONV - 1) + j)
                            dve.scalar_tensor_tensor(out=conv[:, t, :], in0=xpad[:, t, j:j + S],
                                                     scalar=conv_w[:, t, j:j + 1], in1=conv[:, t, :],
                                                     op0=ALU.mult, op1=ALU.add)\
                               .then_inc(sem["spe"] if j < CONV - 1 else sem["conv"], 1)
                    for t in range(TB):
                        dve.bn_stats(st[:, t, :], x[:, b * TB + t, :]).then_inc(sem["stats"], 1)
                    hold(dve, sem["stats"], 1 + 2 * TB * b + TB, c["held"])
                    for t in range(TB):
                        dve.bn_aggr(mv[:, t, :], st[:, t, :]).then_inc(sem["stats"], 1)
                    dve.wait_ge(sem["stats"], 1 + 2 * TB * (b + 1))
                    dve.tensor_scalar(ve[:, :], mv[:, :, 1], LN_EPS, None, ALU.add).then_inc(sem["ve"], 1)
                    dve.wait_ge(sem["xproj"], 1 + b + 1)
                    dve.tensor_copy(xd[:, :], ps_w[0:XD, 0, :]).then_inc(sem["xdc"], 1)
                    dve.wait_ge(sem["rs"], 1 + b + 1)
                    dve.scalar_tensor_tensor(out=nb[:, :], in0=mv[:, :, 0], scalar=-1.0, in1=rs[:, :],
                                             op0=ALU.mult, op1=ALU.mult).then_inc(sem["nb"], 1)
                    for t in range(TB):
                        dve.wait_ge(sem["spa"], 1 + TB * b + t + 1)
                        dve.tensor_scalar(dt[:, t, :], ps_w[:, t, :], dt_b[:, t:t + 1], 0.0, ALU.add, ALU.max)\
                           .then_inc(sem["spm"], 1)
                    dve.wait_ge(sem["spb"], 1 + b + 1)
                    dve.wait_ge(sem["u"], 1 + TB * (b + 1))
                    dve.tensor_scalar(conv[:, :, :], tmp[:, :, :], 1.0, None, ALU.add).then_inc(sem["spc"], 1)
                    dve.wait_ge(sem["spd"], 1 + b + 1)
                    dve.scalar_tensor_tensor(out=tmp[:, :, :], in0=conv[:, :, :], scalar=-1.0, in1=tmp[:, :, :],
                                             op0=ALU.add, op1=ALU.subtract).then_inc(sem["du"], 1)
                    dve.wait_ge(sem["du"], 1 + 4 * b + 1)
                    dve.tensor_tensor(tmp[:, :, :], gate[:, :, :], tmp[:, :, :], ALU.subtract).then_inc(sem["du"], 1)
                    dve.wait_ge(sem["du"], 1 + 4 * b + 2)
                    dve.tensor_tensor(dt[:, :, :], dt[:, :, :], tmp[:, :, :], ALU.add).then_inc(sem["dt"], 1)
                    dve.wait_ge(sem["dt"], 1 + b + 1)
                    dve.tensor_tensor(du[:, :, :], dt[:, :, :], u[:, :, :], ALU.mult).then_inc(sem["du"], 1)
                    dve.wait_ge(sem["du"], 1 + 4 * b + 3)
                    dve.sem_inc(sem["du"], 1)
                    with dve.Fori(0, NST // 2) as n2:
                        for q in range(2):
                            it = b * NST + n2 * 2 + q
                            dve.wait_ge(bcin[q], 1 + 32 * (b * (NST // 2) + n2 + 1))
                            dve.tensor_tensor(dBu[:, :, :], du[:, :, :], bc(bcst[:, q, 0, :], 1, TB), ALU.mult)\
                               .then_inc(sem["dBu"], 1)
                            dve.wait_ge(sem["dBu"], 1 + it + 1)
                            dve.sem_inc(sem["bfree"], 1)
                            dve.wait_ge(sem["dA"], 1 + it + 1)
                            dve.wait_ge(sem["hsfree"], 1 + it + 1)
                            flat = "p t s -> p (t s)"
                            dve.tensor_tensor_scan(hs[:, q, :, :].rearrange(flat), dA[:, q, :, :].rearrange(flat),
                                                   dBu[:, :, :].rearrange(flat), 0.0, ALU.mult, ALU.add)\
                               .then_inc(sem["scan"], 1)
                            dve.wait_ge(sem["scan"], 1 + it + 1)
                            dve.sem_inc(sem["dAfree"], 1)
                    dve.wait_ge(sem["hcfree"], 1 + NST * (b + 1) + 2)
                    dve.wait_ge(sem["gate"], 1 + TB * (b + 1))
                    dve.tensor_tensor(gate[:, :, :], ps_y[:, :, :], gate[:, :, :], ALU.mult).then_inc(sem["yz"], 1)
                    dve.wait_ge(sem["tr"], 1 + b + 1)
                    xb = x[:, bass.ds(b * TB, TB), :]
                    dve.tensor_tensor(xb, ps_w[:, :, :], xb, ALU.add).then_inc(sem["xadd"], 1)

            @block.tensor
            def _(pe):
                pe.sem_inc(sem["hcfree"], 2)
                pe.wait_ge(sem["weights"], 1 + 16 * n_weights)
                pe.wait_ge(sem["diag"], 1 + 1 + TB)
                with pe.Fori(0, B) as b:
                    pe.wait_ge(sem["ctxin"], 1 + 16 * (b + 1))
                    pe.wait_ge(sem["xadd"], 1 + b)
                    for t in range(TB):
                        for k in range(KC):
                            i = pe.matmul(ps_w[:, t, :], w_in[:, k, t * P:(t + 1) * P], ctxT[:, k, :],
                                          start=k == 0, stop=k == KC - 1)
                        i.then_inc(sem["inproj"], 1)
                    pe.wait_ge(sem["u"], 1 + TB * (b + 1))
                    pe.wait_ge(sem["bcout"], 1 + 16 * b)
                    pe.wait_ge(sem["xpadc"], 1 + TB * (b + 1))
                    for k in range(KH):
                        i = pe.matmul(ps_w[0:XD, 0, :], w_xp[:, k, :], u[:, k, :], start=k == 0, stop=k == KH - 1)
                    i.then_inc(sem["xproj"], 1)
                    pe.wait_ge(sem["xdc"], 1 + b + 1)
                    for t in range(TB):
                        pe.matmul(ps_w[:, t, :], w_dt[:, t * P:(t + 1) * P], xd[0:RK, :], start=True, stop=True)\
                          .then_inc(sem["dtmm"], 1)
                    pe.wait_ge(sem["yz"], 1 + b)
                    for t in range(TB):
                        pe.matmul(ps_y[:, t, :], d_diag[:, t, :], u[:, t, :], start=True, stop=False,
                                  skip_group_check=True)
                    with pe.Fori(0, NST // 2) as n2:
                        for q in range(2):
                            pe.wait_ge(sem["hc"], 1 + b * NST + n2 * 2 + q + 1)
                            for t in range(TB):
                                i = pe.matmul(ps_y[:, t, :], c["ident"][:, :], hc[:, q, t, :], start=False,
                                              stop=False, skip_group_check=True)
                            i.then_inc(sem["hcfree"], 1)
                    pe.wait_ge(sem["yz"], 1 + b + 1)
                    for lt in range(TB):
                        for t in range(TB):
                            i = pe.transpose(ps_w[:, lt, t * P:(t + 1) * P], gate[:, t, lt * P:(lt + 1) * P],
                                             c["ident"][:, :])
                    i.then_inc(sem["tr"], 1)


def select(dve, pause, step, vals, m8, k, W, seg, gt, eq, cnt, cum):
    flat = "p t e -> p (t e)"
    pause()
    for j in range(TB):
        last = step(dve.max(m8[:, j, :], vals[:, j, :]), wait=j == TB - 1)
    kth = bc(m8[:, :, k - 1], 2, W)
    step(dve.tensor_tensor(gt, vals, kth, ALU.is_gt), wait=False)
    step(dve.tensor_tensor(eq, vals, kth, ALU.is_equal))
    step(dve.tensor_reduce(cnt, gt, AX_X, ALU.add), wait=False)
    step(dve.tensor_tensor_scan(cum.rearrange(flat), seg, eq.rearrange(flat), 0.0, ALU.mult, ALU.add))
    step(dve.tensor_tensor(cum, cum, bc(cnt, 2, W), ALU.add))
    step(dve.scalar_tensor_tensor(out=eq.rearrange(flat), in0=cum.rearrange(flat), scalar=float(k),
                                  in1=eq.rearrange(flat), op0=ALU.is_le, op1=ALU.mult))
    step(dve.tensor_tensor(gt, gt, eq, ALU.add))


def route_stage(nc, c, I, D, x, L, route):
    K, FS = (K0, FS0) if L == 0 else (K1, FS1)
    FC = FS // P
    NR = E + 1 if L == 0 else E
    R = f"r{L}_"
    slots = D["xs0"] if L == 0 else D["xs1"]
    nslot = NSLOT0 if L == 0 else NSLOT1
    scat, gath, wsel = route["scat"], route["gath"], route["wsel"]
    with ExitStack() as ctx:
        pl = Pools(nc, ctx)
        ctx.callback(pl.clear)
        sb = lambda n, shape, dt=F32: pl.sb(R + n, shape, dt)
        wr = sb("wr", [P, KH, NR])
        wg = sb("wg", [P, KH, FS])
        wu = sb("wu", [P, KH, FS])
        wd = sb("wd", [P, FC, H])
        xn = sb("xn", [P, NT, H])
        xnT = sb("xnT", [P, KH, T])
        h = sb("h", [P, max(FC, 2 * TB), S])
        xnb = h[:, 0:TB, :]
        xnTb = h[:, TB:2 * TB, :]
        sg = sb("sg", [P, 2, S])
        st = sb("st", [P, TB, 6])
        mv = sb("mv", [P, TB, 2])
        ve = sb("ve", [P, TB])
        rs = sb("rs", [P, TB])
        mx = sb("mx", [P, TB])
        sc = sb("sc", [P, TB, E])
        sel = sb("sel", [P, TB, E])
        eq = sb("eq", [P, TB, E])
        cum = sb("cum", [P, TB, E])
        cnt = sb("cnt", [P, TB])
        m8 = sb("m8", [P, TB, 8])
        k8 = sb("k8", [P, TB, 8])
        selb = sb("selb", [P, TB, E], BF16)
        acc = sb("acc", [P, E])
        accb = sb("accb", [P, E], BF16)
        base = sb("base", [P, E])
        gate = sb("gate", [P, NT])
        sel_all = sb("sel_all", [P, NT, E])
        pos_all = sb("pos_all", [P, NT, E])
        w_all = sb("w_all", [P, NT, E])
        hit = sb("hit", [P, TB, K, E])
        tk = sb("tk", [P, TB, K])
        if L == 1:
            bias = sb("bias", [P, E])
            sb_ = sb("sb", [P, TB, E])
            pr = sb("pr", [P, 4, TB * GR])
            gs = sb("gs", [P, TB, GR])
            gm = sb("gm", [P, TB, GR])
            geq = sb("geq", [P, TB, GR])
            gcum = sb("gcum", [P, TB, GR])
            ti = sb("ti", [P, E], I32)
            tf = sb("tf", [P, E])
            tcum = sb("tcum", [P, E])
            te = sb("te", [P, 2])
            tei = sb("tei", [P, 2], I32)
        ps_t = pl.ps(R + "ps_t", [P, 2, S])
        ps_r = pl.ps(R + "ps_r", [P, 512])
        ps_p = pl.ps(R + "ps_p", [P, 512])
        ps_g = pl.ps(R + "ps_g", [P, 2, S])
        ps_u = pl.ps(R + "ps_u", [P, 2, S])
        lg = ps_r[:, 0:TB * NR].rearrange("p (t e) -> p t e", e=NR)
        pp = ps_p[:, 0:TB * E].rearrange("p (t e) -> p t e", e=E)
        sem = {n: pl.sem(R + n) for n in (
            "win", "wrin", "stats", "ve", "rs", "xnb", "xn", "tr", "xnT0", "xnT1", "xnT", "logits", "centred", "score", "gate",
            "chain", "sel", "acc", "pos", "total", "posc", "idx", "g", "u", "sg", "h", "down", "xadd", "eid", "eidout")}
        sem["scat"] = pl.sem0(R + "scat")
        tiled = "(k p) n -> p k n"
        n_in = 3
        n_r = 2 if L == 1 else 1

        pl.start_at_one()
        with nc.Block() as block:

            @block.sync
            def _(sp):
                sp.dma_start(wr[:, :, :], I[f"wr{L}"].rearrange(tiled, p=P)).then_inc(sem["wrin"], 16)
                if L == 1:
                    sp.dma_start(bias[:, :], I["rbias"].to_broadcast([P, E])).then_inc(sem["wrin"], 16)
                sp.dma_start(wg[:, :, :], I[f"wsg{L}"].rearrange(tiled, p=P)).then_inc(sem["win"], 16)
                sp.dma_start(wu[:, :, :], I[f"wsu{L}"].rearrange(tiled, p=P)).then_inc(sem["win"], 16)
                sp.dma_start(wd[:, :, :], I[f"wsd{L}"].rearrange(tiled, p=P)).then_inc(sem["win"], 16)
                if L == 1:
                    sp.wait_ge(sem["eid"], 1 + 1)
                    sp.dma_start(D["expert"].rearrange("(p a) o -> p (a o)", a=2), tei[:, :]).then_inc(sem["eidout"], 16)
                    sp.wait_ge(sem["eidout"], 1 + 16)

            @block.gpsimd
            def _(pool):
                with pool.Fori(0, B) as b:
                    pool.wait_ge(sem["ve"], 1 + b + 1)
                    pool.tensor_tensor(rs[:, :], ve[:, :], c["minus_half"][:, 0:TB], ALU.pow).then_inc(sem["rs"], 1)
                    pool.wait_ge(sem["xnT0"], 1 + 2 * (b + 1))
                    pool.wait_ge(sem["xnT1"], 1 + 2 * (b + 1))
                    pool.tensor_copy(xnT[:, :, bass.ds(b * S, S)], xnTb).then_inc(sem["xnT"], 1)
                for t in range(NT):
                    pool.wait_ge(sem["idx"], 1 + t // TB + 1)
                    for k in range(K):
                        pool.indirect_dma_start(slots[:, :], bass.IndirectOffsetOnAxis(scat[:, t, k:k + 1], 0),
                                                xn[:, t, :], None, bounds_check=nslot - 1, oob_is_err=False)\
                            .then_inc(sem["scat"], 16)
                pool.wait_ge(sem["scat"], 16 * NT * K)

            @block.scalar
            def _(act):
                with act.Fori(0, B) as b:
                    for k in (0, 2):
                        act.wait_ge(sem["tr"], 1 + KH * b + k + 1)
                        act.wait_ge(sem["xnT"], 1 + b)
                        act.wait_ge(sem["logits"], 1 + b)
                        act.activation(xnTb[:, k, :], ps_t[:, 0, :], ACT.Copy).then_inc(sem["xnT0"], 1)
                    if L == 0:
                        act.wait_ge(sem["centred"], 1 + b + 1)
                        act.activation(sc[:, :, :], sc[:, :, :], ACT.Exp).then_inc(sem["score"], 1)
                        act.activation(gate[:, bass.ds(b * TB, TB)], lg[:, :, E], ACT.Sigmoid).then_inc(sem["gate"], 1)
                    else:
                        act.wait_ge(sem["logits"], 1 + b + 1)
                        act.wait_ge(sem["sel"], 1 + b)
                        act.activation(sc[:, :, :], lg[:, :, 0:E], ACT.Sigmoid).then_inc(sem["score"], 1)
                with act.Fori(0, B) as b:
                    for f in range(FC):
                        n = FC * b + f
                        act.wait_ge(sem["g"], 1 + n + 1)
                        if f >= 2:
                            act.wait_ge(sem["h"], 1 + n - 1)
                        else:
                            act.wait_ge(sem["h"], 1 + FC * b)
                        act.activation(sg[:, f % 2, :], ps_g[:, f % 2, :], ACT.Silu).then_inc(sem["sg"], 1)

            @block.vector
            def _(dve):
                done = [0, 0]

                def step(ins, wait=True):
                    ins.then_inc(sem["chain"], 1)
                    done[1] += 1
                    if wait:
                        dve.wait_ge(sem["chain"], 1 + done[0] + done[1])
                    return ins

                def pause():
                    dve.sem_inc(c["held"], 1)

                dve.memset(acc[:, :], 0.0).then_inc(sem["acc"], 1)
                dve.memset(accb[:, :], 0.0).then_inc(sem["acc"], 1)
                dve.wait_ge(sem["acc"], 1 + 2)
                R_STEPS = 32 if L == 0 else 48
                with dve.Fori(0, B) as b:
                    done[0], done[1] = b * R_STEPS, 0
                    for j in range(TB):
                        dve.bn_stats(st[:, j, :], x[:, b * TB + j, :]).then_inc(sem["stats"], 1)
                    hold(dve, sem["stats"], 1 + 2 * TB * b + TB, c["held"])
                    for j in range(TB):
                        dve.bn_aggr(mv[:, j, :], st[:, j, :]).then_inc(sem["stats"], 1)
                    dve.wait_ge(sem["stats"], 1 + 2 * TB * (b + 1))
                    dve.tensor_scalar(ve[:, :], mv[:, :, 1], LN_EPS, None, ALU.add).then_inc(sem["ve"], 1)
                    dve.wait_ge(sem["rs"], 1 + b + 1)
                    dve.wait_ge(sem["tr"], 1 + KH * b)
                    for j in range(TB):
                        for dst in (xnb[:, j, :], xn[:, b * TB + j, :]):
                            i = dve.tensor_scalar(dst, x[:, b * TB + j, :], mv[:, j, 0:1], rs[:, j:j + 1],
                                                  ALU.subtract, ALU.mult)
                    i.then_inc(sem["xnb"], 1)
                    for k in (1, 3):
                        dve.wait_ge(sem["tr"], 1 + KH * b + k + 1)
                        dve.wait_ge(sem["xnT"], 1 + b)
                        dve.wait_ge(sem["logits"], 1 + b)
                        dve.tensor_copy(xnTb[:, k, :], ps_t[:, 1, :]).then_inc(sem["xnT1"], 1)
                    dve.wait_ge(sem["logits"], 1 + b + 1)
                    if L == 0:
                        dve.wait_ge(sem["wrin"], 1 + 16)
                        step(dve.tensor_reduce(mx[:, :], lg[:, :, 0:E], AX_X, ALU.max))
                        dve.tensor_tensor(sc[:, :, :], lg[:, :, 0:E], bc(mx[:, :], 2, E), ALU.subtract)\
                           .then_inc(sem["centred"], 1)
                        dve.wait_ge(sem["score"], 1 + b + 1)
                        chosen_from = sc
                    else:
                        dve.wait_ge(sem["wrin"], 1 + 32)
                        dve.wait_ge(sem["score"], 1 + b + 1)
                        step(dve.tensor_tensor(sb_[:, :, :], sc[:, :, :], bc(bias[:, :], 1, TB), ALU.add))
                        four = sb_[:, :, :].rearrange("p t (g i) -> p (t g) i", i=GR // 2)
                        mx01, mn01, mx23, mn23 = (pr[:, i, :] for i in range(4))
                        step(dve.tensor_tensor(mx01, four[:, :, 0], four[:, :, 1], ALU.max), wait=False)
                        step(dve.tensor_tensor(mn01, four[:, :, 0], four[:, :, 1], ALU.min), wait=False)
                        step(dve.tensor_tensor(mx23, four[:, :, 2], four[:, :, 3], ALU.max), wait=False)
                        step(dve.tensor_tensor(mn23, four[:, :, 2], four[:, :, 3], ALU.min))
                        gflat = gs[:, :, :].rearrange("p t g -> p (t g)")
                        step(dve.tensor_tensor(mn01, mn01, mn23, ALU.max))
                        step(dve.tensor_tensor(mn23, mx01, mx23, ALU.min), wait=False)
                        step(dve.tensor_tensor(gflat, mx01, mx23, ALU.max))
                        step(dve.tensor_tensor(mn01, mn01, mn23, ALU.max))
                        step(dve.tensor_tensor(gflat, gflat, mn01, ALU.add))
                        select(dve, pause, step, gs[:, :, :], m8[:, :, :], GSEL, GR, c["half_seg8"][:, :],
                               gm[:, :, :], geq[:, :, :], cnt[:, :], gcum[:, :, :])
                        step(dve.tensor_tensor(sb_[:, :, :].rearrange("p t (g i) -> p (t g) i", i=GR // 2),
                                               four, bc(gm[:, :, :].rearrange("p t g -> p (t g)"), 2, GR // 2),
                                               ALU.mult))
                        chosen_from = sb_
                    dve.wait_ge(sem["pos"], 1 + b)
                    select(dve, pause, step, chosen_from[:, :, :], m8[:, :, :], K, E, c["seg"][:, :],
                           sel[:, :, :], eq[:, :, :], cnt[:, :], cum[:, :, :])
                    step(dve.tensor_copy(selb[:, :, :], sel[:, :, :]), wait=False)
                    step(dve.tensor_copy(sel_all[:, bass.ds(b * TB, TB), :], sel[:, :, :]))
                    dve.tensor_tensor(sc[:, :, :], sc[:, :, :], sel[:, :, :], ALU.mult).then_inc(sem["sel"], 1)
                    dve.wait_ge(sem["sel"], 1 + b + 1)
                    step(dve.tensor_reduce(cnt[:, :], sc[:, :, :], AX_X, ALU.add))
                    step(dve.reciprocal(mx[:, :], cnt[:, :]))
                    if L == 1:
                        step(dve.tensor_scalar(mx[:, :], mx[:, :], ROUTED, None, ALU.mult))
                    step(dve.tensor_tensor(w_all[:, bass.ds(b * TB, TB), :], sc[:, :, :], bc(mx[:, :], 2, E), ALU.mult))
                    dve.wait_ge(sem["pos"], 1 + b + 1)
                    step(dve.tensor_copy(pos_all[:, bass.ds(b * TB, TB), :], pp))
                    step(dve.tensor_reduce(base[:, :], sel[:, :, :].rearrange("p t e -> p e t"), AX_X, ALU.add))
                    step(dve.tensor_tensor(acc[:, :], acc[:, :], base[:, :], ALU.add))
                    dve.tensor_copy(accb[:, :], acc[:, :]).then_inc(sem["acc"], 1)
                    assert done[1] <= R_STEPS, done
                    if done[1] < R_STEPS:
                        dve.sem_inc(sem["chain"], R_STEPS - done[1])
                done[0], done[1] = B * R_STEPS, 0
                if L == 0:
                    base1 = c["slot0"]
                else:
                    dve.wait_ge(sem["total"], 1 + 1)
                    step(dve.tensor_scalar(tf[:, :], ps_p[:, 0:E], float(P - 1), None, ALU.add))
                    step(dve.tensor_copy(ti[:, :], tf[:, :]))
                    step(dve.tensor_scalar(ti[:, :], ti[:, :], 7, None, ALU.arith_shift_right))
                    step(dve.tensor_copy(tf[:, :], ti[:, :]))
                    step(dve.memset(acc[:, :], 1.0))
                    step(dve.tensor_tensor_scan(tcum[:, :], acc[:, :], tf[:, :], 0.0, ALU.mult, ALU.add))
                    step(dve.tensor_tensor(base[:, :], tcum[:, :], tf[:, :], ALU.subtract))
                    step(dve.tensor_scalar(base[:, :], base[:, :], float(P), 1.0, ALU.mult, ALU.add))
                    for a in range(2):
                        step(dve.tensor_scalar(acc[:, :], tcum[:, :], c["tile_no"][:, a:a + 1], None, ALU.is_le))
                        step(dve.tensor_reduce(te[:, a:a + 1], acc[:, :], AX_X, ALU.add))
                    step(dve.tensor_scalar(te[:, :], te[:, :], float(E - 1), None, ALU.min))
                    dve.tensor_copy(tei[:, :], te[:, :]).then_inc(sem["eid"], 1)
                    base1 = base
                first = done[1]
                F_STEPS = 24
                with dve.Fori(0, B) as b:
                    done[0], done[1] = B * R_STEPS + first + b * F_STEPS, 0

                    def product(f):
                        n = FC * b + f
                        dve.wait_ge(sem["sg"], 1 + n + 1)
                        dve.wait_ge(sem["u"], 1 + n + 1)
                        if f == 0:
                            dve.wait_ge(sem["down"], 1 + TB * b)
                        dve.tensor_tensor(h[:, f, :], ps_u[:, f % 2, :], sg[:, f % 2, :], ALU.mult)\
                           .then_inc(sem["h"], 1)

                    for f in range(2):
                        product(f)
                    bt = bass.ds(b * TB, TB)
                    step(dve.tensor_tensor(cum[:, :, :], pos_all[:, bt, :], bc(base1[:, :], 1, TB), ALU.add))
                    if L == 0:
                        step(dve.scalar_tensor_tensor(out=sel[:, :, :], in0=pos_all[:, bt, :], scalar=float(CAP),
                                                      in1=sel_all[:, bt, :], op0=ALU.is_lt, op1=ALU.mult))
                        step(dve.tensor_tensor(eq[:, :, :], w_all[:, bt, :], sel[:, :, :], ALU.mult))
                        step(dve.tensor_tensor(cum[:, :, :], cum[:, :, :], sel[:, :, :], ALU.mult))
                    else:
                        step(dve.tensor_copy(eq[:, :, :], w_all[:, bt, :]))
                        step(dve.tensor_tensor(cum[:, :, :], cum[:, :, :], sel_all[:, bt, :], ALU.mult))
                    pause()
                    for j in range(TB):
                        step(dve.max(k8[:, j, :], cum[:, j, :]), wait=j == TB - 1)
                    product(2)
                    for j in range(TB):
                        step(dve.tensor_tensor(hit[:, j, :, :], bc(cum[:, j, :], 1, K), bc(k8[:, j, 0:K], 2, E),
                                               ALU.is_equal), wait=j == TB - 1)
                    for j in range(TB):
                        step(dve.tensor_tensor(hit[:, j, :, :], hit[:, j, :, :], bc(eq[:, j, :], 1, K), ALU.mult),
                             wait=j == TB - 1)
                    step(dve.tensor_reduce(wsel[:, bt, 0:K], hit[:, :, :, :], AX_X, ALU.add))
                    ks = k8[:, :, 0:K]
                    step(dve.tensor_scalar(tk[:, :, :], ks, 1.0, float(SKIP), ALU.is_lt, ALU.mult))
                    step(dve.tensor_tensor(tk[:, :, :], tk[:, :, :], ks, ALU.add))
                    step(dve.tensor_scalar(scat[:, bt, 0:K], tk[:, :, :], -1.0, None, ALU.add), wait=False)
                    dve.tensor_scalar(gath[:, bt, 0:K], ks, -1.0, 0.0, ALU.add, ALU.max).then_inc(sem["idx"], 1)
                    assert done[1] <= F_STEPS, done
                    if done[1] < F_STEPS:
                        dve.sem_inc(sem["chain"], F_STEPS - done[1])
                    for f in range(3, FC):
                        product(f)
                    for j in range(TB):
                        dve.wait_ge(sem["down"], 1 + TB * b + j + 1)
                        xt = x[:, b * TB + j, :]
                        if L == 0:
                            dve.scalar_tensor_tensor(out=xt, in0=ps_t[:, j % 2, :], scalar=gate[:, bass.ds(b * TB + j, 1)],
                                                     in1=xt, op0=ALU.mult, op1=ALU.add).then_inc(sem["xadd"], 1)
                        else:
                            dve.tensor_tensor(xt, ps_t[:, j % 2, :], xt, ALU.add).then_inc(sem["xadd"], 1)

            @block.tensor
            def _(pe):
                pe.wait_ge(sem["wrin"], 1 + 16 * n_r)
                with pe.Fori(0, B) as b:
                    pe.wait_ge(sem["xnb"], 1 + b + 1)
                    for k in range(KH):
                        pe.wait_ge(sem["xnT0"] if k % 2 == 0 else sem["xnT1"], 1 + 2 * b + k // 2)
                        for j in range(TB):
                            i = pe.transpose(ps_t[:, k % 2, j * P:(j + 1) * P], xnb[:, j, k * P:(k + 1) * P],
                                             c["ident"][:, :])
                        i.then_inc(sem["tr"], 1)
                    pe.wait_ge(sem["xnT0"], 1 + 2 * (b + 1))
                    pe.wait_ge(sem["xnT1"], 1 + 2 * (b + 1))
                    if L == 0:
                        pe.wait_ge(sem["gate"], 1 + b)
                    pe.wait_ge(sem["score"], 1 + b)
                    for j in range(TB):
                        for k in range(KH):
                            i = pe.matmul(lg[:, j, :], xnTb[:, k, j * P:(j + 1) * P], wr[:, k, :], start=k == 0, stop=k == KH - 1)
                    i.then_inc(sem["logits"], 1)
                    pe.wait_ge(sem["sel"], 1 + b + 1)
                    pe.wait_ge(sem["acc"], 1 + b + 2)
                    for j in range(TB):
                        pe.matmul(pp[:, j, :], c["before_bf"][:, :], selb[:, j, :], start=True, stop=False)
                        for i2 in range(j):
                            pe.matmul(pp[:, j, :], c["ones_bf"][:, :], selb[:, i2, :], start=False, stop=False)
                        i = pe.matmul(pp[:, j, :], c["ones_bf"][:, :], accb[:, :], start=False, stop=True)
                    i.then_inc(sem["pos"], 1)
                if L == 1:
                    pe.wait_ge(sem["acc"], 1 + B + 2)
                    pe.matmul(ps_p[:, 0:E], c["ones_bf"][:, :], accb[:, :], start=True, stop=True).then_inc(sem["total"], 1)
                pe.wait_ge(sem["win"], 1 + 16 * n_in)
                pe.wait_ge(sem["xnT"], 1 + B)
                with pe.Fori(0, B) as b:
                    for f in range(FC):
                        n = FC * b + f
                        for src, ps, w, ready, taken in (("g", ps_g, wg, "sg", None), ("u", ps_u, wu, "h", None)):
                            pe.wait_ge(sem[ready], 1 + (n - 1 if f >= 2 else FC * b))
                            for k in range(KH):
                                i = pe.matmul(ps[:, f % 2, :], w[:, k, f * P:(f + 1) * P], xnT[:, k, bass.ds(b * S, S)],
                                              start=k == 0, stop=k == KH - 1)
                            i.then_inc(sem[src], 1)
                    pe.wait_ge(sem["h"], 1 + FC * (b + 1))
                    for j in range(TB):
                        pe.wait_ge(sem["xadd"], 1 + (TB * b + j - 1 if j >= 2 else TB * b))
                        for f in range(FC):
                            i = pe.matmul(ps_t[:, j % 2, :], h[:, f, j * P:(j + 1) * P], wd[:, f, :],
                                          start=f == 0, stop=f == FC - 1)
                        i.then_inc(sem["down"], 1)


def expert_stage0(nc, c, I, D):
    FR = F0 - 2 * P
    with ExitStack() as ctx:
        pl = Pools(nc, ctx)
        ctx.callback(pl.clear)
        wg = pl.sb("e0_wg", [P, 2, KH, F0])
        wu = pl.sb("e0_wu", [P, 2, KH, F0])
        wd = pl.sb("e0_wd", [P, 2, 3, H])
        xe = pl.sb("e0_xe", [CAP, 2, H])
        xeT = pl.sb("e0_xeT", [P, 2, KH, CAP])
        sg = pl.sb("e0_sg", [P, 2, 3, CAP])
        hT = pl.sb("e0_hT", [P, 2, 3, CAP])
        yo = pl.sb("e0_yo", [CAP, 2, H])
        ps_x = pl.ps("e0_psx", [P, 2, 512])
        ps_g = pl.ps("e0_psg", [P, 2, 512])
        ps_u = pl.ps("e0_psu", [P, 2, 512])
        ps_o = pl.ps("e0_pso", [P, 2, 512])
        sem = {n: pl.sem("e0_" + n) for n in ("in0", "in1", "free", "tr", "xeT", "g", "u", "sg", "hT", "down", "yo", "stored")}
        sem["out"] = pl.sem0("e0_out")
        fin = (sem["in0"], sem["in1"])
        last = ((0, 2, P), (2, 3, FR))

        pl.start_at_one()
        with nc.Block() as block:

            @block.sync
            def _(sp):
                with sp.Fori(0, E // 2) as i:
                    for q in range(2):
                        e = i * 2 + q
                        hold(sp, sem["free"], 1 + e + 1, c["held"])
                        sp.dma_start(xe[:, q, :], D["xs0"][bass.ds(e * CAP, CAP), :]).then_inc(fin[q], 16)
                        for w, name in ((wg, "wg0"), (wu, "wu0")):
                            sp.dma_start(w[:, q, :, :], I[name][bass.ds(e, 1), :, :]
                                         .rearrange("o (p k) f -> p (o k) f", k=KH)).then_inc(fin[q], 16)
                        sp.dma_start(wd[:, q, 0:2, :], I["wd0"][bass.ds(e, 1), 0:2 * P, :]
                                     .rearrange("o (c p) n -> p (o c) n", p=P)).then_inc(fin[q], 16)
                        sp.dma_start(wd[0:FR, q, 2, :], I["wd0"][bass.ds(e, 1), 2 * P:F0, :]
                                     .rearrange("o p n -> p (o n)")).then_inc(fin[q], 16)

            @block.gpsimd
            def _(pool):
                with pool.Fori(0, E // 2) as i:
                    for q in range(2):
                        e = i * 2 + q
                        hold(pool, sem["yo"], 1 + e + 1, c["held"])
                        pool.dma_start(D["y0"][bass.ds(e * CAP, CAP), :], yo[:, q, :]).then_inc(sem["out"], 16)
                        hold(pool, sem["out"], 16 * (e + 1), c["held"])
                        pool.sem_inc(sem["stored"], 1)

            @block.scalar
            def _(act):
                with act.Fori(0, E // 2) as i:
                    for q in range(2):
                        e = i * 2 + q
                        act.wait_ge(sem["g"], 1 + e + 1)
                        act.wait_ge(sem["down"], 1 + e)
                        for a, z, m in last:
                            j = act.activation(sg[0:m, q, a:z, :],
                                               ps_g[0:m, q, a * CAP:z * CAP].rearrange("p (c s) -> p c s", s=CAP),
                                               ACT.Silu)
                        j.then_inc(sem["sg"], 1)
                        act.wait_ge(sem["down"], 1 + e + 1)
                        act.wait_ge(sem["stored"], 1 + e)
                        act.activation(yo[:, q, :], ps_o[0:CAP, q, :], ACT.Copy).then_inc(sem["yo"], 1)

            @block.vector
            def _(dve):
                with dve.Fori(0, E // 2) as i:
                    for q in range(2):
                        e = i * 2 + q
                        dve.wait_ge(sem["tr"], 1 + e + 1)
                        dve.wait_ge(sem["free"], 1 + e + 1)
                        dve.tensor_copy(xeT[:, q, :, :], ps_x[:, q, 0:KH * CAP].rearrange("p (k s) -> p k s", s=CAP))\
                           .then_inc(sem["xeT"], 1)
                        dve.wait_ge(sem["sg"], 1 + e + 1)
                        dve.wait_ge(sem["u"], 1 + e + 1)
                        for a, z, m in last:
                            j = dve.tensor_tensor(hT[0:m, q, a:z, :],
                                                  ps_u[0:m, q, a * CAP:z * CAP].rearrange("p (c s) -> p c s", s=CAP),
                                                  sg[0:m, q, a:z, :], ALU.mult)
                        j.then_inc(sem["hT"], 1)

            @block.tensor
            def _(pe):
                pe.sem_inc(sem["free"], 2)

                def up(e, q, half):
                    pe.wait_ge(fin[q], 1 + 80 * (half + 1))
                    hold(pe, sem["xeT"], 1 + e, c["held"])
                    for k in range(KH):
                        i = pe.transpose(ps_x[:, q, k * CAP:(k + 1) * CAP], xe[:, q, k:H:KH], c["ident"][0:CAP, 0:CAP])
                    i.then_inc(sem["tr"], 1)
                    pe.wait_ge(sem["xeT"], 1 + e + 1)
                    for ps, w, name in ((ps_g, wg, "g"), (ps_u, wu, "u")):
                        for f in range(3):
                            m = P if f < 2 else FR
                            for k in range(KH):
                                i = pe.matmul(ps[0:m, q, f * CAP:(f + 1) * CAP], w[:, q, k, f * P:f * P + m],
                                              xeT[:, q, k, :], start=k == 0, stop=k == KH - 1)
                        i.then_inc(sem[name], 1)

                def down(e, q):
                    pe.wait_ge(sem["hT"], 1 + e + 1)
                    for f in range(3):
                        m = P if f < 2 else FR
                        i = pe.matmul(ps_o[0:CAP, q, :], hT[0:m, q, f, :], wd[0:m, q, f, :], start=f == 0, stop=f == 2)
                    i.then_inc(sem["down"], 1)
                    pe.wait_ge(sem["down"], 1 + e + 1)
                    pe.sem_inc(sem["free"], 1)

                with pe.Fori(0, E // 2) as i:
                    for q in range(2):
                        up(i * 2 + q, q, i)
                        pe.wait_ge(sem["yo"], 1 + i * 2 + q)
                        down(i * 2 + q, q)


def expert_stage1(nc, c, I, D):
    with ExitStack() as ctx:
        pl = Pools(nc, ctx)
        ctx.callback(pl.clear)
        NW = F1 // P
        wgu = pl.sb("e1_wgu", [P, 2, KH, 2 * F1])
        wd = pl.sb("e1_wd", [P, 2, NW, H])
        xs = pl.sb("e1_xs", [P, 2, H])
        xsT = pl.sb("e1_xsT", [P, 2, KH, P])
        sg = pl.sb("e1_sg", [P, 2, F1])
        h = pl.sb("e1_h", [P, 2, F1])
        hT = pl.sb("e1_hT", [P, 2, NW, P])
        yo = pl.sb("e1_yo", [P, 2, H])
        ids = pl.sb("e1_ids", [1, NTILE1], I32)
        ps_x = pl.ps("e1_psx", [P, 512])
        ps_g = pl.ps("e1_psg", [P, 2, 512])
        ps_h = pl.ps("e1_psh", [P, 512])
        ps_o = pl.ps("e1_pso", [P, 2, 512])
        sem = {n: pl.sem("e1_" + n) for n in ("ids", "in0", "in1", "free", "tr", "xsT", "gu", "sg", "h", "htr", "hT",
                                              "down", "yo", "stored")}
        sem["out"] = pl.sem0("e1_out")
        fin = (sem["in0"], sem["in1"])

        pl.start_at_one()
        with nc.Block() as block:

            @block.sync
            def _(sp):
                sp.dma_start(ids[0:1, :], D["expert"][0:NTILE1, :].rearrange("n o -> o n")).then_inc(sem["ids"], 16)
                sp.wait_ge(sem["ids"], 1 + 16)
                with sp.Fori(0, NTILE1 // 2) as i:
                    for q in range(2):
                        t = i * 2 + q
                        hold(sp, sem["free"], 1 + t + 1, c["held"])
                        e = sp.value_load(ids[0:1, bass.ds(t, 1)], min_val=0, max_val=E - 1)
                        sp.dma_start(xs[:, q, :], D["xs1"][bass.ds(t * P, P), :]).then_inc(fin[q], 16)
                        for a, name in ((0, "wg1"), (1, "wu1")):
                            sp.dma_start(wgu[:, q, :, a * F1:(a + 1) * F1], I[name][bass.ds(e, 1), :, :]
                                         .rearrange("o (p k) f -> p (o k) f", k=KH)).then_inc(fin[q], 16)
                        sp.dma_start(wd[:, q, :, :], I["wd1"][bass.ds(e, 1), :, :]
                                     .rearrange("o (p c) n -> p (o c) n", c=NW)).then_inc(fin[q], 16)

            @block.gpsimd
            def _(pool):
                with pool.Fori(0, NTILE1 // 2) as i:
                    for q in range(2):
                        t = i * 2 + q
                        hold(pool, sem["yo"], 1 + t + 1, c["held"])
                        pool.dma_start(D["y1"][bass.ds(t * P, P), :], yo[:, q, :]).then_inc(sem["out"], 16)
                        hold(pool, sem["out"], 16 * (t + 1), c["held"])
                        pool.sem_inc(sem["stored"], 1)

            @block.scalar
            def _(act):
                with act.Fori(0, NTILE1 // 2) as i:
                    for q in range(2):
                        t = i * 2 + q
                        act.wait_ge(sem["gu"], 1 + t + 1)
                        act.wait_ge(sem["h"], 1 + t)
                        act.activation(sg[:, q, :], ps_g[:, q, 0:F1], ACT.Silu).then_inc(sem["sg"], 1)
                        act.wait_ge(sem["down"], 1 + t + 1)
                        act.wait_ge(sem["stored"], 1 + t)
                        act.activation(yo[:, q, :], ps_o[:, q, :], ACT.Copy).then_inc(sem["yo"], 1)

            @block.vector
            def _(dve):
                with dve.Fori(0, NTILE1 // 2) as i:
                    for q in range(2):
                        t = i * 2 + q
                        dve.wait_ge(sem["tr"], 1 + t + 1)
                        dve.wait_ge(sem["free"], 1 + t + 1)
                        dve.tensor_copy(xsT[:, q, :, :], ps_x[:, :].rearrange("p (k s) -> p k s", s=P))\
                           .then_inc(sem["xsT"], 1)
                        dve.wait_ge(sem["sg"], 1 + t + 1)
                        dve.wait_ge(sem["htr"], 1 + t)
                        dve.tensor_tensor(h[:, q, :], ps_g[:, q, F1:], sg[:, q, :], ALU.mult).then_inc(sem["h"], 1)
                        dve.wait_ge(sem["htr"], 1 + t + 1)
                        dve.tensor_copy(hT[:, q, :, :], ps_h[:, 0:NW * P].rearrange("p (c s) -> p c s", s=P))\
                           .then_inc(sem["hT"], 1)

            @block.tensor
            def _(pe):
                pe.sem_inc(sem["free"], 2)
                with pe.Fori(0, NTILE1 // 2) as i:
                    for q in range(2):
                        t = i * 2 + q
                        pe.wait_ge(fin[q], 1 + 64 * (i + 1))
                        pe.wait_ge(sem["xsT"], 1 + t)
                        for k in range(KH):
                            j = pe.transpose(ps_x[:, k * P:(k + 1) * P], xs[:, q, k:H:KH], c["ident"][:, :])
                        j.then_inc(sem["tr"], 1)
                        pe.wait_ge(sem["xsT"], 1 + t + 1)
                        for k in range(KH):
                            j = pe.matmul(ps_g[:, q, :], xsT[:, q, k, :], wgu[:, q, k, :], start=k == 0, stop=k == KH - 1)
                        j.then_inc(sem["gu"], 1)
                        pe.wait_ge(sem["h"], 1 + t + 1)
                        pe.wait_ge(sem["hT"], 1 + t)
                        for a in range(NW):
                            j = pe.transpose(ps_h[:, a * P:(a + 1) * P], h[:, q, a:F1:NW], c["ident"][:, :])
                        j.then_inc(sem["htr"], 1)
                        pe.wait_ge(sem["hT"], 1 + t + 1)
                        pe.wait_ge(sem["yo"], 1 + t)
                        for a in range(NW):
                            j = pe.matmul(ps_o[:, q, :], hT[:, q, a, :], wd[:, q, a, :], start=a == 0, stop=a == NW - 1)
                        j.then_inc(sem["down"], 1)
                        pe.wait_ge(sem["down"], 1 + t + 1)
                        pe.sem_inc(sem["free"], 1)


def combine_stage(nc, c, I, D, x, L, route):
    K = K0 if L == 0 else K1
    NB = 8
    y = D["y0"] if L == 0 else D["y1"]
    per = NB // K
    with ExitStack() as ctx:
        pl = Pools(nc, ctx)
        ctx.callback(pl.clear)
        rows = pl.sb(f"c{L}_rows", [P, NB, H])
        got = [pl.sem0(f"c{L}_got{i}") for i in range(NB)]
        used = pl.sem(f"c{L}_used")
        pl.start_at_one()
        with nc.Block() as block:

            @block.gpsimd
            def _(pool):
                for t in range(NT):
                    for k in range(K):
                        n = t * K + k
                        if n >= NB:
                            pool.wait_ge(used, 1 + n - NB + 1)
                        pool.indirect_dma_start(rows[:, n % NB, :], None, y[:, :],
                                                bass.IndirectOffsetOnAxis(route["gath"][:, t, k:k + 1], 0))\
                            .then_inc(got[n % NB], 16)

            @block.vector
            def _(dve):
                with dve.Fori(0, NT // per) as r:
                    for n in range(NB):
                        t, k = n // K, n % K
                        dve.wait_ge(got[n], 16 * (r + 1))
                        dve.wait_ge(used, 1 + r * NB + n)
                        xt = x[:, r * per + t, :]
                        dve.scalar_tensor_tensor(out=xt, in0=rows[:, n, :],
                                                 scalar=route["wsel"][:, bass.ds(r * per + t, 1), k],
                                                 in1=xt, op0=ALU.mult, op1=ALU.add).then_inc(used, 1)


def attention_stage(nc, c, I, D, x):
    ND = HG * DCA
    QK = 2 * TB * HG
    NR = QK + HG
    with ExitStack() as ctx:
        pl = Pools(nc, ctx)
        ctx.callback(pl.clear)
        sb = lambda n, shape, dt=F32: pl.sb("a_" + n, shape, dt)
        wq = sb("wq", [P, KH, H])
        wkv = sb("wkv", [P, KC, 2 * H])
        wkvd = sb("wkvd", [P, KC, 2 * H])
        wo = sb("wo", [P, KH, H])
        bq = sb("bq", [1, H])
        bkv = sb("bkv", [1, 2 * H])
        bkvd = sb("bkvd", [1, 2 * H])
        bo = sb("bo", [1, H])
        hw = sb("hw", [P, 6])
        xnb = sb("xnb", [P, TB, H])
        xnT = sb("xnT", [P, KH, S])
        ctxT = sb("ctxT", [P, KC, S])
        ctxd = sb("ctxd", [P, KC, P // DCA, DCA])
        mask_r = sb("mask_r", [ND, HG, HD])
        mask_c = sb("mask_c", [P, HG, DCA])
        st = sb("st", [P, TB, 6])
        mv = sb("mv", [P, TB, 2])
        ve = sb("ve", [P, TB])
        rs = sb("rs", [P, TB])
        hd = sb("hd", [P, NR, HD])
        hsq = sb("hsq", [P, NR, HD])
        mu = sb("mu", [P, NR])
        hv = sb("hv", [P, NR])
        v = sb("v", [P, TB, HG, HD])
        dv = sb("dv", [ND, HG, HD])
        qT = sb("qT", [P, S])
        kT = sb("kT", [P, S])
        kd = sb("kd", [P, HG, DCA])
        sd = sb("sd", [P, TB * HG, DCA])
        md = sb("md", [P, TB * HG])
        pdT = sb("pdT", [ND, TB, P])
        cd = sb("cd", [P, TB, GW])
        p = sb("p", [P, 2, S])
        pt = sb("pt", [P, 2, TB, P])
        nm = sb("nm", [P, TB * HG])
        sm = sb("sm", [P, TB * HG])
        rm = sb("rm", [P, TB * HG])
        ct = sb("ct", [P, TB, GW])
        ctxo = sb("ctxo", [P, TB, H])
        oT = sb("oT", [P, KH, S])
        ps_s = pl.ps("a_pss", [P, 3, 512])
        ps_pt = pl.ps("a_pspt", [P, 2, 512])
        ps_w = pl.ps("a_psw", [P, 3, 512])
        sem = {n: pl.sem("a_" + n) for n in (
            "win", "ctx", "ctxd", "const", "stats", "ve", "rs", "xnb", "xtr", "xnT", "q", "kv", "d", "cq", "ck", "cv",
            "chain", "cent", "sq", "var", "sqrt", "hn", "htr", "htrc", "sd", "sdc", "pdexp", "pd", "pdT", "pdTc", "cdmm",
            "cd", "s", "max", "exp", "ptr", "pt0", "pt1", "pv", "ctxo", "otr", "oT0", "oT1", "om", "xadd")}
        N = TB * HG
        n_in = 8 + HG
        f3 = "p a b -> p (a b)"

        pl.start_at_one()
        with nc.Block() as block:

            @block.sync
            def _(sp):
                for dst, name in ((wq, "wq"), (wkv, "wkv"), (wkvd, "wkvd"), (wo, "wo")):
                    sp.dma_start(dst[:, :, :], I[name].rearrange("(k p) n -> p k n", p=P)).then_inc(sem["win"], 16)
                for dst, name in ((bq, "bq"), (bkv, "bkv"), (bkvd, "bkvd"), (bo, "bo")):
                    sp.dma_start(dst[:, :], I[name]).then_inc(sem["win"], 16)
                for i in range(HG):
                    sp.dma_start(hw[i * HD:(i + 1) * HD, :], I["headnorm"]).then_inc(sem["win"], 16)
                with sp.Fori(0, B) as b:
                    hold(sp, sem["cv"], 1 + NG * b, c["held"])
                    hold(sp, sem["d"], 1 + NG * b, c["held"])
                    sp.dma_start(ctxT[:, :, :], I["ctxT"][:, bass.ds(b * S, S)].rearrange("(k p) n -> p k n", p=P))\
                      .then_inc(sem["ctx"], 16)

            @block.gpsimd
            def _(pool):
                pool.memset(mask_r[:, :, :], 1.0).then_inc(sem["const"], 1)
                pool.memset(mask_c[:, :, :], 1.0).then_inc(sem["const"], 1)
                pool.memset(hd[:, :, :], 0.0).then_inc(sem["const"], 1)
                pool.memset(p[:, :, :], 0.0).then_inc(sem["const"], 1)
                pool.memset(kT[:, :], 0.0).then_inc(sem["const"], 1)
                pool.wait_ge(sem["const"], 1 + 5)
                n = 5
                for m, width, rows in ((mask_r, HD, DCA), (mask_c, DCA, HD)):
                    pool.affine_select(out=m[:, :, :], in_=m[:, :, :], compare_op=ALU.is_ge, fill=0.0, base=0,
                                       pattern=[[-rows, HG], [0, width]], channel_multiplier=1).then_inc(sem["const"], 1)
                    n += 1
                    pool.wait_ge(sem["const"], 1 + n)
                    pool.affine_select(out=m[:, :, :], in_=m[:, :, :], compare_op=ALU.is_ge, fill=0.0, base=rows - 1,
                                       pattern=[[rows, HG], [0, width]], channel_multiplier=-1).then_inc(sem["const"], 1)
                    n += 1
                with pool.Fori(0, B) as b:
                    pool.wait_ge(sem["ctx"], 1 + 16 * (b + 1))
                    pool.sem_inc(c["held"], 1)
                    for i in range(P // DCA):
                        j = pool.tensor_copy(ctxd[:, :, i, :], ctxT[:, :, S2:])
                    j.then_inc(sem["ctxd"], 1)
                    pool.wait_ge(sem["ve"], 1 + b + 1)
                    pool.tensor_tensor(rs[:, :], ve[:, :], c["minus_half"][:, 0:TB], ALU.pow).then_inc(sem["rs"], 1)

            @block.scalar
            def _(act):
                with act.Fori(0, B) as b:
                    with act.Fori(0, NG) as g:
                        G = b * NG + g
                        act.wait_ge(sem["const"], 1 + 9)
                        act.wait_ge(sem["q"], 1 + G + 1)
                        act.wait_ge(sem["htr"], 1 + 3 * G)
                        act.activation(hd[:, 0:N, :].rearrange("p a d -> p (a d)"), ps_w[:, 0, :], ACT.Copy)\
                           .then_inc(sem["cq"], 1)
                        act.wait_ge(sem["d"], 1 + G + 1)
                        dview = ps_s[0:ND, 2, 0:HG * 2 * HD].rearrange("p (h z d) -> p h z d", h=HG, z=2)
                        act.activation(hd[0:ND, QK:NR, :], dview[:, :, 0, :], ACT.Copy).then_inc(sem["cq"], 1)
                        act.wait_ge(sem["cent"], 1 + G + 1)
                        act.activation(hsq[:, :, :], hd[:, :, :], ACT.Square).then_inc(sem["sq"], 1)
                        act.wait_ge(sem["var"], 1 + G + 1)
                        act.activation(hv[:, :], hv[:, :], ACT.Sqrt).then_inc(sem["sqrt"], 1)
                        act.wait_ge(sem["sdc"], 1 + G + 1)
                        act.activation(sd[:, :, :], sd[:, :, :], ACT.Exp).then_inc(sem["pdexp"], 1)
                        act.wait_ge(sem["pdT"], 1 + G + 1)
                        act.activation(pdT[:, :, :], ps_w[0:ND, 1, :].rearrange("p (j s) -> p j s", s=P), ACT.Copy)\
                           .then_inc(sem["pdTc"], 1)
                        act.wait_ge(sem["cdmm"], 1 + G + 1)
                        act.activation(cd[:, :, :].rearrange("p a b -> p (a b)"), ps_w[:, 2, :], ACT.Copy)\
                           .then_inc(sem["cd"], 1)

                        def turned(n):
                            if n % 2 == 1:
                                act.wait_ge(sem["ptr"], 1 + G * N + n + 1)
                                act.activation(pt[:, 1, :, :], ps_pt[:, 1, :].rearrange("p (j s) -> p j s", s=P), ACT.Copy)\
                                   .then_inc(sem["pt1"], 1)

                        for n in range(N):
                            act.wait_ge(sem["max"], 1 + G * N + n + 1)
                            if n >= 2:
                                act.wait_ge(sem["ptr"], 1 + G * N + n - 1)
                            act.activation(p[:, n % 2, 0:S2], ps_s[:, n % 3, 0:S2], ACT.Exp, bias=nm[:, n:n + 1],
                                           accum_out=sm[:, n:n + 1]).then_inc(sem["exp"], 1)
                            if n >= 2:
                                turned(n - 2)
                        for n in range(N - 2, N):
                            turned(n)
                    for k in (0, 2):
                        act.wait_ge(sem["otr"], 1 + KH * b + k + 1)
                        act.activation(oT[:, k, :], ps_s[:, 0, :], ACT.Copy).then_inc(sem["oT0"], 1)

            @block.vector
            def _(dve):
                done = [0, 0]

                def step(ins, wait=True):
                    ins.then_inc(sem["chain"], 1)
                    done[1] += 1
                    if wait:
                        dve.wait_ge(sem["chain"], 1 + done[0] + done[1])

                dve.wait_ge(sem["win"], 1 + 16 * n_in)
                dve.tensor_scalar(hw[:, 0:2], hw[:, 0:2], SCALE, None, ALU.mult).then_inc(sem["hn"], 1)
                dve.wait_ge(sem["hn"], 1 + 1)
                G_STEPS = 80
                with dve.Fori(0, B) as b:
                    for j in range(TB):
                        dve.bn_stats(st[:, j, :], x[:, b * TB + j, :]).then_inc(sem["stats"], 1)
                    hold(dve, sem["stats"], 1 + 2 * TB * b + TB, c["held"])
                    for j in range(TB):
                        dve.bn_aggr(mv[:, j, :], st[:, j, :]).then_inc(sem["stats"], 1)
                    dve.wait_ge(sem["stats"], 1 + 2 * TB * (b + 1))
                    dve.tensor_scalar(ve[:, :], mv[:, :, 1], LN_EPS, None, ALU.add).then_inc(sem["ve"], 1)
                    dve.wait_ge(sem["rs"], 1 + b + 1)
                    for j in range(TB):
                        i = dve.tensor_scalar(xnb[:, j, :], x[:, b * TB + j, :], mv[:, j, 0:1], rs[:, j:j + 1],
                                              ALU.subtract, ALU.mult)
                    i.then_inc(sem["xnb"], 1)
                    for k in range(KH):
                        dve.wait_ge(sem["xtr"], 1 + KH * b + k + 1)
                        dve.tensor_copy(xnT[:, k, :], ps_pt[:, k % 2, :]).then_inc(sem["xnT"], 1)
                    with dve.Fori(0, NG) as g:
                        G = b * NG + g
                        done[0], done[1] = G * G_STEPS, 0
                        kv = ps_w[:, 1:3, :].rearrange("p a (j h z d) -> p (a j) h z d", j=2, h=HG, z=2)
                        dve.wait_ge(sem["kv"], 1 + G + 1)
                        step(dve.tensor_copy(hd[:, N:QK, :].rearrange("p (j h) d -> p j h d", h=HG), kv[:, :, :, 0, :]),
                             wait=False)
                        dve.tensor_copy(v[:, :, :, :], kv[:, :, :, 1, :]).then_inc(sem["cv"], 1)
                        dve.wait_ge(sem["cq"], 1 + 2 * (G + 1))
                        dview = ps_s[0:ND, 2, 0:HG * 2 * HD].rearrange("p (h z d) -> p h z d", h=HG, z=2)
                        step(dve.tensor_tensor(dv[:, :, :], dview[:, :, 1, :], mask_r[:, :, :], ALU.mult))
                        step(dve.tensor_reduce(mu[:, :], hd[:, :, :], AX_X, ALU.add))
                        step(dve.tensor_scalar(mu[:, :], mu[:, :], 1.0 / HD, None, ALU.mult))
                        dve.tensor_tensor(hd[:, :, :], hd[:, :, :], bc(mu[:, :], 2, HD), ALU.subtract).then_inc(sem["cent"], 1)
                        dve.wait_ge(sem["sq"], 1 + G + 1)
                        step(dve.tensor_reduce(hv[:, :], hsq[:, :, :], AX_X, ALU.add))
                        dve.tensor_scalar(hv[:, :], hv[:, :], 1.0 / HD, HEAD_EPS, ALU.mult, ALU.add).then_inc(sem["var"], 1)
                        dve.wait_ge(sem["sqrt"], 1 + G + 1)
                        step(dve.reciprocal(mu[:, :], hv[:, :]))
                        dve.tensor_tensor(hd[:, :, :], hd[:, :, :], bc(mu[:, :], 2, HD), ALU.mult).then_inc(sem["hn"], 1)
                        dve.wait_ge(sem["htr"], 1 + 3 * G + 1)
                        dve.tensor_scalar(qT[:, :], ps_w[:, 0, :], hw[:, 0:1], hw[:, 1:2], ALU.mult, ALU.add)\
                           .then_inc(sem["htrc"], 1)
                        dve.wait_ge(sem["htr"], 1 + 3 * G + 2)
                        dve.tensor_scalar(kT[:, 0:S2], ps_w[:, 1, 0:S2], hw[:, 2:3], hw[:, 3:4], ALU.mult, ALU.add)\
                           .then_inc(sem["htrc"], 1)
                        dve.wait_ge(sem["htr"], 1 + 3 * G + 3)
                        step(dve.tensor_scalar(kd[:, :, :].rearrange("p h s -> p (h s)"), ps_w[:, 2, 0:ND], hw[:, 4:5],
                                               hw[:, 5:6], ALU.mult, ALU.add))
                        dve.tensor_tensor(kd[:, :, :], kd[:, :, :], mask_c[:, :, :], ALU.mult).then_inc(sem["htrc"], 1)
                        sdv = ps_w[:, 0, 0:N * DCA].rearrange("p (a s) -> p a s", s=DCA)
                        dve.wait_ge(sem["sd"], 1 + G + 1)
                        step(dve.tensor_reduce(md[:, :], sdv, AX_X, ALU.max))
                        dve.tensor_tensor(sd[:, :, :], sdv, bc(md[:, :], 2, DCA), ALU.subtract).then_inc(sem["sdc"], 1)
                        dve.wait_ge(sem["pdexp"], 1 + G + 1)
                        step(dve.tensor_reduce(md[:, :], sd[:, :, :], AX_X, ALU.add))
                        step(dve.reciprocal(md[:, :], md[:, :]))
                        dve.tensor_tensor(sd[:, :, :], sd[:, :, :], bc(md[:, :], 2, DCA), ALU.mult).then_inc(sem["pd"], 1)

                        def turned(n):
                            if n % 2 == 0:
                                dve.wait_ge(sem["ptr"], 1 + G * N + n + 1)
                                dve.tensor_copy(pt[:, 0, :, :], ps_pt[:, 0, :].rearrange("p (j s) -> p j s", s=P))\
                                   .then_inc(sem["pt0"], 1)

                        def finish(j):
                            a = slice(j * HG, (j + 1) * HG)
                            dve.wait_ge(sem["pv"], 1 + G * N + (j + 1) * HG)
                            step(dve.reciprocal(rm[:, a], sm[:, a]))
                            cv = ct[:, j, :].rearrange("p (h d) -> p h d", d=HD)
                            step(dve.tensor_tensor(cv, ps_w[:, j % 2, 0:GW].rearrange("p (h d) -> p h d", d=HD),
                                                   bc(rm[:, a], 2, HD), ALU.mult))
                            dve.wait_ge(sem["cd"], 1 + G + 1)
                            dve.tensor_tensor(ctxo[:, j, bass.ds(g * GW, GW)], ct[:, j, :], cd[:, j, :], ALU.add)\
                               .then_inc(sem["ctxo"], 1)

                        for n in range(N):
                            dve.wait_ge(sem["s"], 1 + G * N + n + 1)
                            dve.tensor_reduce(nm[:, n:n + 1], ps_s[:, n % 3, 0:S2], AX_X, ALU.max, negate=True)\
                               .then_inc(sem["max"], 1)
                            if n >= 2:
                                turned(n - 2)
                            if n >= 5 and (n - 5) % HG == HG - 1:
                                finish((n - 5) // HG)
                        for n in range(N - 2, N):
                            turned(n)
                        for j in range((N - 6) // HG, TB):
                            if (j + 1) * HG + 4 >= N:
                                finish(j)
                        assert done[1] <= G_STEPS
                        dve.sem_inc(sem["chain"], G_STEPS - done[1])
                    for k in (1, 3):
                        dve.wait_ge(sem["otr"], 1 + KH * b + k + 1)
                        dve.tensor_copy(oT[:, k, :], ps_s[:, 1, :]).then_inc(sem["oT1"], 1)
                    for j in range(TB):
                        dve.wait_ge(sem["om"], 1 + TB * b + j + 1)
                        xt = x[:, b * TB + j, :]
                        dve.tensor_tensor(xt, ps_w[:, j % 2, :], xt, ALU.add).then_inc(sem["xadd"], 1)

            @block.tensor
            def _(pe):
                pe.wait_ge(sem["win"], 1 + 16 * n_in)
                ones = c["ones_row"]
                with pe.Fori(0, B) as b:
                    pe.wait_ge(sem["xnb"], 1 + b + 1)
                    for k in range(KH):
                        pe.wait_ge(sem["xnT"], 1 + KH * b + max(k - 1, 0))
                        for j in range(TB):
                            i = pe.transpose(ps_pt[:, k % 2, j * P:(j + 1) * P], xnb[:, j, k * P:(k + 1) * P],
                                             c["ident"][:, :])
                        i.then_inc(sem["xtr"], 1)
                    pe.wait_ge(sem["xnT"], 1 + KH * (b + 1))
                    pe.wait_ge(sem["ctx"], 1 + 16 * (b + 1))
                    pe.wait_ge(sem["ctxd"], 1 + b + 1)
                    hold(pe, sem["xadd"], 1 + TB * b, c["held"])
                    with pe.Fori(0, NG) as g:
                        G = b * NG + g
                        gq, gkv = bass.ds(g * GW, GW), bass.ds(g * 2 * GW, 2 * GW)
                        pe.wait_ge(sem["ctxo"], 1 + TB * G)
                        for j in range(TB):
                            o = ps_w[:, 0, j * P:(j + 1) * P]
                            for k in range(KH):
                                pe.matmul(o, xnT[:, k, j * P:(j + 1) * P], wq[:, k, gq], start=k == 0, stop=False)
                            i = pe.matmul(o, ones[:, :], bq[0:1, gq], start=False, stop=True)
                        i.then_inc(sem["q"], 1)
                        for k in range(KC):
                            pe.matmul(ps_s[:, 2, 0:2 * GW], ctxd[:, k, :, :].rearrange("p h s -> p (h s)"),
                                      wkvd[:, k, gkv], start=k == 0, stop=False)
                        pe.matmul(ps_s[:, 2, 0:2 * GW], ones[:, :], bkvd[0:1, gkv], start=False, stop=True)\
                          .then_inc(sem["d"], 1)
                        for j in range(TB):
                            o = ps_w[:, 1 + j // 2, (j % 2) * 2 * GW:(j % 2 + 1) * 2 * GW]
                            for k in range(KC):
                                pe.matmul(o, ctxT[:, k, j * P:(j + 1) * P], wkv[:, k, gkv], start=k == 0, stop=False)
                            i = pe.matmul(o, ones[:, :], bkv[0:1, gkv], start=False, stop=True)
                        i.then_inc(sem["kv"], 1)
                        pe.wait_ge(sem["hn"], 1 + G + 2)
                        pe.wait_ge(sem["cv"], 1 + G + 1)
                        for z in range(2):
                            for j in range(TB):
                                i = pe.transpose(ps_w[:, z, j * P:(j + 1) * P],
                                                 hd[:, (z * TB + j) * HG:(z * TB + j + 1) * HG, :].rearrange(f3), c["ident"][:, :])
                            i.then_inc(sem["htr"], 1)
                        pe.transpose(ps_w[:, 2, 0:ND], hd[0:ND, QK:NR, :].rearrange(f3), c["ident"][0:ND, 0:ND])\
                          .then_inc(sem["htr"], 1)
                        pe.wait_ge(sem["htrc"], 1 + 3 * (G + 1))
                        for j in range(TB):
                            i = pe.matmul(ps_w[:, 0, j * ND:(j + 1) * ND], qT[:, j * P:(j + 1) * P],
                                          kd[:, :, :].rearrange("p h s -> p (h s)"), start=True, stop=True)
                        i.then_inc(sem["sd"], 1)

                        def scores(n):
                            j, hh = n // HG, n % HG
                            if n >= 3:
                                pe.wait_ge(sem["exp"], 1 + G * N + n - 2)
                            strip = slice(hh * HD, (hh + 1) * HD)
                            pe.matmul(ps_s[:, n % 3, 0:S2], qT[strip, j * P:(j + 1) * P], kT[strip, 0:S2],
                                      start=True, stop=True).then_inc(sem["s"], 1)

                        def turn(n):
                            pe.wait_ge(sem["exp"], 1 + G * N + n + 1)
                            half = G * (N // 2) + n // 2
                            pe.wait_ge(sem["pt0"] if n % 2 == 0 else sem["pt1"], 1 + half)
                            for a in range(TB):
                                i = pe.transpose(ps_pt[:, n % 2, a * P:(a + 1) * P], p[:, n % 2, a * P:(a + 1) * P],
                                                 c["ident"][:, :])
                            i.then_inc(sem["ptr"], 1)

                        def weigh(n):
                            j, hh = n // HG, n % HG
                            half = G * (N // 2) + n // 2
                            pe.wait_ge(sem["pt0"] if n % 2 == 0 else sem["pt1"], 1 + half + 1)
                            if n % HG == 0 and j >= 2:
                                pe.wait_ge(sem["ctxo"], 1 + G * TB + j - 1)
                            for a in range(TB):
                                i = pe.matmul(ps_w[:, j % 2, hh * HD:(hh + 1) * HD], pt[:, n % 2, a, :], v[:, a, hh, :],
                                              start=a == 0, stop=a == TB - 1)
                            i.then_inc(sem["pv"], 1)

                        scores(0)
                        scores(1)
                        hold(pe, sem["pd"], 1 + G + 1, c["held"])
                        for j in range(TB):
                            i = pe.transpose(ps_w[0:ND, 1, j * P:(j + 1) * P],
                                             sd[:, j * HG:(j + 1) * HG, :].rearrange(f3), c["ident"][:, :])
                        i.then_inc(sem["pdT"], 1)
                        pe.wait_ge(sem["pdTc"], 1 + G + 1)
                        for j in range(TB):
                            i = pe.matmul(ps_w[:, 2, j * GW:(j + 1) * GW], pdT[:, j, :], dv[:, :, :].rearrange(f3),
                                          start=True, stop=True)
                        i.then_inc(sem["cdmm"], 1)
                        for n in range(2, N + 3):
                            if n < N:
                                scores(n)
                            if 0 <= n - 2 < N:
                                turn(n - 2)
                            if n >= 3:
                                weigh(n - 3)
                    pe.wait_ge(sem["ctxo"], 1 + TB * NG * (b + 1))
                    for k in range(KH):
                        if k >= 2:
                            pe.wait_ge(sem["oT0"] if k == 2 else sem["oT1"], 1 + 2 * b + 1)
                        for j in range(TB):
                            i = pe.transpose(ps_s[:, k % 2, j * P:(j + 1) * P], ctxo[:, j, k * P:(k + 1) * P],
                                             c["ident"][:, :])
                        i.then_inc(sem["otr"], 1)
                    pe.wait_ge(sem["oT0"], 1 + 2 * (b + 1))
                    pe.wait_ge(sem["oT1"], 1 + 2 * (b + 1))
                    for j in range(TB):
                        if j >= 2:
                            pe.wait_ge(sem["xadd"], 1 + TB * b + j - 1)
                        for k in range(KH):
                            pe.matmul(ps_w[:, j % 2, :], oT[:, k, j * P:(j + 1) * P], wo[:, k, :], start=k == 0, stop=False)
                        pe.matmul(ps_w[:, j % 2, :], ones[:, :], bo[0:1, :], start=False, stop=True).then_inc(sem["om"], 1)


def program(nc, I, out, upto=9):
    with ExitStack() as ctx:
        pl = Pools(nc, ctx)
        D = {"bc": nc.dram_tensor("bc_rows", (B * 2 * NST, S), F32).ap(),
             "xs0": nc.dram_tensor("slots_in0", (NSLOT0, H), F32).ap(),
             "xs1": nc.dram_tensor("slots_in1", (NSLOT1, H), F32).ap(),
             "y0": nc.dram_tensor("slots_out0", (NSLOT0, H), F32).ap(),
             "y1": nc.dram_tensor("slots_out1", (NSLOT1, H), F32).ap(),
             "expert": nc.dram_tensor("tile_expert", (2 * P, 1), I32).ap()}
        c = {}
        x = pl.sb("x_resid", [P, NT, H])
        constants(nc, pl, c)
        mamba_stage(nc, pl, c, I, D, x)
        def routes(L, K):
            return {"scat": pl.sb(f"scat{L}", [P, NT, K], I32), "gath": pl.sb(f"gath{L}", [P, NT, K], I32),
                    "wsel": pl.sb(f"wsel{L}", [P, NT, K])}

        if upto >= 2:
            route0 = routes(0, K0)
            route_stage(nc, c, I, D, x, 0, route0)
        if upto >= 3:
            expert_stage0(nc, c, I, D)
            combine_stage(nc, c, I, D, x, 0, route0)
        if upto >= 4:
            attention_stage(nc, c, I, D, x)
        if upto >= 5:
            route1 = routes(1, K1)
            route_stage(nc, c, I, D, x, 1, route1)
        if upto >= 6:
            expert_stage1(nc, c, I, D)
            combine_stage(nc, c, I, D, x, 1, route1)
        stored = pl.sem("stored")
        with nc.Block() as block:

            @block.sync
            def _(sp):
                sp.dma_start(out.rearrange("(t p) h -> p t h", p=P), x[:, :, :]).then_inc(stored, 16)
                sp.wait_ge(stored, 16)


def layouts(a):
    f = np.ascontiguousarray
    col = lambda v: f(v.reshape(TB, P).T)
    i = {"x": f(a["x"].reshape(T, H)), "ctxT": f(a["ctx_1024"].reshape(T, DM).T),
         "in_projT": f(a["L0_xattn_in_proj_w"].T), "x_projT": f(a["L0_xattn_x_proj_w"].T),
         "dt_projT": f(a["L0_xattn_dt_proj_w"].T), "conv_w": f(a["L0_xattn_conv_w"].reshape(H, CONV)),
         "conv_b": col(a["L0_xattn_conv_b"]), "dt_b": col(a["L0_xattn_dt_proj_b"]), "d_col": col(a["L0_xattn_D"]),
         "a_log": f(a["L0_xattn_A_log"].reshape(TB, P, NST).transpose(1, 2, 0).reshape(P, NST * TB))}
    i["wr0"] = f(np.concatenate([a["L0_ffn_Wr"], a["L0_ffn_Wse"]], 1))
    i["wsg0"], i["wsu0"], i["wsd0"] = (f(a["L0_ffn_" + n]) for n in ("Wsg", "Wsu", "Wsd"))
    i["wg0"], i["wu0"], i["wd0"] = (f(a["L0_ffn_" + n]) for n in ("Wg", "Wu", "Wd"))
    i["wr1"] = f(a["L1_ffn_router_w"])
    i["rbias"] = f(a["L1_ffn_router_bias"].reshape(1, E))
    i["wsg1"], i["wsu1"], i["wsd1"] = (f(a["L1_ffn_" + n]) for n in ("sw_gate", "sw_up", "sw_down"))
    i["wg1"], i["wu1"], i["wd1"] = (f(a["L1_ffn_" + n]) for n in ("w_gate", "w_up", "w_down"))
    i["wq"], i["wo"] = f(a["L1_xattn_Wq"]), f(a["L1_xattn_Wo"])
    i["wkv"] = f(np.concatenate([a["L1_xattn_Wk"], a["L1_xattn_Wv"]], 1))
    i["wkvd"] = f(a["L1_xattn_Wkv_dca"].reshape(DM, 2, NH, HD).transpose(0, 2, 1, 3).reshape(DM, 2 * H))
    i["bkvd"] = f(a["L1_xattn_bkv_dca"].reshape(2, NH, HD).transpose(1, 0, 2).reshape(1, 2 * H))
    i["bkv"] = f(np.concatenate([a["L1_xattn_bk"], a["L1_xattn_bv"]]).reshape(1, 2 * H))
    i["bq"], i["bo"] = f(a["L1_xattn_bq"].reshape(1, H)), f(a["L1_xattn_bo"].reshape(1, H))
    i["headnorm"] = f(np.stack([a["L1_xattn_" + n] for n in ("qn_w", "qn_b", "kn_w", "kn_b", "kn_dca_w", "kn_dca_b")], 1))
    return i


def kernel(**inputs):
    import concourse.bacc as bacc
    from concourse.bass_utils import run_bass_kernel_spmd

    nc = bacc.Bacc("TRN2", target_bir_lowering=False, num_devices=1)
    host = layouts({k: np.asarray(v) for k, v in inputs.items()})
    I = {k: nc.dram_tensor("in_" + k, v.shape, mybir.dt.from_np(v.dtype), kind="ExternalInput").ap()
         for k, v in host.items()}
    out = nc.dram_tensor("out_x", (T, H), F32, kind="ExternalOutput").ap()
    program(nc, I, out)
    r = run_bass_kernel_spmd(nc, [{"in_" + k: v for k, v in host.items()}], core_ids=[0])
    return r.results[0]["out_x"].reshape(B, S, H)
```

```python
from contextlib import ExitStack

import numpy as np

import concourse.bass as bass
from concourse import mybir

F32 = mybir.dt.float32
BF16 = mybir.dt.bfloat16
I32 = mybir.dt.int32
ALU = mybir.AluOpType
ACT = mybir.ActivationFunctionType
AX_X = mybir.AxisListType.X

P = 128
B, S, H = 4, 512, 512
T = B * S
NT = T // P
TB = S // P
KH = H // P
DM = 256
KC = DM // P
LN_EPS = 1e-5

NST, RK, CONV = 16, 16, 4
XD = RK + 2 * NST

E = 32
F0, FS0, CAP, K0 = 352, 1408, 64, 4
F1, FS1, K1 = 256, 512, 8
GR, GSEL = 8, 4
ROUTED = 2.5
NSLOT0 = E * CAP
NTILE1 = T * K1 // P + E
NSLOT1 = NTILE1 * P
SKIP = 1 << 20

NH, HD = 16, 32
DCA = 16
S2 = S - DCA
HG = 4
NG = NH // HG
GW = HG * HD
SCALE = float(HD) ** -0.5
HEAD_EPS = 1e-6


def bc(ap, axis, n):
    u = ap.unsqueeze(axis)
    shape = list(u.shape)
    shape[axis] = n
    return u.to_broadcast(shape)


def hold(eng, sem, value, held):
    eng.wait_ge(sem, value)
    eng.sem_inc(held, 1)


class Pools:

    def __init__(self, nc, ctx):
        self.nc, self.ctx, self.sems, self.from0 = nc, ctx, [], []

    def sb(self, name, shape, dt=F32):
        return self.ctx.enter_context(self.nc.sbuf_tensor(name, shape, dt))

    def ps(self, name, shape):
        return self.ctx.enter_context(self.nc.psum_tensor(name, shape, F32))

    def sem(self, name):
        self.sems.append(self.nc.alloc_semaphore(name))
        return self.sems[-1]

    def sem0(self, name):
        self.from0.append(self.sem(name))
        return self.from0[-1]

    def start_at_one(self):
        for i, s in enumerate(s for s in self.sems if s not in self.from0):
            (self.nc.gpsimd, self.nc.vector, self.nc.scalar, self.nc.sync)[i % 4].sem_inc(s, 1)
        self.nc.all_engine_barrier()

    def clear(self):
        self.nc.clear_and_free_semaphores(self.sems)
        self.nc.all_engine_barrier()


def constants(nc, pl, c):
    c["ident"] = pl.sb("ident", [P, P])
    c["zeros"] = pl.sb("zeros", [P, 2 * H])
    c["ones_bf"] = pl.sb("ones_bf", [P, P], BF16)
    c["before_bf"] = pl.sb("before_bf", [P, P], BF16)
    c["ones_row"] = pl.sb("ones_row", [1, P])
    c["seg"] = pl.sb("seg", [P, TB * E])
    c["slot0"] = pl.sb("slot0", [P, E])
    c["tile_no"] = pl.sb("tile_no", [P, 2])
    c["minus_half"] = pl.sb("minus_half", [P, E])
    c["half_seg8"] = pl.sb("half_seg8", [P, TB * GR])
    tri_all = pl.sb("tri_all", [P, P])
    idx_i = pl.sb("idx_i", [P, E], I32)
    tile_i = pl.sb("tile_i", [P, 2], I32)
    made, filled, cast = pl.sem("const_made"), pl.sem("const_filled"), pl.sem("const_cast")
    c["held"] = pl.sem("held")
    with nc.Block() as block:

        @block.gpsimd
        def _(pool):
            pool.memset(c["ident"][:, :], 0.0).then_inc(filled, 1)
            pool.memset(tri_all[:, :], 1.0).then_inc(filled, 1)
            pool.memset(c["seg"][:, :], 1.0).then_inc(filled, 1)
            pool.memset(c["half_seg8"][:, :], 1.0).then_inc(filled, 1)
            pool.memset(c["zeros"][:, :], 0.0).then_inc(filled, 1)
            pool.memset(c["ones_bf"][:, :], 1.0).then_inc(filled, 1)
            pool.memset(c["ones_row"][:, :], 1.0).then_inc(filled, 1)
            pool.memset(c["minus_half"][:, :], -0.5).then_inc(filled, 1)
            pool.iota(idx_i[:, :], [[CAP, E]], base=1, channel_multiplier=0).then_inc(filled, 1)
            pool.iota(tile_i[:, :], [[1, 2]], base=0, channel_multiplier=2).then_inc(filled, 1)
            pool.wait_ge(filled, 10)
            pool.affine_select(out=c["ident"][:, :], in_=c["ident"][:, :], compare_op=ALU.not_equal, fill=1.0,
                               base=0, pattern=[[-1, P]], channel_multiplier=1).then_inc(made, 1)
            pool.affine_select(out=tri_all[:, :], in_=tri_all[:, :], compare_op=ALU.is_gt, fill=0.0,
                               base=0, pattern=[[1, P]], channel_multiplier=-1).then_inc(made, 1)
            seg = c["seg"][:, :].rearrange("p (t e) -> p t e", e=E)
            pool.memset(seg[:, :, 0], 0.0).then_inc(made, 1)
            seg8 = c["half_seg8"][:, :].rearrange("p (t e) -> p t e", e=GR)
            pool.memset(seg8[:, :, 0], 0.0).then_inc(made, 1)

        @block.vector
        def _(dve):
            dve.wait_ge(made, 4)
            dve.wait_ge(filled, 10)
            dve.tensor_copy(c["before_bf"][:, :], tri_all[:, :]).then_inc(cast, 1)
            dve.tensor_copy(c["slot0"][:, :], idx_i[:, :]).then_inc(cast, 1)
            dve.tensor_copy(c["tile_no"][:, :], tile_i[:, :]).then_inc(cast, 1)


def mamba_stage(nc, pl0, c, I, D, x):
    with ExitStack() as ctx:
        pl = Pools(nc, ctx)
        ctx.callback(pl.clear)
        w_in = pl.sb("w_in", [P, KC, H])
        w_xp = pl.sb("w_xp", [P, KH, XD])
        w_dt = pl.sb("w_dt", [RK, H])
        conv_w = pl.sb("conv_w", [P, TB, CONV])
        conv_b = pl.sb("conv_b", [P, TB])
        dt_b = pl.sb("dt_b", [P, TB])
        a_log = pl.sb("a_log", [P, NST, TB])
        a_neg = pl.sb("a_neg", [P, NST, TB])
        d_col = pl.sb("d_col", [P, TB])
        d_diag = pl.sb("d_diag", [P, TB, P])
        ctxT = pl.sb("ctxT", [P, KC, S])
        xpad = pl.sb("xpad", [P, TB, S + CONV - 1])
        conv = pl.sb("conv", [P, TB, S])
        u = pl.sb("u", [P, TB, S])
        xd = pl.sb("xd", [XD, S])
        dt = pl.sb("dt", [P, TB, S])
        du = pl.sb("du", [P, TB, S])
        tmp = pl.sb("tmp", [P, TB, S])
        gate = pl.sb("gate", [P, TB, S])
        dA = pl.sb("dA", [P, 2, TB, S])
        dBu = pl.sb("dBu", [P, TB, S])
        hs = pl.sb("hs", [P, 2, TB, S])
        hc = pl.sb("hc", [P, 2, TB, S])
        bcst = pl.sb("bcst", [P, 2, 2, S])
        st = pl.sb("st", [P, TB, 6])
        mv = pl.sb("mv", [P, TB, 2])
        ve = pl.sb("ve", [P, TB])
        rs = pl.sb("rs", [P, TB])
        nb = pl.sb("nb", [P, TB])
        ps_y = pl.ps("ps_y", [P, TB, S])
        ps_w = pl.ps("ps_w", [P, TB, S])

        sem = {n: pl.sem("m_" + n) for n in (
            "weights", "xin", "ctxin", "pad", "aexp", "aneg", "diag", "inproj", "xpadc", "conv", "u", "xproj", "xdc",
            "bcout", "bcin0", "bcin1", "bfree", "cfree", "dtmm", "spa", "spb", "spc", "spd", "spe", "spm", "dt", "du",
            "dA", "dAfree", "dBu", "scan", "hsfree", "hc", "hcfree", "seed",
            "stats", "ve", "rs", "nb", "gate", "yz", "tr", "xadd")}
        sem["zfill"] = pl.sem0("m_zfill")
        bcin = (sem["bcin0"], sem["bcin1"])
        n_weights = 8
        n_zero = (NSLOT0 + NSLOT1) // (2 * P)

        pl.start_at_one()
        with nc.Block() as block:

            @block.sync
            def _(sp):
                for dst, src in ((w_in[:, :, :], I["in_projT"].rearrange("(k p) n -> p k n", p=P)),
                                 (w_xp[:, :, :], I["x_projT"].rearrange("(k p) n -> p k n", p=P)),
                                 (w_dt[:, :], I["dt_projT"]),
                                 (conv_w[:, :, :], I["conv_w"].rearrange("(t p) j -> p t j", p=P)),
                                 (conv_b[:, :], I["conv_b"]), (dt_b[:, :], I["dt_b"]),
                                 (a_log[:, :, :], I["a_log"].rearrange("p (n t) -> p n t", t=TB)),
                                 (d_col[:, :], I["d_col"])):
                    sp.dma_start(dst, src).then_inc(sem["weights"], 16)
                sp.dma_start(x[:, :, :], I["x"].rearrange("(t p) h -> p t h", p=P)).then_inc(sem["xin"], 16)
                with sp.Fori(0, B) as b:
                    hold(sp, sem["inproj"], 1 + TB * b, c["held"])
                    sp.dma_start(ctxT[:, :, :], I["ctxT"][:, bass.ds(b * S, S)].rearrange("(k p) n -> p k n", p=P))\
                      .then_inc(sem["ctxin"], 16)
                    hold(sp, sem["xdc"], 1 + b + 1, c["held"])
                    sp.dma_start(D["bc"][bass.ds(b * 2 * NST, 2 * NST), :], xd[RK:XD, :]).then_inc(sem["bcout"], 16)
                    with sp.Fori(0, NST // 2) as n2:
                        for q in range(2):
                            hold(sp, sem["bcout"], 1 + 16 * (b + 1), c["held"])
                            hold(sp, sem["bfree"], 1 + b * NST + n2 * 2 + q + 1, c["held"])
                            hold(sp, sem["cfree"], 1 + b * NST + n2 * 2 + q + 1, c["held"])
                            for w in range(2):
                                row = D["bc"][bass.ds(b * 2 * NST + w * NST + n2 * 2 + q, 1), :]
                                sp.dma_start(bcst[:, q, w, :], row.to_broadcast([P, S])).then_inc(bcin[q], 16)

            @block.gpsimd
            def _(pool):
                pool.sem_inc(sem["cfree"], 2)
                for buf, rows in ((D["xs1"], NSLOT1), (D["xs0"], NSLOT0)):
                    with pool.Fori(0, rows // (2 * P)) as i:
                        pool.dma_start(buf[bass.ds(i * 2 * P, 2 * P), :].rearrange("(p a) h -> p (a h)", a=2),
                                       c["zeros"][:, :]).then_inc(sem["zfill"], 16)
                with pool.Fori(0, B) as b:
                    pool.wait_ge(sem["ve"], 1 + b + 1)
                    pool.tensor_tensor(rs[:, :], ve[:, :], c["minus_half"][:, 0:TB], ALU.pow).then_inc(sem["rs"], 1)
                    with pool.Fori(0, NST // 2) as n2:
                        for q in range(2):
                            it = b * NST + n2 * 2 + q
                            pool.wait_ge(bcin[q], 1 + 32 * (b * (NST // 2) + n2 + 1))
                            pool.wait_ge(sem["scan"], 1 + it + 1)
                            pool.wait_ge(sem["hcfree"], 1 + it + 1)
                            pool.tensor_tensor(hc[:, q, :, :], hs[:, q, :, :], bc(bcst[:, q, 1, :], 1, TB), ALU.mult)\
                                .then_inc(sem["hc"], 1)
                            pool.wait_ge(sem["hc"], 1 + it + 1)
                            pool.sem_inc(sem["cfree"], 1)
                            pool.sem_inc(sem["hsfree"], 1)
                pool.wait_ge(sem["zfill"], 16 * n_zero)

            @block.scalar
            def _(act):
                act.wait_ge(sem["weights"], 1 + 16 * n_weights)
                act.activation(a_neg[:, :, :], a_log[:, :, :], ACT.Exp).then_inc(sem["aexp"], 1)
                with act.Fori(0, B) as b:
                    for t in range(TB):
                        act.wait_ge(sem["inproj"], 1 + TB * b + t + 1)
                        act.wait_ge(sem["conv"], 1 + TB * b)
                        act.wait_ge(sem["pad"], 1 + 1)
                        act.activation(xpad[:, t, CONV - 1:], ps_w[:, t, :], ACT.Copy).then_inc(sem["xpadc"], 1)
                    act.wait_ge(sem["yz"], 1 + b)
                    for t in range(TB):
                        act.wait_ge(sem["conv"], 1 + TB * b + t + 1)
                        act.activation(u[:, t, :], conv[:, t, :], ACT.Silu, bias=conv_b[:, t:t + 1]).then_inc(sem["u"], 1)
                    for t in range(TB):
                        act.wait_ge(sem["dtmm"], 1 + TB * b + t + 1)
                        act.activation(tmp[:, t, :], ps_w[:, t, :], ACT.Abs, bias=dt_b[:, t:t + 1]).then_inc(sem["spa"], 1)
                    act.wait_ge(sem["spa"], 1 + TB * (b + 1))
                    act.activation(tmp[:, :, :], tmp[:, :, :], ACT.Exp, scale=-1.0).then_inc(sem["spb"], 1)
                    act.wait_ge(sem["spc"], 1 + b + 1)
                    act.activation(gate[:, :, :], conv[:, :, :], ACT.Ln).then_inc(sem["spd"], 1)
                    act.wait_ge(sem["dt"], 1 + b + 1)
                    act.wait_ge(sem["nb"], 1 + b + 1)
                    for t in range(TB):
                        act.activation(gate[:, t, :], x[:, b * TB + t, :], ACT.Silu, scale=rs[:, t:t + 1],
                                       bias=nb[:, t:t + 1]).then_inc(sem["gate"], 1)
                    act.wait_ge(sem["aneg"], 1 + 1)
                    with act.Fori(0, NST // 2) as n2:
                        for q in range(2):
                            act.wait_ge(sem["dAfree"], 1 + b * NST + n2 * 2 + q + 1)
                            for t in range(TB):
                                i = act.activation(dA[:, q, t, 1:], dt[:, t, 1:], ACT.Exp,
                                                   scale=a_neg[:, n2 * 2 + q, t:t + 1])
                            i.then_inc(sem["dA"], 1)

            @block.vector
            def _(dve):
                dve.sem_inc(sem["bfree"], 2)
                dve.sem_inc(sem["dAfree"], 2)
                dve.sem_inc(sem["hsfree"], 2)
                dve.memset(xpad[:, :, 0:CONV - 1], 0.0).then_inc(sem["pad"], 1)
                dve.memset(dA[:, :, :, 0:1], 0.0).then_inc(sem["diag"], 1)
                dve.wait_ge(sem["aexp"], 1 + 1)
                dve.tensor_scalar(a_neg[:, :, :], a_neg[:, :, :], -1.0, None, ALU.mult).then_inc(sem["aneg"], 1)
                for t in range(TB):
                    dve.tensor_scalar(d_diag[:, t, :], c["ident"][:, :], d_col[:, t:t + 1], None, ALU.mult)\
                       .then_inc(sem["diag"], 1)
                dve.wait_ge(sem["xin"], 1 + 16)
                dve.wait_ge(sem["diag"], 1 + 1)
                with dve.Fori(0, B) as b:
                    for t in range(TB):
                        dve.wait_ge(sem["xpadc"], 1 + TB * b + t + 1)
                        dve.tensor_scalar(conv[:, t, :], xpad[:, t, 0:S], conv_w[:, t, 0:1], None, ALU.mult)\
                           .then_inc(sem["spe"], 1)
                        for j in range(1, CONV):
                            dve.wait_ge(sem["spe"], 1 + (TB * b + t) * (CONV - 1) + j)
                            dve.scalar_tensor_tensor(out=conv[:, t, :], in0=xpad[:, t, j:j + S],
                                                     scalar=conv_w[:, t, j:j + 1], in1=conv[:, t, :],
                                                     op0=ALU.mult, op1=ALU.add)\
                               .then_inc(sem["spe"] if j < CONV - 1 else sem["conv"], 1)
                    for t in range(TB):
                        dve.bn_stats(st[:, t, :], x[:, b * TB + t, :]).then_inc(sem["stats"], 1)
                    hold(dve, sem["stats"], 1 + 2 * TB * b + TB, c["held"])
                    for t in range(TB):
                        dve.bn_aggr(mv[:, t, :], st[:, t, :]).then_inc(sem["stats"], 1)
                    dve.wait_ge(sem["stats"], 1 + 2 * TB * (b + 1))
                    dve.tensor_scalar(ve[:, :], mv[:, :, 1], LN_EPS, None, ALU.add).then_inc(sem["ve"], 1)
                    dve.wait_ge(sem["xproj"], 1 + b + 1)
                    dve.tensor_copy(xd[:, :], ps_w[0:XD, 0, :]).then_inc(sem["xdc"], 1)
                    dve.wait_ge(sem["rs"], 1 + b + 1)
                    dve.scalar_tensor_tensor(out=nb[:, :], in0=mv[:, :, 0], scalar=-1.0, in1=rs[:, :],
                                             op0=ALU.mult, op1=ALU.mult).then_inc(sem["nb"], 1)
                    for t in range(TB):
                        dve.wait_ge(sem["spa"], 1 + TB * b + t + 1)
                        dve.tensor_scalar(dt[:, t, :], ps_w[:, t, :], dt_b[:, t:t + 1], 0.0, ALU.add, ALU.max)\
                           .then_inc(sem["spm"], 1)
                    dve.wait_ge(sem["spb"], 1 + b + 1)
                    dve.wait_ge(sem["u"], 1 + TB * (b + 1))
                    dve.tensor_scalar(conv[:, :, :], tmp[:, :, :], 1.0, None, ALU.add).then_inc(sem["spc"], 1)
                    dve.wait_ge(sem["spd"], 1 + b + 1)
                    dve.scalar_tensor_tensor(out=tmp[:, :, :], in0=conv[:, :, :], scalar=-1.0, in1=tmp[:, :, :],
                                             op0=ALU.add, op1=ALU.subtract).then_inc(sem["du"], 1)
                    dve.wait_ge(sem["du"], 1 + 4 * b + 1)
                    dve.tensor_tensor(tmp[:, :, :], gate[:, :, :], tmp[:, :, :], ALU.subtract).then_inc(sem["du"], 1)
                    dve.wait_ge(sem["du"], 1 + 4 * b + 2)
                    dve.tensor_tensor(dt[:, :, :], dt[:, :, :], tmp[:, :, :], ALU.add).then_inc(sem["dt"], 1)
                    dve.wait_ge(sem["dt"], 1 + b + 1)
                    dve.tensor_tensor(du[:, :, :], dt[:, :, :], u[:, :, :], ALU.mult).then_inc(sem["du"], 1)
                    dve.wait_ge(sem["du"], 1 + 4 * b + 3)
                    dve.sem_inc(sem["du"], 1)
                    with dve.Fori(0, NST // 2) as n2:
                        for q in range(2):
                            it = b * NST + n2 * 2 + q
                            dve.wait_ge(bcin[q], 1 + 32 * (b * (NST // 2) + n2 + 1))
                            dve.tensor_tensor(dBu[:, :, :], du[:, :, :], bc(bcst[:, q, 0, :], 1, TB), ALU.mult)\
                               .then_inc(sem["dBu"], 1)
                            dve.wait_ge(sem["dBu"], 1 + it + 1)
                            dve.sem_inc(sem["bfree"], 1)
                            dve.wait_ge(sem["dA"], 1 + it + 1)
                            dve.wait_ge(sem["hsfree"], 1 + it + 1)
                            flat = "p t s -> p (t s)"
                            dve.tensor_tensor_scan(hs[:, q, :, :].rearrange(flat), dA[:, q, :, :].rearrange(flat),
                                                   dBu[:, :, :].rearrange(flat), 0.0, ALU.mult, ALU.add)\
                               .then_inc(sem["scan"], 1)
                            dve.wait_ge(sem["scan"], 1 + it + 1)
                            dve.sem_inc(sem["dAfree"], 1)
                    dve.wait_ge(sem["hcfree"], 1 + NST * (b + 1) + 2)
                    dve.wait_ge(sem["gate"], 1 + TB * (b + 1))
                    dve.tensor_tensor(gate[:, :, :], ps_y[:, :, :], gate[:, :, :], ALU.mult).then_inc(sem["yz"], 1)
                    dve.wait_ge(sem["tr"], 1 + b + 1)
                    xb = x[:, bass.ds(b * TB, TB), :]
                    dve.tensor_tensor(xb, ps_w[:, :, :], xb, ALU.add).then_inc(sem["xadd"], 1)

            @block.tensor
            def _(pe):
                pe.sem_inc(sem["hcfree"], 2)
                pe.wait_ge(sem["weights"], 1 + 16 * n_weights)
                pe.wait_ge(sem["diag"], 1 + 1 + TB)
                with pe.Fori(0, B) as b:
                    pe.wait_ge(sem["ctxin"], 1 + 16 * (b + 1))
                    pe.wait_ge(sem["xadd"], 1 + b)
                    for t in range(TB):
                        for k in range(KC):
                            i = pe.matmul(ps_w[:, t, :], w_in[:, k, t * P:(t + 1) * P], ctxT[:, k, :],
                                          start=k == 0, stop=k == KC - 1)
                        i.then_inc(sem["inproj"], 1)
                    pe.wait_ge(sem["u"], 1 + TB * (b + 1))
                    pe.wait_ge(sem["bcout"], 1 + 16 * b)
                    pe.wait_ge(sem["xpadc"], 1 + TB * (b + 1))
                    for k in range(KH):
                        i = pe.matmul(ps_w[0:XD, 0, :], w_xp[:, k, :], u[:, k, :], start=k == 0, stop=k == KH - 1)
                    i.then_inc(sem["xproj"], 1)
                    pe.wait_ge(sem["xdc"], 1 + b + 1)
                    for t in range(TB):
                        pe.matmul(ps_w[:, t, :], w_dt[:, t * P:(t + 1) * P], xd[0:RK, :], start=True, stop=True)\
                          .then_inc(sem["dtmm"], 1)
                    pe.wait_ge(sem["yz"], 1 + b)
                    for t in range(TB):
                        pe.matmul(ps_y[:, t, :], d_diag[:, t, :], u[:, t, :], start=True, stop=False,
                                  skip_group_check=True)
                    with pe.Fori(0, NST // 2) as n2:
                        for q in range(2):
                            pe.wait_ge(sem["hc"], 1 + b * NST + n2 * 2 + q + 1)
                            for t in range(TB):
                                i = pe.matmul(ps_y[:, t, :], c["ident"][:, :], hc[:, q, t, :], start=False,
                                              stop=False, skip_group_check=True)
                            i.then_inc(sem["hcfree"], 1)
                    pe.wait_ge(sem["yz"], 1 + b + 1)
                    for lt in range(TB):
                        for t in range(TB):
                            i = pe.transpose(ps_w[:, lt, t * P:(t + 1) * P], gate[:, t, lt * P:(lt + 1) * P],
                                             c["ident"][:, :])
                    i.then_inc(sem["tr"], 1)


def select(dve, pause, step, vals, m8, k, W, seg, gt, eq, cnt, cum):
    flat = "p t e -> p (t e)"
    pause()
    for j in range(TB):
        last = step(dve.max(m8[:, j, :], vals[:, j, :]), wait=j == TB - 1)
    kth = bc(m8[:, :, k - 1], 2, W)
    step(dve.tensor_tensor(gt, vals, kth, ALU.is_gt), wait=False)
    step(dve.tensor_tensor(eq, vals, kth, ALU.is_equal))
    step(dve.tensor_reduce(cnt, gt, AX_X, ALU.add), wait=False)
    step(dve.tensor_tensor_scan(cum.rearrange(flat), seg, eq.rearrange(flat), 0.0, ALU.mult, ALU.add))
    step(dve.tensor_tensor(cum, cum, bc(cnt, 2, W), ALU.add))
    step(dve.scalar_tensor_tensor(out=eq.rearrange(flat), in0=cum.rearrange(flat), scalar=float(k),
                                  in1=eq.rearrange(flat), op0=ALU.is_le, op1=ALU.mult))
    step(dve.tensor_tensor(gt, gt, eq, ALU.add))


def route_stage(nc, c, I, D, x, L, route):
    K, FS = (K0, FS0) if L == 0 else (K1, FS1)
    FC = FS // P
    NR = E + 1 if L == 0 else E
    R = f"r{L}_"
    slots = D["xs0"] if L == 0 else D["xs1"]
    nslot = NSLOT0 if L == 0 else NSLOT1
    scat, gath, wsel = route["scat"], route["gath"], route["wsel"]
    with ExitStack() as ctx:
        pl = Pools(nc, ctx)
        ctx.callback(pl.clear)
        sb = lambda n, shape, dt=F32: pl.sb(R + n, shape, dt)
        wr = sb("wr", [P, KH, NR])
        wg = sb("wg", [P, KH, FS])
        wu = sb("wu", [P, KH, FS])
        wd = sb("wd", [P, FC, H])
        xn = sb("xn", [P, NT, H])
        xnT = sb("xnT", [P, KH, T])
        h = sb("h", [P, max(FC, 2 * TB), S])
        xnb = h[:, 0:TB, :]
        xnTb = h[:, TB:2 * TB, :]
        sg = sb("sg", [P, 2, S])
        st = sb("st", [P, TB, 6])
        mv = sb("mv", [P, TB, 2])
        ve = sb("ve", [P, TB])
        rs = sb("rs", [P, TB])
        mx = sb("mx", [P, TB])
        sc = sb("sc", [P, TB, E])
        sel = sb("sel", [P, TB, E])
        eq = sb("eq", [P, TB, E])
        cum = sb("cum", [P, TB, E])
        cnt = sb("cnt", [P, TB])
        m8 = sb("m8", [P, TB, 8])
        k8 = sb("k8", [P, TB, 8])
        selb = sb("selb", [P, TB, E], BF16)
        acc = sb("acc", [P, E])
        accb = sb("accb", [P, E], BF16)
        base = sb("base", [P, E])
        gate = sb("gate", [P, NT])
        sel_all = sb("sel_all", [P, NT, E])
        pos_all = sb("pos_all", [P, NT, E])
        w_all = sb("w_all", [P, NT, E])
        hit = sb("hit", [P, TB, K, E])
        tk = sb("tk", [P, TB, K])
        if L == 1:
            bias = sb("bias", [P, E])
            sb_ = sb("sb", [P, TB, E])
            pr = sb("pr", [P, 4, TB * GR])
            gs = sb("gs", [P, TB, GR])
            gm = sb("gm", [P, TB, GR])
            geq = sb("geq", [P, TB, GR])
            gcum = sb("gcum", [P, TB, GR])
            ti = sb("ti", [P, E], I32)
            tf = sb("tf", [P, E])
            tcum = sb("tcum", [P, E])
            te = sb("te", [P, 2])
            tei = sb("tei", [P, 2], I32)
        ps_t = pl.ps(R + "ps_t", [P, 2, S])
        ps_r = pl.ps(R + "ps_r", [P, 512])
        ps_p = pl.ps(R + "ps_p", [P, 512])
        ps_g = pl.ps(R + "ps_g", [P, 2, S])
        ps_u = pl.ps(R + "ps_u", [P, 2, S])
        lg = ps_r[:, 0:TB * NR].rearrange("p (t e) -> p t e", e=NR)
        pp = ps_p[:, 0:TB * E].rearrange("p (t e) -> p t e", e=E)
        sem = {n: pl.sem(R + n) for n in (
            "win", "wrin", "stats", "ve", "rs", "xnb", "xn", "tr", "xnT0", "xnT1", "xnT", "logits", "centred", "score", "gate",
            "chain", "sel", "acc", "pos", "total", "posc", "idx", "g", "u", "sg", "h", "down", "xadd", "eid", "eidout")}
        sem["scat"] = pl.sem0(R + "scat")
        tiled = "(k p) n -> p k n"
        n_in = 3
        n_r = 2 if L == 1 else 1

        pl.start_at_one()
        with nc.Block() as block:

            @block.sync
            def _(sp):
                sp.dma_start(wr[:, :, :], I[f"wr{L}"].rearrange(tiled, p=P)).then_inc(sem["wrin"], 16)
                if L == 1:
                    sp.dma_start(bias[:, :], I["rbias"].to_broadcast([P, E])).then_inc(sem["wrin"], 16)
                sp.dma_start(wg[:, :, :], I[f"wsg{L}"].rearrange(tiled, p=P)).then_inc(sem["win"], 16)
                sp.dma_start(wu[:, :, :], I[f"wsu{L}"].rearrange(tiled, p=P)).then_inc(sem["win"], 16)
                sp.dma_start(wd[:, :, :], I[f"wsd{L}"].rearrange(tiled, p=P)).then_inc(sem["win"], 16)
                if L == 1:
                    sp.wait_ge(sem["eid"], 1 + 1)
                    sp.dma_start(D["expert"].rearrange("(p a) o -> p (a o)", a=2), tei[:, :]).then_inc(sem["eidout"], 16)
                    sp.wait_ge(sem["eidout"], 1 + 16)

            @block.gpsimd
            def _(pool):
                with pool.Fori(0, B) as b:
                    pool.wait_ge(sem["ve"], 1 + b + 1)
                    pool.tensor_tensor(rs[:, :], ve[:, :], c["minus_half"][:, 0:TB], ALU.pow).then_inc(sem["rs"], 1)
                    pool.wait_ge(sem["xnT0"], 1 + 2 * (b + 1))
                    pool.wait_ge(sem["xnT1"], 1 + 2 * (b + 1))
                    pool.tensor_copy(xnT[:, :, bass.ds(b * S, S)], xnTb).then_inc(sem["xnT"], 1)
                for t in range(NT):
                    pool.wait_ge(sem["idx"], 1 + t // TB + 1)
                    for k in range(K):
                        pool.indirect_dma_start(slots[:, :], bass.IndirectOffsetOnAxis(scat[:, t, k:k + 1], 0),
                                                xn[:, t, :], None, bounds_check=nslot - 1, oob_is_err=False)\
                            .then_inc(sem["scat"], 16)
                pool.wait_ge(sem["scat"], 16 * NT * K)

            @block.scalar
            def _(act):
                with act.Fori(0, B) as b:
                    for k in (0, 2):
                        act.wait_ge(sem["tr"], 1 + KH * b + k + 1)
                        act.wait_ge(sem["xnT"], 1 + b)
                        act.wait_ge(sem["logits"], 1 + b)
                        act.activation(xnTb[:, k, :], ps_t[:, 0, :], ACT.Copy).then_inc(sem["xnT0"], 1)
                    if L == 0:
                        act.wait_ge(sem["centred"], 1 + b + 1)
                        act.activation(sc[:, :, :], sc[:, :, :], ACT.Exp).then_inc(sem["score"], 1)
                        act.activation(gate[:, bass.ds(b * TB, TB)], lg[:, :, E], ACT.Sigmoid).then_inc(sem["gate"], 1)
                    else:
                        act.wait_ge(sem["logits"], 1 + b + 1)
                        act.wait_ge(sem["sel"], 1 + b)
                        act.activation(sc[:, :, :], lg[:, :, 0:E], ACT.Sigmoid).then_inc(sem["score"], 1)
                with act.Fori(0, B) as b:
                    for f in range(FC):
                        n = FC * b + f
                        act.wait_ge(sem["g"], 1 + n + 1)
                        if f >= 2:
                            act.wait_ge(sem["h"], 1 + n - 1)
                        else:
                            act.wait_ge(sem["h"], 1 + FC * b)
                        act.activation(sg[:, f % 2, :], ps_g[:, f % 2, :], ACT.Silu).then_inc(sem["sg"], 1)

            @block.vector
            def _(dve):
                done = [0, 0]

                def step(ins, wait=True):
                    ins.then_inc(sem["chain"], 1)
                    done[1] += 1
                    if wait:
                        dve.wait_ge(sem["chain"], 1 + done[0] + done[1])
                    return ins

                def pause():
                    dve.sem_inc(c["held"], 1)

                dve.memset(acc[:, :], 0.0).then_inc(sem["acc"], 1)
                dve.memset(accb[:, :], 0.0).then_inc(sem["acc"], 1)
                dve.wait_ge(sem["acc"], 1 + 2)
                R_STEPS = 32 if L == 0 else 48
                with dve.Fori(0, B) as b:
                    done[0], done[1] = b * R_STEPS, 0
                    for j in range(TB):
                        dve.bn_stats(st[:, j, :], x[:, b * TB + j, :]).then_inc(sem["stats"], 1)
                    hold(dve, sem["stats"], 1 + 2 * TB * b + TB, c["held"])
                    for j in range(TB):
                        dve.bn_aggr(mv[:, j, :], st[:, j, :]).then_inc(sem["stats"], 1)
                    dve.wait_ge(sem["stats"], 1 + 2 * TB * (b + 1))
                    dve.tensor_scalar(ve[:, :], mv[:, :, 1], LN_EPS, None, ALU.add).then_inc(sem["ve"], 1)
                    dve.wait_ge(sem["rs"], 1 + b + 1)
                    dve.wait_ge(sem["tr"], 1 + KH * b)
                    for j in range(TB):
                        for dst in (xnb[:, j, :], xn[:, b * TB + j, :]):
                            i = dve.tensor_scalar(dst, x[:, b * TB + j, :], mv[:, j, 0:1], rs[:, j:j + 1],
                                                  ALU.subtract, ALU.mult)
                    i.then_inc(sem["xnb"], 1)
                    for k in (1, 3):
                        dve.wait_ge(sem["tr"], 1 + KH * b + k + 1)
                        dve.wait_ge(sem["xnT"], 1 + b)
                        dve.wait_ge(sem["logits"], 1 + b)
                        dve.tensor_copy(xnTb[:, k, :], ps_t[:, 1, :]).then_inc(sem["xnT1"], 1)
                    dve.wait_ge(sem["logits"], 1 + b + 1)
                    if L == 0:
                        dve.wait_ge(sem["wrin"], 1 + 16)
                        step(dve.tensor_reduce(mx[:, :], lg[:, :, 0:E], AX_X, ALU.max))
                        dve.tensor_tensor(sc[:, :, :], lg[:, :, 0:E], bc(mx[:, :], 2, E), ALU.subtract)\
                           .then_inc(sem["centred"], 1)
                        dve.wait_ge(sem["score"], 1 + b + 1)
                        chosen_from = sc
                    else:
                        dve.wait_ge(sem["wrin"], 1 + 32)
                        dve.wait_ge(sem["score"], 1 + b + 1)
                        step(dve.tensor_tensor(sb_[:, :, :], sc[:, :, :], bc(bias[:, :], 1, TB), ALU.add))
                        four = sb_[:, :, :].rearrange("p t (g i) -> p (t g) i", i=GR // 2)
                        mx01, mn01, mx23, mn23 = (pr[:, i, :] for i in range(4))
                        step(dve.tensor_tensor(mx01, four[:, :, 0], four[:, :, 1], ALU.max), wait=False)
                        step(dve.tensor_tensor(mn01, four[:, :, 0], four[:, :, 1], ALU.min), wait=False)
                        step(dve.tensor_tensor(mx23, four[:, :, 2], four[:, :, 3], ALU.max), wait=False)
                        step(dve.tensor_tensor(mn23, four[:, :, 2], four[:, :, 3], ALU.min))
                        gflat = gs[:, :, :].rearrange("p t g -> p (t g)")
                        step(dve.tensor_tensor(mn01, mn01, mn23, ALU.max))
                        step(dve.tensor_tensor(mn23, mx01, mx23, ALU.min), wait=False)
                        step(dve.tensor_tensor(gflat, mx01, mx23, ALU.max))
                        step(dve.tensor_tensor(mn01, mn01, mn23, ALU.max))
                        step(dve.tensor_tensor(gflat, gflat, mn01, ALU.add))
                        select(dve, pause, step, gs[:, :, :], m8[:, :, :], GSEL, GR, c["half_seg8"][:, :],
                               gm[:, :, :], geq[:, :, :], cnt[:, :], gcum[:, :, :])
                        step(dve.tensor_tensor(sb_[:, :, :].rearrange("p t (g i) -> p (t g) i", i=GR // 2),
                                               four, bc(gm[:, :, :].rearrange("p t g -> p (t g)"), 2, GR // 2),
                                               ALU.mult))
                        chosen_from = sb_
                    dve.wait_ge(sem["pos"], 1 + b)
                    select(dve, pause, step, chosen_from[:, :, :], m8[:, :, :], K, E, c["seg"][:, :],
                           sel[:, :, :], eq[:, :, :], cnt[:, :], cum[:, :, :])
                    step(dve.tensor_copy(selb[:, :, :], sel[:, :, :]), wait=False)
                    step(dve.tensor_copy(sel_all[:, bass.ds(b * TB, TB), :], sel[:, :, :]))
                    dve.tensor_tensor(sc[:, :, :], sc[:, :, :], sel[:, :, :], ALU.mult).then_inc(sem["sel"], 1)
                    dve.wait_ge(sem["sel"], 1 + b + 1)
                    step(dve.tensor_reduce(cnt[:, :], sc[:, :, :], AX_X, ALU.add))
                    step(dve.reciprocal(mx[:, :], cnt[:, :]))
                    if L == 1:
                        step(dve.tensor_scalar(mx[:, :], mx[:, :], ROUTED, None, ALU.mult))
                    step(dve.tensor_tensor(w_all[:, bass.ds(b * TB, TB), :], sc[:, :, :], bc(mx[:, :], 2, E), ALU.mult))
                    dve.wait_ge(sem["pos"], 1 + b + 1)
                    step(dve.tensor_copy(pos_all[:, bass.ds(b * TB, TB), :], pp))
                    step(dve.tensor_reduce(base[:, :], sel[:, :, :].rearrange("p t e -> p e t"), AX_X, ALU.add))
                    step(dve.tensor_tensor(acc[:, :], acc[:, :], base[:, :], ALU.add))
                    dve.tensor_copy(accb[:, :], acc[:, :]).then_inc(sem["acc"], 1)
                    assert done[1] <= R_STEPS, done
                    if done[1] < R_STEPS:
                        dve.sem_inc(sem["chain"], R_STEPS - done[1])
                done[0], done[1] = B * R_STEPS, 0
                if L == 0:
                    base1 = c["slot0"]
                else:
                    dve.wait_ge(sem["total"], 1 + 1)
                    step(dve.tensor_scalar(tf[:, :], ps_p[:, 0:E], float(P - 1), None, ALU.add))
                    step(dve.tensor_copy(ti[:, :], tf[:, :]))
                    step(dve.tensor_scalar(ti[:, :], ti[:, :], 7, None, ALU.arith_shift_right))
                    step(dve.tensor_copy(tf[:, :], ti[:, :]))
                    step(dve.memset(acc[:, :], 1.0))
                    step(dve.tensor_tensor_scan(tcum[:, :], acc[:, :], tf[:, :], 0.0, ALU.mult, ALU.add))
                    step(dve.tensor_copy(route["ends"][0:1, 1:], tcum[0:1, :]), wait=False)
                    step(dve.memset(route["ends"][0:1, 0:1], 0), wait=False)
                    step(dve.tensor_tensor(base[:, :], tcum[:, :], tf[:, :], ALU.subtract))
                    step(dve.tensor_scalar(base[:, :], base[:, :], float(P), 1.0, ALU.mult, ALU.add))
                    for a in range(2):
                        step(dve.tensor_scalar(acc[:, :], tcum[:, :], c["tile_no"][:, a:a + 1], None, ALU.is_le))
                        step(dve.tensor_reduce(te[:, a:a + 1], acc[:, :], AX_X, ALU.add))
                    step(dve.tensor_scalar(te[:, :], te[:, :], float(E - 1), None, ALU.min))
                    dve.tensor_copy(tei[:, :], te[:, :]).then_inc(sem["eid"], 1)
                    base1 = base
                first = done[1]
                F_STEPS = 24
                with dve.Fori(0, B) as b:
                    done[0], done[1] = B * R_STEPS + first + b * F_STEPS, 0

                    def product(f):
                        n = FC * b + f
                        dve.wait_ge(sem["sg"], 1 + n + 1)
                        dve.wait_ge(sem["u"], 1 + n + 1)
                        if f == 0:
                            dve.wait_ge(sem["down"], 1 + TB * b)
                        dve.tensor_tensor(h[:, f, :], ps_u[:, f % 2, :], sg[:, f % 2, :], ALU.mult)\
                           .then_inc(sem["h"], 1)

                    for f in range(2):
                        product(f)
                    bt = bass.ds(b * TB, TB)
                    step(dve.tensor_tensor(cum[:, :, :], pos_all[:, bt, :], bc(base1[:, :], 1, TB), ALU.add))
                    if L == 0:
                        step(dve.scalar_tensor_tensor(out=sel[:, :, :], in0=pos_all[:, bt, :], scalar=float(CAP),
                                                      in1=sel_all[:, bt, :], op0=ALU.is_lt, op1=ALU.mult))
                        step(dve.tensor_tensor(eq[:, :, :], w_all[:, bt, :], sel[:, :, :], ALU.mult))
                        step(dve.tensor_tensor(cum[:, :, :], cum[:, :, :], sel[:, :, :], ALU.mult))
                    else:
                        step(dve.tensor_copy(eq[:, :, :], w_all[:, bt, :]))
                        step(dve.tensor_tensor(cum[:, :, :], cum[:, :, :], sel_all[:, bt, :], ALU.mult))
                    pause()
                    for j in range(TB):
                        step(dve.max(k8[:, j, :], cum[:, j, :]), wait=j == TB - 1)
                    product(2)
                    for j in range(TB):
                        step(dve.tensor_tensor(hit[:, j, :, :], bc(cum[:, j, :], 1, K), bc(k8[:, j, 0:K], 2, E),
                                               ALU.is_equal), wait=j == TB - 1)
                    for j in range(TB):
                        step(dve.tensor_tensor(hit[:, j, :, :], hit[:, j, :, :], bc(eq[:, j, :], 1, K), ALU.mult),
                             wait=j == TB - 1)
                    step(dve.tensor_reduce(wsel[:, bt, 0:K], hit[:, :, :, :], AX_X, ALU.add))
                    ks = k8[:, :, 0:K]
                    step(dve.tensor_scalar(tk[:, :, :], ks, 1.0, float(SKIP), ALU.is_lt, ALU.mult))
                    step(dve.tensor_tensor(tk[:, :, :], tk[:, :, :], ks, ALU.add))
                    step(dve.tensor_scalar(scat[:, bt, 0:K], tk[:, :, :], -1.0, None, ALU.add), wait=False)
                    dve.tensor_scalar(gath[:, bt, 0:K], ks, -1.0, 0.0, ALU.add, ALU.max).then_inc(sem["idx"], 1)
                    assert done[1] <= F_STEPS, done
                    if done[1] < F_STEPS:
                        dve.sem_inc(sem["chain"], F_STEPS - done[1])
                    for f in range(3, FC):
                        product(f)
                    for j in range(TB):
                        dve.wait_ge(sem["down"], 1 + TB * b + j + 1)
                        xt = x[:, b * TB + j, :]
                        if L == 0:
                            dve.scalar_tensor_tensor(out=xt, in0=ps_t[:, j % 2, :], scalar=gate[:, bass.ds(b * TB + j, 1)],
                                                     in1=xt, op0=ALU.mult, op1=ALU.add).then_inc(sem["xadd"], 1)
                        else:
                            dve.tensor_tensor(xt, ps_t[:, j % 2, :], xt, ALU.add).then_inc(sem["xadd"], 1)

            @block.tensor
            def _(pe):
                pe.wait_ge(sem["wrin"], 1 + 16 * n_r)
                with pe.Fori(0, B) as b:
                    pe.wait_ge(sem["xnb"], 1 + b + 1)
                    for k in range(KH):
                        pe.wait_ge(sem["xnT0"] if k % 2 == 0 else sem["xnT1"], 1 + 2 * b + k // 2)
                        for j in range(TB):
                            i = pe.transpose(ps_t[:, k % 2, j * P:(j + 1) * P], xnb[:, j, k * P:(k + 1) * P],
                                             c["ident"][:, :])
                        i.then_inc(sem["tr"], 1)
                    pe.wait_ge(sem["xnT0"], 1 + 2 * (b + 1))
                    pe.wait_ge(sem["xnT1"], 1 + 2 * (b + 1))
                    if L == 0:
                        pe.wait_ge(sem["gate"], 1 + b)
                    pe.wait_ge(sem["score"], 1 + b)
                    for j in range(TB):
                        for k in range(KH):
                            i = pe.matmul(lg[:, j, :], xnTb[:, k, j * P:(j + 1) * P], wr[:, k, :], start=k == 0, stop=k == KH - 1)
                    i.then_inc(sem["logits"], 1)
                    pe.wait_ge(sem["sel"], 1 + b + 1)
                    pe.wait_ge(sem["acc"], 1 + b + 2)
                    for j in range(TB):
                        pe.matmul(pp[:, j, :], c["before_bf"][:, :], selb[:, j, :], start=True, stop=False)
                        for i2 in range(j):
                            pe.matmul(pp[:, j, :], c["ones_bf"][:, :], selb[:, i2, :], start=False, stop=False)
                        i = pe.matmul(pp[:, j, :], c["ones_bf"][:, :], accb[:, :], start=False, stop=True)
                    i.then_inc(sem["pos"], 1)
                if L == 1:
                    pe.wait_ge(sem["acc"], 1 + B + 2)
                    pe.matmul(ps_p[:, 0:E], c["ones_bf"][:, :], accb[:, :], start=True, stop=True).then_inc(sem["total"], 1)
                pe.wait_ge(sem["win"], 1 + 16 * n_in)
                pe.wait_ge(sem["xnT"], 1 + B)
                with pe.Fori(0, B) as b:
                    for f in range(FC):
                        n = FC * b + f
                        for src, ps, w, ready, taken in (("g", ps_g, wg, "sg", None), ("u", ps_u, wu, "h", None)):
                            pe.wait_ge(sem[ready], 1 + (n - 1 if f >= 2 else FC * b))
                            for k in range(KH):
                                i = pe.matmul(ps[:, f % 2, :], w[:, k, f * P:(f + 1) * P], xnT[:, k, bass.ds(b * S, S)],
                                              start=k == 0, stop=k == KH - 1)
                            i.then_inc(sem[src], 1)
                    pe.wait_ge(sem["h"], 1 + FC * (b + 1))
                    for j in range(TB):
                        pe.wait_ge(sem["xadd"], 1 + (TB * b + j - 1 if j >= 2 else TB * b))
                        for f in range(FC):
                            i = pe.matmul(ps_t[:, j % 2, :], h[:, f, j * P:(j + 1) * P], wd[:, f, :],
                                          start=f == 0, stop=f == FC - 1)
                        i.then_inc(sem["down"], 1)


def expert_stage0(nc, c, I, D):
    FR = F0 - 2 * P
    with ExitStack() as ctx:
        pl = Pools(nc, ctx)
        ctx.callback(pl.clear)
        wg = pl.sb("e0_wg", [P, 2, KH, F0])
        wu = pl.sb("e0_wu", [P, 2, KH, F0])
        wd = pl.sb("e0_wd", [P, 2, 3, H])
        xe = pl.sb("e0_xe", [CAP, 2, H])
        xeT = pl.sb("e0_xeT", [P, 2, KH, CAP])
        sg = pl.sb("e0_sg", [P, 2, 3, CAP])
        hT = pl.sb("e0_hT", [P, 2, 3, CAP])
        yo = pl.sb("e0_yo", [CAP, 2, H])
        ps_x = pl.ps("e0_psx", [P, 2, 512])
        ps_g = pl.ps("e0_psg", [P, 2, 512])
        ps_u = pl.ps("e0_psu", [P, 2, 512])
        ps_o = pl.ps("e0_pso", [P, 2, 512])
        sem = {n: pl.sem("e0_" + n) for n in ("in0", "in1", "free", "tr", "xeT", "g", "u", "sg", "hT", "down", "yo", "stored")}
        sem["out"] = pl.sem0("e0_out")
        fin = (sem["in0"], sem["in1"])
        last = ((0, 2, P), (2, 3, FR))

        pl.start_at_one()
        with nc.Block() as block:

            @block.sync
            def _(sp):
                with sp.Fori(0, E // 2) as i:
                    for q in range(2):
                        e = i * 2 + q
                        hold(sp, sem["free"], 1 + e + 1, c["held"])
                        sp.dma_start(xe[:, q, :], D["xs0"][bass.ds(e * CAP, CAP), :]).then_inc(fin[q], 16)
                        for w, name in ((wg, "wg0"), (wu, "wu0")):
                            sp.dma_start(w[:, q, :, :], I[name][bass.ds(e, 1), :, :]
                                         .rearrange("o (p k) f -> p (o k) f", k=KH)).then_inc(fin[q], 16)
                        sp.dma_start(wd[:, q, 0:2, :], I["wd0"][bass.ds(e, 1), 0:2 * P, :]
                                     .rearrange("o (c p) n -> p (o c) n", p=P)).then_inc(fin[q], 16)
                        sp.dma_start(wd[0:FR, q, 2, :], I["wd0"][bass.ds(e, 1), 2 * P:F0, :]
                                     .rearrange("o p n -> p (o n)")).then_inc(fin[q], 16)

            @block.gpsimd
            def _(pool):
                with pool.Fori(0, E // 2) as i:
                    for q in range(2):
                        e = i * 2 + q
                        hold(pool, sem["yo"], 1 + e + 1, c["held"])
                        pool.dma_start(D["y0"][bass.ds(e * CAP, CAP), :], yo[:, q, :]).then_inc(sem["out"], 16)
                        hold(pool, sem["out"], 16 * (e + 1), c["held"])
                        pool.sem_inc(sem["stored"], 1)

            @block.scalar
            def _(act):
                with act.Fori(0, E // 2) as i:
                    for q in range(2):
                        e = i * 2 + q
                        act.wait_ge(sem["g"], 1 + e + 1)
                        act.wait_ge(sem["down"], 1 + e)
                        for a, z, m in last:
                            j = act.activation(sg[0:m, q, a:z, :],
                                               ps_g[0:m, q, a * CAP:z * CAP].rearrange("p (c s) -> p c s", s=CAP),
                                               ACT.Silu)
                        j.then_inc(sem["sg"], 1)
                        act.wait_ge(sem["down"], 1 + e + 1)
                        act.wait_ge(sem["stored"], 1 + e)
                        act.activation(yo[:, q, :], ps_o[0:CAP, q, :], ACT.Copy).then_inc(sem["yo"], 1)

            @block.vector
            def _(dve):
                with dve.Fori(0, E // 2) as i:
                    for q in range(2):
                        e = i * 2 + q
                        dve.wait_ge(sem["tr"], 1 + e + 1)
                        dve.wait_ge(sem["free"], 1 + e + 1)
                        dve.tensor_copy(xeT[:, q, :, :], ps_x[:, q, 0:KH * CAP].rearrange("p (k s) -> p k s", s=CAP))\
                           .then_inc(sem["xeT"], 1)
                        dve.wait_ge(sem["sg"], 1 + e + 1)
                        dve.wait_ge(sem["u"], 1 + e + 1)
                        for a, z, m in last:
                            j = dve.tensor_tensor(hT[0:m, q, a:z, :],
                                                  ps_u[0:m, q, a * CAP:z * CAP].rearrange("p (c s) -> p c s", s=CAP),
                                                  sg[0:m, q, a:z, :], ALU.mult)
                        j.then_inc(sem["hT"], 1)

            @block.tensor
            def _(pe):
                pe.sem_inc(sem["free"], 2)

                def up(e, q, half):
                    pe.wait_ge(fin[q], 1 + 80 * (half + 1))
                    hold(pe, sem["xeT"], 1 + e, c["held"])
                    for k in range(KH):
                        i = pe.transpose(ps_x[:, q, k * CAP:(k + 1) * CAP], xe[:, q, k:H:KH], c["ident"][0:CAP, 0:CAP])
                    i.then_inc(sem["tr"], 1)
                    pe.wait_ge(sem["xeT"], 1 + e + 1)
                    for ps, w, name in ((ps_g, wg, "g"), (ps_u, wu, "u")):
                        for f in range(3):
                            m = P if f < 2 else FR
                            for k in range(KH):
                                i = pe.matmul(ps[0:m, q, f * CAP:(f + 1) * CAP], w[:, q, k, f * P:f * P + m],
                                              xeT[:, q, k, :], start=k == 0, stop=k == KH - 1)
                        i.then_inc(sem[name], 1)

                def down(e, q):
                    pe.wait_ge(sem["hT"], 1 + e + 1)
                    for f in range(3):
                        m = P if f < 2 else FR
                        i = pe.matmul(ps_o[0:CAP, q, :], hT[0:m, q, f, :], wd[0:m, q, f, :], start=f == 0, stop=f == 2)
                    i.then_inc(sem["down"], 1)
                    pe.wait_ge(sem["down"], 1 + e + 1)
                    pe.sem_inc(sem["free"], 1)

                with pe.Fori(0, E // 2) as i:
                    for q in range(2):
                        up(i * 2 + q, q, i)
                        pe.wait_ge(sem["yo"], 1 + i * 2 + q)
                        down(i * 2 + q, q)


def expert_stage1(nc, c, I, D, ends):
    with ExitStack() as ctx:
        pl = Pools(nc, ctx)
        ctx.callback(pl.clear)
        NW = F1 // P
        RING = 4
        assert NTILE1 % RING == 0 and E % RING == 0
        wgu = pl.sb("e1_wgu", [P, RING, KH, 2 * F1])
        wd = pl.sb("e1_wd", [P, RING, NW, H])
        xs = pl.sb("e1_xs", [P, RING, H])
        xsT = pl.sb("e1_xsT", [P, 2, KH, P])
        sg = pl.sb("e1_sg", [P, 2, F1])
        h = pl.sb("e1_h", [P, 2, F1])
        hT = pl.sb("e1_hT", [P, 2, NW, P])
        yo = pl.sb("e1_yo", [P, RING, H])
        ids = pl.sb("e1_ids", [1, NTILE1], I32)
        ps_x = pl.ps("e1_psx", [P, 2, 512])
        ps_g = pl.ps("e1_psg", [P, 2, 512])
        ps_h = pl.ps("e1_psh", [P, 2, 512])
        ps_o = pl.ps("e1_pso", [P, 2, 512])
        sem = {n: pl.sem("e1_" + n) for n in ("ids", "w0", "w1", "w2", "w3", "ready", "tr", "xsT", "gu", "sg", "h",
                                              "htr", "hT", "down", "yo", "stored")}
        landed = [sem[f"w{s}"] for s in range(RING)]
        rows_in = [pl.sem0(f"e1_rows{q}") for q in range(RING)]
        sem["out"] = pl.sem0("e1_out")
        ROUNDS = NTILE1 // RING

        pl.start_at_one()
        with nc.Block() as block:

            @block.sync
            def _(sp):
                sp.dma_start(ids[0:1, :], D["expert"][0:NTILE1, :].rearrange("n o -> o n")).then_inc(sem["ids"], 16)

                def fetch(e, s):
                    for a, name in ((0, "wg1"), (1, "wu1")):
                        sp.dma_start(wgu[:, s, :, a * F1:(a + 1) * F1], I[name][bass.ds(e, 1), :, :]
                                     .rearrange("o (p k) f -> p (o k) f", k=KH)).then_inc(landed[s], 16)
                    sp.dma_start(wd[:, s, :, :], I["wd1"][bass.ds(e, 1), :, :]
                                 .rearrange("o (p c) n -> p (o c) n", c=NW)).then_inc(landed[s], 16)

                def announce(s, turn):
                    hold(sp, landed[s], 1 + 48 * (turn + 1), c["held"])
                    sp.sem_inc(sem["ready"], 1)

                def refill(e, q):
                    last = sp.value_load(ends[0:1, bass.ds(e, 1)], min_val=0, max_val=NTILE1)
                    hold(sp, sem["down"], 1 + last, c["held"])
                    fetch(e + RING - 1, (q + RING - 1) % RING)

                for e in range(RING - 1):
                    fetch(e, e)
                with sp.Fori(0, E // RING - 1) as i:
                    for q in range(RING):
                        announce(q, i)
                        refill(i * RING + q, q)
                for q in range(RING):
                    announce(q, E // RING - 1)
                    if q == 0:
                        refill(E - RING, 0)

            @block.gpsimd
            def _(pool):
                def load(t, q):
                    pool.dma_start(xs[:, q, :], D["xs1"][bass.ds(t * P, P), :]).then_inc(rows_in[q], 16)

                def store(t, q):
                    hold(pool, sem["yo"], 1 + t + 1, c["held"])
                    pool.dma_start(D["y1"][bass.ds(t * P, P), :], yo[:, q, :]).then_inc(sem["out"], 16)

                def tell(t):
                    hold(pool, sem["out"], 16 * (t + 1), c["held"])
                    pool.sem_inc(sem["stored"], 1)

                for q in range(RING):
                    load(q, q)
                with pool.Fori(0, ROUNDS - 1) as i:
                    for q in range(RING):
                        t = i * RING + q
                        hold(pool, sem["tr"], 1 + t + 1, c["held"])
                        load(t + RING, q)
                        store(t, q)
                        tell(t)
                for q in range(RING):
                    t = NTILE1 - RING + q
                    store(t, q)
                    tell(t)

            @block.scalar
            def _(act):
                def gate(t, q):
                    act.wait_ge(sem["gu"], 1 + t + 1)
                    act.wait_ge(sem["h"], 1 + t)
                    act.activation(sg[:, q % 2, :], ps_g[:, q % 2, 0:F1], ACT.Silu).then_inc(sem["sg"], 1)

                def empty(t, q, first=False):
                    act.wait_ge(sem["down"], 1 + t + 1)
                    if not first:
                        act.wait_ge(sem["stored"], 1 + t - RING + 1)
                    act.activation(yo[:, q % RING, :], ps_o[:, q % 2, :], ACT.Copy).then_inc(sem["yo"], 1)

                for t in range(RING):
                    gate(t, t)
                    if t > 0:
                        empty(t - 1, t - 1, first=True)
                gate(RING, 0)
                empty(RING - 1, RING - 1, first=True)
                for q in range(1, RING):
                    gate(RING + q, q)
                    empty(RING + q - 1, q - 1)
                with act.Fori(2, ROUNDS) as i:
                    for q in range(RING):
                        gate(i * RING + q, q)
                        empty(i * RING + q - 1, q + RING - 1)
                empty(NTILE1 - 1, RING - 1)

            @block.vector
            def _(dve):
                def turned_rows(t, q):
                    dve.wait_ge(sem["tr"], 1 + t + 1)
                    dve.wait_ge(sem["gu"], 1 + t - 1)
                    dve.tensor_copy(xsT[:, q % 2, :, :], ps_x[:, q % 2, :].rearrange("p (k s) -> p k s", s=P))\
                       .then_inc(sem["xsT"], 1)

                def turned_hidden(t, q):
                    dve.wait_ge(sem["htr"], 1 + t + 1)
                    dve.tensor_copy(hT[:, q % 2, :, :], ps_h[:, q % 2, 0:NW * P].rearrange("p (c s) -> p c s", s=P))\
                       .then_inc(sem["hT"], 1)

                def product(t, q):
                    dve.wait_ge(sem["sg"], 1 + t + 1)
                    dve.tensor_tensor(h[:, q % 2, :], ps_g[:, q % 2, F1:], sg[:, q % 2, :], ALU.mult).then_inc(sem["h"], 1)

                def a_round(i, first=False, last=False):
                    for q in range(RING):
                        t = i * RING + q
                        if not (last and q == RING - 1):
                            turned_rows(t + 1, q + 1)
                        if not (first and q == 0):
                            turned_hidden(t - 1, q + RING - 1)
                        product(t, q)

                dve.wait_ge(sem["tr"], 1 + 1)
                dve.tensor_copy(xsT[:, 0, :, :], ps_x[:, 0, :].rearrange("p (k s) -> p k s", s=P)).then_inc(sem["xsT"], 1)
                a_round(0, first=True)
                with dve.Fori(1, ROUNDS - 1) as i:
                    a_round(i)
                a_round(ROUNDS - 1, last=True)
                turned_hidden(NTILE1 - 1, RING - 1)

            @block.tensor
            def _(pe):
                def turn_rows(q, landed_count):
                    pe.wait_ge(rows_in[q % RING], landed_count)
                    for k in range(KH):
                        j = pe.transpose(ps_x[:, q % 2, k * P:(k + 1) * P], xs[:, q % RING, k:H:KH], c["ident"][:, :])
                    j.then_inc(sem["tr"], 1)

                def up(t, q):
                    e = pe.value_load(ids[0:1, bass.ds(t, 1)], min_val=0, max_val=E - 1)
                    hold(pe, sem["ready"], 1 + e + 1, c["held"])
                    pe.wait_ge(sem["xsT"], 1 + t + 1)
                    for k in range(KH):
                        j = pe.matmul(ps_g[:, q % 2, :], xsT[:, q % 2, k, :], wgu[:, bass.ds(e % RING, 1), k, :],
                                      start=k == 0, stop=k == KH - 1)
                    j.then_inc(sem["gu"], 1)

                def turn_hidden(t, q):
                    pe.wait_ge(sem["h"], 1 + t + 1)
                    for a in range(NW):
                        j = pe.transpose(ps_h[:, q % 2, a * P:(a + 1) * P], h[:, q % 2, a:F1:NW], c["ident"][:, :])
                    j.then_inc(sem["htr"], 1)

                def down(t, q, first=False):
                    e = pe.value_load(ids[0:1, bass.ds(t, 1)], min_val=0, max_val=E - 1)
                    pe.wait_ge(sem["hT"], 1 + t + 1)
                    if not first:
                        pe.wait_ge(sem["yo"], 1 + t - 1)
                    for a in range(NW):
                        j = pe.matmul(ps_o[:, q % 2, :], hT[:, q % 2, a, :], wd[:, bass.ds(e % RING, 1), a, :],
                                      start=a == 0, stop=a == NW - 1)
                    j.then_inc(sem["down"], 1)

                def a_round(i, first=False, last=False):
                    for q in range(RING):
                        t = i * RING + q
                        if not (last and q == RING - 1):
                            pe.wait_ge(sem["xsT"], 1 + t)
                            turn_rows(q + 1, 16 * (i + 1 + (q + 1) // RING))
                        if not (first and q == 0):
                            turn_hidden(t - 1, q + RING - 1)
                        up(t, q)
                        if not (first and q == 0):
                            down(t - 1, q + RING - 1, first and q == 1)

                pe.wait_ge(sem["ids"], 1 + 16)
                turn_rows(0, 16)
                a_round(0, first=True)
                with pe.Fori(1, ROUNDS - 1) as i:
                    a_round(i)
                a_round(ROUNDS - 1, last=True)
                turn_hidden(NTILE1 - 1, RING - 1)
                down(NTILE1 - 1, RING - 1)


def combine_stage(nc, c, I, D, x, L, route):
    K = K0 if L == 0 else K1
    NB = 8
    y = D["y0"] if L == 0 else D["y1"]
    per = NB // K
    with ExitStack() as ctx:
        pl = Pools(nc, ctx)
        ctx.callback(pl.clear)
        rows = pl.sb(f"c{L}_rows", [P, NB, H])
        got = [pl.sem0(f"c{L}_got{i}") for i in range(NB)]
        used = pl.sem(f"c{L}_used")
        pl.start_at_one()
        with nc.Block() as block:

            @block.gpsimd
            def _(pool):
                for t in range(NT):
                    for k in range(K):
                        n = t * K + k
                        if n >= NB:
                            pool.wait_ge(used, 1 + n - NB + 1)
                        pool.indirect_dma_start(rows[:, n % NB, :], None, y[:, :],
                                                bass.IndirectOffsetOnAxis(route["gath"][:, t, k:k + 1], 0))\
                            .then_inc(got[n % NB], 16)

            @block.vector
            def _(dve):
                with dve.Fori(0, NT // per) as r:
                    for n in range(NB):
                        t, k = n // K, n % K
                        dve.wait_ge(got[n], 16 * (r + 1))
                        dve.wait_ge(used, 1 + r * NB + n)
                        xt = x[:, r * per + t, :]
                        dve.scalar_tensor_tensor(out=xt, in0=rows[:, n, :],
                                                 scalar=route["wsel"][:, bass.ds(r * per + t, 1), k],
                                                 in1=xt, op0=ALU.mult, op1=ALU.add).then_inc(used, 1)


def attention_stage(nc, c, I, D, x):
    ND = HG * DCA
    NI = 2 * TB + 1
    KI, DI, QI = 0, TB, TB + 1
    NG_STEPS = TB * HG
    N = NG * NG_STEPS
    SB, PB = 4, 4
    BT, BO = 4, 6
    LAG = 3
    T_KT, T_DKT, T_V, T_DV, T_QT = NI, NI + NG, NI + NG + 1, NI + NG + 1 + TB, NI + NG + 2 + TB
    TAKEN = T_QT + NG
    with ExitStack() as ctx:
        pl = Pools(nc, ctx)
        ctx.callback(pl.clear)
        sb = lambda n, shape, dt=F32: pl.sb("a_" + n, shape, dt)
        wq = sb("wq", [P, KH, H])
        wkv = sb("wkv", [P, KC, 2, H])
        wkvd = sb("wkvd", [P, KC, 2, H])
        wo = sb("wo", [P, KH, H])
        bq = sb("bq", [P, H])
        bkv = sb("bkv", [P, 2, H])
        bkvd = sb("bkvd", [P, 2, H])
        bo = sb("bo", [P, H])
        hw = sb("hw", [P, 6])
        xnb = sb("xnb", [P, TB, H])
        xnT = sb("xnT", [P, KH, S])
        ctxT = sb("ctxT", [P, KC, S])
        ctxd = sb("ctxd", [P, KC, P // DCA, DCA])
        mask_r = sb("mask_r", [ND, HG, HD])
        mask_c = sb("mask_c", [P, HG, DCA])
        st = sb("st", [P, NT, 6])
        mv = sb("mv", [P, NT, 2])
        ve = sb("ve", [P, NT])
        rs = sb("rs", [P, NT])
        hd = sb("hd", [P, NI, NH, HD])
        hsq = sb("hsq", [P, 2, NH, HD])
        mu = sb("mu", [P, NI, NH])
        hv = sb("hv", [P, NI, NH])
        v = sb("v", [P, TB, H])
        dv = sb("dv", [ND, NG, HG, HD])
        qT = sb("qT", [P, NG, S])
        kT = sb("kT", [P, NG, S])
        kd = sb("kd", [P, NG, HG, DCA])
        sd = sb("sd", [P, TB, NG, ND])
        md = sb("md", [P, TB * NH])
        pdT = sb("pdT", [ND, NG, S])
        p = sb("p", [P, PB, S])
        pt = sb("pt", [P, 2, TB, P])
        nm = sb("nm", [P, N])
        sm = sb("sm", [P, N])
        rm = sb("rm", [P, N])
        oT = sb("oT", [P, NG, S])
        ps = pl.ps("a_ps", [P, 8, 512])
        sem = {n: pl.sem("a_" + n) for n in (
            "win", "ctx", "ctxd", "const", "stats", "ve", "rs", "xnb", "xtr", "xnT", "item", "chain", "cent", "sq",
            "var", "sqrt", "hn", "val", "ktr", "qtr", "taken", "sd", "sdc", "pdexp", "pd", "pdT", "pdTc",
            "s", "max", "exp", "inv", "prob", "ptr", "pt", "pv", "oT", "bias", "om", "xadd")}
        n_in = 8 + HG
        f3 = "p a b -> p (a b)"

        pl.start_at_one()
        with nc.Block() as block:

            @block.sync
            def _(sp):
                sp.dma_start(wq[:, :, :], I["wq"].rearrange("(k p) n -> p k n", p=P)).then_inc(sem["win"], 16)
                sp.dma_start(wo[:, :, :], I["wo"].rearrange("(k p) n -> p k n", p=P)).then_inc(sem["win"], 16)
                for dst, name in ((wkv, "wkv"), (wkvd, "wkvd")):
                    sp.dma_start(dst[:, :, :, :].rearrange("p k z n -> p k (z n)"),
                                 I[name].rearrange("(k p) n -> p k n", p=P)).then_inc(sem["win"], 16)
                for dst, name in ((bq[:, :], "bq"), (bkv[:, :, :].rearrange(f3), "bkv"),
                                  (bkvd[:, :, :].rearrange(f3), "bkvd"), (bo[:, :], "bo")):
                    sp.dma_start(dst, I[name].to_broadcast([P, I[name].shape[1]])).then_inc(sem["win"], 16)
                for i in range(HG):
                    sp.dma_start(hw[i * HD:(i + 1) * HD, :], I["headnorm"]).then_inc(sem["win"], 16)
                with sp.Fori(0, B) as b:
                    hold(sp, sem["val"], 1 + (TB + 1) * b, c["held"])
                    sp.dma_start(ctxT[:, :, :], I["ctxT"][:, bass.ds(b * S, S)].rearrange("(k p) n -> p k n", p=P))\
                      .then_inc(sem["ctx"], 16)

            @block.gpsimd
            def _(pool):
                pool.memset(mask_r[:, :, :], 1.0).then_inc(sem["const"], 1)
                pool.memset(mask_c[:, :, :], 1.0).then_inc(sem["const"], 1)
                pool.memset(p[:, :, :], 0.0).then_inc(sem["const"], 1)
                pool.wait_ge(sem["const"], 1 + 3)
                n = 3
                for m, width, rows in ((mask_r, HD, DCA), (mask_c, DCA, HD)):
                    pool.affine_select(out=m[:, :, :], in_=m[:, :, :], compare_op=ALU.is_ge, fill=0.0, base=0,
                                       pattern=[[-rows, HG], [0, width]], channel_multiplier=1).then_inc(sem["const"], 1)
                    n += 1
                    pool.wait_ge(sem["const"], 1 + n)
                    pool.affine_select(out=m[:, :, :], in_=m[:, :, :], compare_op=ALU.is_ge, fill=0.0, base=rows - 1,
                                       pattern=[[rows, HG], [0, width]], channel_multiplier=-1).then_inc(sem["const"], 1)
                    n += 1
                pool.wait_ge(sem["ve"], 1 + 1)
                pool.tensor_tensor(rs[:, :], ve[:, :], c["minus_half"][:, 0:NT], ALU.pow).then_inc(sem["rs"], 1)
                with pool.Fori(0, B) as b:
                    pool.wait_ge(sem["ctx"], 1 + 16 * (b + 1))
                    pool.sem_inc(c["held"], 1)
                    for i in range(P // DCA):
                        j = pool.tensor_copy(ctxd[:, :, i, :], ctxT[:, :, S2:])
                    j.then_inc(sem["ctxd"], 1)
                    pool.wait_ge(sem["xnb"], 1 + b + 1)
                    xb = x[:, bass.ds(b * TB, TB), :]
                    pool.tensor_tensor(xb, xb, bc(bo[:, :], 1, TB), ALU.add).then_inc(sem["bias"], 1)

            @block.scalar
            def _(act):
                act.wait_ge(sem["const"], 1 + 7)
                with act.Fori(0, B) as b:

                    def turn_x():
                        for k in range(KH):
                            act.wait_ge(sem["xtr"], 1 + KH * b + k + 1)
                            act.wait_ge(sem["om"], 1 + TB * b)
                            act.activation(xnT[:, k, :], ps[:, 5 + k % 3, :], ACT.Copy).then_inc(sem["xnT"], 1)

                    for i in range(NI + 1):
                        if i < NI:
                            act.wait_ge(sem["cent"], 1 + NI * b + i + 1)
                            act.activation(hsq[:, i % 2, :, :], hd[:, i, :, :], ACT.Square).then_inc(sem["sq"], 1)
                        if i >= 1:
                            act.wait_ge(sem["var"], 1 + NI * b + i)
                            act.activation(hv[:, i - 1, :], hv[:, i - 1, :], ACT.Sqrt).then_inc(sem["sqrt"], 1)
                        if i == 1:
                            turn_x()
                    act.wait_ge(sem["sdc"], 1 + b + 1)
                    act.activation(sd[:, :, :, :], sd[:, :, :, :], ACT.Exp).then_inc(sem["pdexp"], 1)

                    def exponentials(n):
                        act.wait_ge(sem["max"], 1 + N * b + n + 1)
                        act.activation(p[:, n % PB, 0:S2], ps[:, n % SB, 0:S2], ACT.Exp, bias=nm[:, n:n + 1],
                                       accum_out=sm[:, n:n + 1]).then_inc(sem["exp"], 1)

                    def turned(n):
                        act.wait_ge(sem["ptr"], 1 + N * b + n + 1)
                        if n >= 2:
                            act.wait_ge(sem["pv"], 1 + N * b + n - 1)
                        act.activation(pt[:, n % 2, :, :], ps[:, BT + n % 2, :].rearrange("p (j s) -> p j s", s=P),
                                       ACT.Copy).then_inc(sem["pt"], 1)

                    exponentials(0)
                    for g in range(NG):
                        act.wait_ge(sem["pdT"], 1 + NG * b + g + 1)
                        act.activation(pdT[:, g, :], ps[0:ND, BT + g % 2, :], ACT.Copy).then_inc(sem["pdTc"], 1)
                    for n in range(1, N + LAG):
                        if n >= LAG:
                            turned(n - LAG)
                        if n < N:
                            exponentials(n)

            @block.vector
            def _(dve):
                done = [0, 0]

                def step(ins, wait=True):
                    ins.then_inc(sem["chain"], 1)
                    done[1] += 1
                    if wait:
                        dve.wait_ge(sem["chain"], 1 + done[0] + done[1])

                dve.wait_ge(sem["win"], 1 + 16 * n_in)
                dve.tensor_scalar(hw[:, 0:2], hw[:, 0:2], SCALE, None, ALU.mult).then_inc(sem["hn"], 1)
                dve.wait_ge(sem["hn"], 1 + 1)
                for j in range(NT):
                    dve.bn_stats(st[:, j, :], x[:, j, :]).then_inc(sem["stats"], 1)
                dve.wait_ge(sem["stats"], 1 + NT)
                for j in range(NT):
                    dve.bn_aggr(mv[:, j, :], st[:, j, :]).then_inc(sem["stats"], 1)
                dve.wait_ge(sem["stats"], 1 + 2 * NT)
                dve.tensor_scalar(ve[:, :], mv[:, :, 1], LN_EPS, None, ALU.add).then_inc(sem["ve"], 1)
                dve.wait_ge(sem["rs"], 1 + 1)
                CHAIN = 64
                with dve.Fori(0, B) as b:
                    done[0], done[1] = b * CHAIN, 0
                    for j in range(TB):
                        t = b * TB + j
                        i = dve.tensor_scalar(xnb[:, j, :], x[:, t, :], mv[:, bass.ds(t, 1), 0], rs[:, bass.ds(t, 1)],
                                              ALU.subtract, ALU.mult)
                    i.then_inc(sem["xnb"], 1)

                    bank = [0, 1, 2, 3, 4, 0, 1, 2, 3]
                    biases = [bkv[:, 0, :]] * TB + [bkvd[:, 0, :]] + [bq[:, :]] * TB

                    def centre(i):
                        dve.wait_ge(sem["item"], 1 + NI * b + i + 1)
                        dve.tensor_tensor(hd[:, i, :, :].rearrange(f3), ps[:, bank[i], :], biases[i], ALU.add)\
                           .then_inc(sem["taken"], 1)
                        dve.wait_ge(sem["taken"], 1 + TAKEN * b + i + 1)
                        step(dve.tensor_reduce(mu[:, i, :], hd[:, i, :, :], AX_X, ALU.add))
                        step(dve.tensor_scalar(mu[:, i, :], mu[:, i, :], 1.0 / HD, None, ALU.mult))
                        dve.tensor_tensor(hd[:, i, :, :], hd[:, i, :, :], bc(mu[:, i, :], 2, HD), ALU.subtract)\
                           .then_inc(sem["cent"], 1)

                    def variance(i):
                        dve.wait_ge(sem["sq"], 1 + NI * b + i + 1)
                        step(dve.tensor_reduce(hv[:, i, :], hsq[:, i % 2, :, :], AX_X, ALU.add))
                        dve.tensor_scalar(hv[:, i, :], hv[:, i, :], 1.0 / HD, HEAD_EPS, ALU.mult, ALU.add)\
                           .then_inc(sem["var"], 1)

                    def scale(i):
                        dve.wait_ge(sem["sqrt"], 1 + NI * b + i + 1)
                        step(dve.reciprocal(mu[:, i, :], hv[:, i, :]))
                        dve.tensor_tensor(hd[:, i, :, :], hd[:, i, :, :], bc(mu[:, i, :], 2, HD), ALU.mult)\
                           .then_inc(sem["hn"], 1)

                    for i in range(NI + 2):
                        if i < NI:
                            centre(i)
                        if 1 <= i < NI + 1:
                            variance(i - 1)
                        if i >= 2:
                            scale(i - 2)
                    for g in range(NG):
                        dve.wait_ge(sem["ktr"], 1 + (NG + 1) * b + g + 1)
                        dve.tensor_scalar(kT[:, g, 0:S2], ps[:, g, 0:S2], hw[:, 2:3], hw[:, 3:4], ALU.mult, ALU.add)\
                           .then_inc(sem["taken"], 1)
                    dve.wait_ge(sem["ktr"], 1 + (NG + 1) * (b + 1))
                    step(dve.tensor_scalar(kd[:, :, :, :].rearrange("p g h s -> p (g h s)"), ps[:, 4, 0:NG * ND],
                                           hw[:, 4:5], hw[:, 5:6], ALU.mult, ALU.add))
                    dve.tensor_tensor(kd[:, :, :, :], kd[:, :, :, :], bc(mask_c[:, :, :], 1, NG), ALU.mult)\
                       .then_inc(sem["taken"], 1)
                    for j in range(TB):
                        dve.wait_ge(sem["val"], 1 + (TB + 1) * b + j + 1)
                        dve.tensor_tensor(v[:, j, :], ps[:, (5, 6, 7, 0)[j], :], bkv[:, 1, :], ALU.add)\
                           .then_inc(sem["taken"], 1)
                    dve.wait_ge(sem["val"], 1 + (TB + 1) * (b + 1))
                    step(dve.tensor_tensor(dv[:, :, :, :].rearrange("p g h d -> p (g h d)"), ps[0:ND, 1, :],
                                           bkvd[0:ND, 1, :], ALU.add))
                    dve.tensor_tensor(dv[:, :, :, :], dv[:, :, :, :], bc(mask_r[:, :, :], 1, NG), ALU.mult)\
                       .then_inc(sem["taken"], 1)
                    for g in range(NG):
                        dve.wait_ge(sem["qtr"], 1 + NG * b + g + 1)
                        dve.tensor_scalar(qT[:, g, :], ps[:, 2 + g, :], hw[:, 0:1], hw[:, 1:2], ALU.mult, ALU.add)\
                           .then_inc(sem["taken"], 1)
                    sdf = sd[:, :, :, :].rearrange("p j g (h s) -> p (j g h) s", s=DCA)
                    sdp = ps[:, BO:BO + 2, :].rearrange("p a (r s) -> p (a r) s", s=DCA)
                    dve.wait_ge(sem["sd"], 1 + b + 1)
                    step(dve.tensor_reduce(md[:, :], sdp, AX_X, ALU.max))
                    dve.tensor_tensor(sdf, sdp, bc(md[:, :], 2, DCA), ALU.subtract).then_inc(sem["sdc"], 1)

                    def maximum(n):
                        dve.wait_ge(sem["s"], 1 + N * b + n + 1)
                        dve.tensor_reduce(nm[:, n:n + 1], ps[:, n % SB, 0:S2], AX_X, ALU.max, negate=True)\
                           .then_inc(sem["max"], 1)

                    def invert(n):
                        dve.wait_ge(sem["exp"], 1 + N * b + n + 1)
                        dve.reciprocal(rm[:, n:n + 1], sm[:, n:n + 1]).then_inc(sem["inv"], 1)

                    def normalise(n):
                        dve.wait_ge(sem["inv"], 1 + N * b + n + 1)
                        dve.tensor_scalar(p[:, n % PB, 0:S2], p[:, n % PB, 0:S2], rm[:, n:n + 1], None, ALU.mult)\
                           .then_inc(sem["prob"], 1)

                    maximum(0)
                    dve.wait_ge(sem["pdexp"], 1 + b + 1)
                    step(dve.tensor_reduce(md[:, :], sdf, AX_X, ALU.add))
                    step(dve.reciprocal(md[:, :], md[:, :]))
                    dve.tensor_tensor(sdf, sdf, bc(md[:, :], 2, DCA), ALU.mult).then_inc(sem["pd"], 1)
                    for n in range(1, N + LAG + 2):
                        if n <= N:
                            invert(n - 1)
                        if n < N:
                            maximum(n)
                        if n <= N:
                            normalise(n - 1)
                        if n > LAG + 1 and (n - LAG - 1) % NG_STEPS == 0:
                            g = (n - LAG - 1) // NG_STEPS - 1
                            dve.wait_ge(sem["pv"], 1 + N * b + (g + 1) * NG_STEPS)
                            dve.tensor_copy(oT[:, g, :], ps[:, BO + g % 2, :]).then_inc(sem["oT"], 1)
                    assert done[1] <= CHAIN
                    dve.sem_inc(sem["chain"], CHAIN - done[1])
                    dve.wait_ge(sem["bias"], 1 + b + 1)
                    for j in range(TB):
                        dve.wait_ge(sem["om"], 1 + TB * b + j + 1)
                        xt = x[:, b * TB + j, :]
                        dve.tensor_tensor(xt, ps[:, 4 + j, :], xt, ALU.add).then_inc(sem["xadd"], 1)

            @block.tensor
            def _(pe):
                pe.wait_ge(sem["win"], 1 + 16 * n_in)
                ident = c["ident"]
                with pe.Fori(0, B) as b:

                    def taken(n):
                        pe.wait_ge(sem["taken"], 1 + TAKEN * b + n + 1)

                    def project(bank, src, w, signal):
                        for k in range(len(w)):
                            i = pe.matmul(ps[:, bank, :], src[k], w[k], start=k == 0, stop=k == len(w) - 1)
                        i.then_inc(sem[signal], 1)

                    pe.wait_ge(sem["ctx"], 1 + 16 * (b + 1))
                    pe.wait_ge(sem["exp"], 1 + N * b)
                    tok = lambda j: [ctxT[:, k, j * P:(j + 1) * P] for k in range(KC)]
                    dtok = [ctxd[:, k, :, :].rearrange("p h s -> p (h s)") for k in range(KC)]
                    for j in range(TB):
                        project(j, tok(j), [wkv[:, k, 0, :] for k in range(KC)], "item")
                    pe.wait_ge(sem["ctxd"], 1 + b + 1)
                    pe.wait_ge(sem["xadd"], 1 + TB * b)
                    project(4, dtok, [wkvd[:, k, 0, :] for k in range(KC)], "item")
                    pe.wait_ge(sem["xnb"], 1 + b + 1)
                    for k in range(KH):
                        if k == 3:
                            pe.wait_ge(sem["xnT"], 1 + KH * b + 1)
                        for j in range(TB):
                            i = pe.transpose(ps[:, 5 + k % 3, j * P:(j + 1) * P], xnb[:, j, k * P:(k + 1) * P], ident[:, :])
                        i.then_inc(sem["xtr"], 1)
                    pe.wait_ge(sem["xnT"], 1 + KH * (b + 1))
                    for j in range(TB):
                        taken(j)
                        project(j, [xnT[:, k, j * P:(j + 1) * P] for k in range(KH)], [wq[:, k, :] for k in range(KH)], "item")
                    pe.wait_ge(sem["hn"], 1 + NI * b + 1 + DI)
                    for g in range(NG):
                        taken(QI + g)
                        for j in range(TB):
                            i = pe.transpose(ps[:, g, j * P:(j + 1) * P],
                                             hd[:, KI + j, g * HG:(g + 1) * HG, :].rearrange(f3), ident[:, :])
                        i.then_inc(sem["ktr"], 1)
                    hold(pe, sem["hn"], 1 + NI * b + 1 + QI, c["held"])
                    for g in range(NG):
                        i = pe.transpose(ps[:, 4, g * ND:(g + 1) * ND],
                                         hd[0:ND, DI, g * HG:(g + 1) * HG, :].rearrange(f3), ident[0:ND, 0:ND])
                    i.then_inc(sem["ktr"], 1)
                    for j in range(TB):
                        if j == 3:
                            taken(T_KT)
                        project((5, 6, 7, 0)[j], tok(j), [wkv[:, k, 1, :] for k in range(KC)], "val")
                    taken(T_KT + 1)
                    project(1, dtok, [wkvd[:, k, 1, :] for k in range(KC)], "val")
                    pe.wait_ge(sem["hn"], 1 + NI * b + 1 + NI)
                    for g in range(NG):
                        taken((T_KT + 2, T_KT + 3, T_DKT, T_V)[g])
                        for j in range(TB):
                            i = pe.transpose(ps[:, 2 + g, j * P:(j + 1) * P],
                                             hd[:, QI + j, g * HG:(g + 1) * HG, :].rearrange(f3), ident[:, :])
                        i.then_inc(sem["qtr"], 1)
                    taken(T_QT + 3)
                    for j in range(TB):
                        for g in range(NG):
                            a = (j % 2 * NG + g) * ND
                            i = pe.matmul(ps[:, BO + j // 2, a:a + ND], qT[:, g, j * P:(j + 1) * P],
                                          kd[:, g, :, :].rearrange("p h s -> p (h s)"), start=True, stop=True)
                    i.then_inc(sem["sd"], 1)

                    def where(n):
                        return n // NG_STEPS, n // HG % TB, n % HG

                    def scores(n):
                        g, j, hh = where(n)
                        if n >= SB:
                            pe.wait_ge(sem["exp"], 1 + N * b + n - SB + 1)
                        strip = slice(hh * HD, (hh + 1) * HD)
                        pe.matmul(ps[:, n % SB, 0:S2], qT[strip, g, j * P:(j + 1) * P], kT[strip, g, 0:S2],
                                  start=True, stop=True).then_inc(sem["s"], 1)

                    def turn(n):
                        pe.wait_ge(sem["prob"], 1 + N * b + n + 1)
                        if n >= 2:
                            pe.wait_ge(sem["pt"], 1 + N * b + n - 1)
                        for a in range(TB):
                            i = pe.transpose(ps[:, BT + n % 2, a * P:(a + 1) * P], p[:, n % PB, a * P:(a + 1) * P], ident[:, :])
                        i.then_inc(sem["ptr"], 1)

                    def dca(g):
                        if g >= 2:
                            pe.wait_ge(sem["oT"], 1 + NG * b + g - 1)
                        pe.matmul(ps[:, BO + g % 2, :], dv[:, g, :, :].rearrange(f3), pdT[:, g, :],
                                  start=True, stop=False, skip_group_check=True)

                    def weigh(n):
                        g, j, hh = where(n)
                        if n % NG_STEPS == 0:
                            dca(g)
                        pe.wait_ge(sem["pt"], 1 + N * b + n + 1)
                        for a in range(TB):
                            col = (g * HG + hh) * HD
                            i = pe.matmul(ps[hh * HD:(hh + 1) * HD, BO + g % 2, j * P:(j + 1) * P], v[:, a, col:col + HD],
                                          pt[:, n % 2, a, :], start=False, stop=a == TB - 1, skip_group_check=True,
                                          tile_position=(0, hh * HD))
                        i.then_inc(sem["pv"], 1)

                    for n in range(LAG):
                        scores(n)
                    for g in range(NG):
                        if g >= 2:
                            hold(pe, sem["pdTc"], 1 + NG * b + g - 1, c["held"])
                        else:
                            hold(pe, sem["pd"], 1 + b + 1, c["held"])
                        for j in range(TB):
                            i = pe.transpose(ps[0:ND, BT + g % 2, j * P:(j + 1) * P], sd[:, j, g, :], ident[:, :])
                        i.then_inc(sem["pdT"], 1)
                    pe.wait_ge(sem["pdTc"], 1 + NG * (b + 1))
                    for n in range(LAG, N + LAG + 1):
                        if n < N:
                            scores(n)
                        if n - LAG < N:
                            turn(n - LAG)
                        if n > LAG:
                            weigh(n - LAG - 1)
                    pe.wait_ge(sem["pt"], 1 + N * (b + 1))
                    for j in range(TB):
                        if j == 0:
                            pe.wait_ge(sem["oT"], 1 + NG * (b + 1))
                        project(4 + j, [oT[:, g, j * P:(j + 1) * P] for g in range(NG)], [wo[:, g, :] for g in range(NG)], "om")


def program(nc, I, out, upto=9):
    with ExitStack() as ctx:
        pl = Pools(nc, ctx)
        D = {"bc": nc.dram_tensor("bc_rows", (B * 2 * NST, S), F32).ap(),
             "xs0": nc.dram_tensor("slots_in0", (NSLOT0, H), F32).ap(),
             "xs1": nc.dram_tensor("slots_in1", (NSLOT1, H), F32).ap(),
             "y0": nc.dram_tensor("slots_out0", (NSLOT0, H), F32).ap(),
             "y1": nc.dram_tensor("slots_out1", (NSLOT1, H), F32).ap(),
             "expert": nc.dram_tensor("tile_expert", (2 * P, 1), I32).ap()}
        c = {}
        x = pl.sb("x_resid", [P, NT, H])
        constants(nc, pl, c)
        mamba_stage(nc, pl, c, I, D, x)
        def routes(L, K):
            return {"scat": pl.sb(f"scat{L}", [P, NT, K], I32), "gath": pl.sb(f"gath{L}", [P, NT, K], I32),
                    "wsel": pl.sb(f"wsel{L}", [P, NT, K])}

        if upto >= 2:
            route0 = routes(0, K0)
            route_stage(nc, c, I, D, x, 0, route0)
        if upto >= 3:
            expert_stage0(nc, c, I, D)
            combine_stage(nc, c, I, D, x, 0, route0)
        if upto >= 4:
            attention_stage(nc, c, I, D, x)
        if upto >= 5:
            route1 = routes(1, K1)
            route1["ends"] = pl.sb("ends", [1, 1 + E], I32)
            route_stage(nc, c, I, D, x, 1, route1)
        if upto >= 6:
            expert_stage1(nc, c, I, D, route1["ends"])
            combine_stage(nc, c, I, D, x, 1, route1)
        stored = pl.sem("stored")
        with nc.Block() as block:

            @block.sync
            def _(sp):
                sp.dma_start(out.rearrange("(t p) h -> p t h", p=P), x[:, :, :]).then_inc(stored, 16)
                sp.wait_ge(stored, 16)


def layouts(a):
    f = np.ascontiguousarray
    col = lambda v: f(v.reshape(TB, P).T)
    i = {"x": f(a["x"].reshape(T, H)), "ctxT": f(a["ctx_1024"].reshape(T, DM).T),
         "in_projT": f(a["L0_xattn_in_proj_w"].T), "x_projT": f(a["L0_xattn_x_proj_w"].T),
         "dt_projT": f(a["L0_xattn_dt_proj_w"].T), "conv_w": f(a["L0_xattn_conv_w"].reshape(H, CONV)),
         "conv_b": col(a["L0_xattn_conv_b"]), "dt_b": col(a["L0_xattn_dt_proj_b"]), "d_col": col(a["L0_xattn_D"]),
         "a_log": f(a["L0_xattn_A_log"].reshape(TB, P, NST).transpose(1, 2, 0).reshape(P, NST * TB))}
    i["wr0"] = f(np.concatenate([a["L0_ffn_Wr"], a["L0_ffn_Wse"]], 1))
    i["wsg0"], i["wsu0"], i["wsd0"] = (f(a["L0_ffn_" + n]) for n in ("Wsg", "Wsu", "Wsd"))
    i["wg0"], i["wu0"], i["wd0"] = (f(a["L0_ffn_" + n]) for n in ("Wg", "Wu", "Wd"))
    i["wr1"] = f(a["L1_ffn_router_w"])
    i["rbias"] = f(a["L1_ffn_router_bias"].reshape(1, E))
    i["wsg1"], i["wsu1"], i["wsd1"] = (f(a["L1_ffn_" + n]) for n in ("sw_gate", "sw_up", "sw_down"))
    i["wg1"], i["wu1"], i["wd1"] = (f(a["L1_ffn_" + n]) for n in ("w_gate", "w_up", "w_down"))
    i["wq"], i["wo"] = f(a["L1_xattn_Wq"]), f(a["L1_xattn_Wo"])
    by_head = lambda w: f(w.reshape(-1, NH, 2, HD).transpose(0, 2, 1, 3).reshape(-1, 2 * H))
    i["wkv"] = by_head(np.concatenate([a["L1_xattn_Wk"], a["L1_xattn_Wv"]], 1))
    i["bkv"] = by_head(np.concatenate([a["L1_xattn_bk"], a["L1_xattn_bv"]]))
    i["wkvd"] = f(a["L1_xattn_Wkv_dca"])
    i["bkvd"] = f(a["L1_xattn_bkv_dca"].reshape(1, 2 * H))
    i["bq"], i["bo"] = f(a["L1_xattn_bq"].reshape(1, H)), f(a["L1_xattn_bo"].reshape(1, H))
    i["headnorm"] = f(np.stack([a["L1_xattn_" + n] for n in ("qn_w", "qn_b", "kn_w", "kn_b", "kn_dca_w", "kn_dca_b")], 1))
    return i


def kernel(**inputs):
    import concourse.bacc as bacc
    from concourse.bass_utils import run_bass_kernel_spmd

    nc = bacc.Bacc("TRN2", target_bir_lowering=False, num_devices=1)
    host = layouts({k: np.asarray(v) for k, v in inputs.items()})
    I = {k: nc.dram_tensor("in_" + k, v.shape, mybir.dt.from_np(v.dtype), kind="ExternalInput").ap()
         for k, v in host.items()}
    out = nc.dram_tensor("out_x", (T, H), F32, kind="ExternalOutput").ap()
    program(nc, I, out)
    r = run_bass_kernel_spmd(nc, [{"in_" + k: v for k, v in host.items()}], core_ids=[0])
    return r.results[0]["out_x"].reshape(B, S, H)
```

```python
from contextlib import ExitStack

import numpy as np

import concourse.bass as bass
from concourse import mybir

F32 = mybir.dt.float32
BF16 = mybir.dt.bfloat16
I32 = mybir.dt.int32
ALU = mybir.AluOpType
ACT = mybir.ActivationFunctionType
AX_X = mybir.AxisListType.X

P = 128
B, S, H = 4, 512, 512
T = B * S
NT = T // P
TB = S // P
KH = H // P
DM = 256
KC = DM // P
LN_EPS = 1e-5

NST, RK, CONV = 16, 16, 4
XD = RK + 2 * NST

E = 32
F0, FS0, CAP, K0 = 352, 1408, 64, 4
F1, FS1, K1 = 256, 512, 8
GR, GSEL = 8, 4
ROUTED = 2.5
NSLOT0 = E * CAP
NTILE1 = T * K1 // P + E
NSLOT1 = NTILE1 * P
SKIP = 1 << 20

NH, HD = 16, 32
DCA = 16
S2 = S - DCA
HG = 4
NG = NH // HG
GW = HG * HD
SCALE = float(HD) ** -0.5
HEAD_EPS = 1e-6


def bc(ap, axis, n):
    u = ap.unsqueeze(axis)
    shape = list(u.shape)
    shape[axis] = n
    return u.to_broadcast(shape)


def hold(eng, sem, value, held):
    eng.wait_ge(sem, value)
    eng.sem_inc(held, 1)


class Pools:

    def __init__(self, nc, ctx):
        self.nc, self.ctx, self.sems, self.from0 = nc, ctx, [], []

    def sb(self, name, shape, dt=F32):
        return self.ctx.enter_context(self.nc.sbuf_tensor(name, shape, dt))

    def ps(self, name, shape):
        return self.ctx.enter_context(self.nc.psum_tensor(name, shape, F32))

    def sem(self, name):
        self.sems.append(self.nc.alloc_semaphore(name))
        return self.sems[-1]

    def sem0(self, name):
        self.from0.append(self.sem(name))
        return self.from0[-1]

    def start_at_one(self):
        for i, s in enumerate(s for s in self.sems if s not in self.from0):
            (self.nc.gpsimd, self.nc.vector, self.nc.scalar, self.nc.sync)[i % 4].sem_inc(s, 1)
        self.nc.all_engine_barrier()

    def clear(self):
        self.nc.clear_and_free_semaphores(self.sems)
        self.nc.all_engine_barrier()


def constants(nc, pl, c):
    c["ident"] = pl.sb("ident", [P, P])
    c["zeros"] = pl.sb("zeros", [P, P])
    c["ones_bf"] = pl.sb("ones_bf", [P, P], BF16)
    c["before_bf"] = pl.sb("before_bf", [P, P], BF16)
    c["ones_row"] = pl.sb("ones_row", [1, P])
    c["seg"] = pl.sb("seg", [P, NT * E])
    c["seg_t"] = pl.sb("seg_t", [P, E * NT], BF16)
    c["slot0"] = pl.sb("slot0", [P, E])
    c["tile_no"] = pl.sb("tile_no", [P, 2])
    c["minus_half"] = pl.sb("minus_half", [P, E])
    c["half_seg8"] = pl.sb("half_seg8", [P, NT * GR])
    tri_all = pl.sb("tri_all", [P, P])
    idx_i = pl.sb("idx_i", [P, E], I32)
    tile_i = pl.sb("tile_i", [P, 2], I32)
    made, filled, cast = pl.sem("const_made"), pl.sem("const_filled"), pl.sem("const_cast")
    c["held"] = pl.sem("held")
    with nc.Block() as block:

        @block.gpsimd
        def _(pool):
            pool.memset(c["ident"][:, :], 0.0).then_inc(filled, 1)
            pool.memset(tri_all[:, :], 1.0).then_inc(filled, 1)
            pool.memset(c["seg"][:, :], 1.0).then_inc(filled, 1)
            pool.memset(c["half_seg8"][:, :], 1.0).then_inc(filled, 1)
            pool.memset(c["seg_t"][:, :], 1.0).then_inc(filled, 1)
            pool.memset(c["zeros"][:, :], 0.0).then_inc(filled, 1)
            pool.memset(c["ones_bf"][:, :], 1.0).then_inc(filled, 1)
            pool.memset(c["ones_row"][:, :], 1.0).then_inc(filled, 1)
            pool.memset(c["minus_half"][:, :], -0.5).then_inc(filled, 1)
            pool.iota(idx_i[:, :], [[CAP, E]], base=1, channel_multiplier=0).then_inc(filled, 1)
            pool.iota(tile_i[:, :], [[1, 2]], base=0, channel_multiplier=2).then_inc(filled, 1)
            pool.wait_ge(filled, 11)
            pool.affine_select(out=c["ident"][:, :], in_=c["ident"][:, :], compare_op=ALU.not_equal, fill=1.0,
                               base=0, pattern=[[-1, P]], channel_multiplier=1).then_inc(made, 1)
            pool.affine_select(out=tri_all[:, :], in_=tri_all[:, :], compare_op=ALU.is_gt, fill=0.0,
                               base=0, pattern=[[1, P]], channel_multiplier=-1).then_inc(made, 1)
            seg = c["seg"][:, :].rearrange("p (t e) -> p t e", e=E)
            pool.memset(seg[:, :, 0], 0.0).then_inc(made, 1)
            seg8 = c["half_seg8"][:, :].rearrange("p (t e) -> p t e", e=GR)
            pool.memset(seg8[:, :, 0], 0.0).then_inc(made, 1)
            seg_t = c["seg_t"][:, :].rearrange("p (e t) -> p e t", t=NT)
            pool.memset(seg_t[:, :, 0], 0.0).then_inc(made, 1)

        @block.vector
        def _(dve):
            dve.wait_ge(made, 5)
            dve.wait_ge(filled, 11)
            dve.tensor_copy(c["before_bf"][:, :], tri_all[:, :]).then_inc(cast, 1)
            dve.tensor_copy(c["slot0"][:, :], idx_i[:, :]).then_inc(cast, 1)
            dve.tensor_copy(c["tile_no"][:, :], tile_i[:, :]).then_inc(cast, 1)


def mamba_stage(nc, pl0, c, I, D, x):
    with ExitStack() as ctx:
        pl = Pools(nc, ctx)
        ctx.callback(pl.clear)
        RING = 4
        w_in = pl.sb("w_in", [P, KC, H])
        w_xp = pl.sb("w_xp", [P, KH, XD])
        w_dt = pl.sb("w_dt", [RK, H])
        conv_w = pl.sb("conv_w", [P, TB, CONV])
        conv_b = pl.sb("conv_b", [P, TB])
        dt_b = pl.sb("dt_b", [P, TB])
        a_log = pl.sb("a_log", [P, NST, TB])
        a_neg = pl.sb("a_neg", [P, NST, TB])
        d_col = pl.sb("d_col", [P, TB])
        d_diag = pl.sb("d_diag", [P, TB, P])
        ctxT = pl.sb("ctxT", [P, KC, S])
        xpad = pl.sb("xpad", [P, TB, S + CONV - 1])
        conv = pl.sb("conv", [P, TB, S])
        u = pl.sb("u", [P, TB, S])
        xd = pl.sb("xd", [XD, S])
        dt = pl.sb("dt", [P, TB, S])
        du = pl.sb("du", [P, TB, S])
        tmp = pl.sb("tmp", [P, TB, S])
        gate = pl.sb("gate", [P, TB, S])
        dA = pl.sb("dA", [P, 2, TB, S])
        dBu = pl.sb("dBu", [P, 2, TB, S])
        hs = pl.sb("hs", [P, 2, TB, S])
        hc = pl.sb("hc", [P, 2, TB, S])
        bcst = pl.sb("bcst", [P, RING, 2, S])
        st = pl.sb("st", [P, NT, 6])
        mv = pl.sb("mv", [P, NT, 2])
        ve = pl.sb("ve", [P, NT])
        rs = pl.sb("rs", [P, NT])
        nb = pl.sb("nb", [P, NT])
        norm = pl.sb("norm", [P, 2, TB])
        ps_y = pl.ps("ps_y", [P, TB, S])
        ps_w = pl.ps("ps_w", [P, TB, S])

        sem = {n: pl.sem("m_" + n) for n in (
            "weights", "xin", "ctxin", "pad", "aexp", "aneg", "diag", "inproj", "xpadc", "conv", "u", "xproj", "xdc",
            "bcout", "bcin0", "bcin1", "bcin2", "bcin3", "dtmm", "spa", "spb", "spc", "spd", "spe", "spm", "corr",
            "dtc", "dt", "du", "dA", "dBu", "scan", "hc", "sum", "stats", "ve", "rs", "nb", "norm", "gate", "yz",
            "tr", "xadd")}
        sem["zfill"] = pl.sem0("m_zfill")
        bcin = [sem[f"bcin{q}"] for q in range(RING)]
        AHEAD = {"dBu": RING, "hc": RING, "scan": 2, "sum": 2}
        after = lambda name, it: 1 + AHEAD[name] + it + 1
        n_weights = 8
        n_zero = NSLOT0 // (2 * P)

        pl.start_at_one()
        with nc.Block() as block:

            @block.sync
            def _(sp):
                for dst, src in ((w_in[:, :, :], I["in_projT"].rearrange("(k p) n -> p k n", p=P)),
                                 (w_xp[:, :, :], I["x_projT"].rearrange("(k p) n -> p k n", p=P)),
                                 (w_dt[:, :], I["dt_projT"]),
                                 (conv_w[:, :, :], I["conv_w"].rearrange("(t p) j -> p t j", p=P)),
                                 (conv_b[:, :], I["conv_b"]), (dt_b[:, :], I["dt_b"]),
                                 (a_log[:, :, :], I["a_log"].rearrange("p (n t) -> p n t", t=TB)),
                                 (d_col[:, :], I["d_col"])):
                    sp.dma_start(dst, src).then_inc(sem["weights"], 16)
                sp.dma_start(x[:, :, :], I["x"].rearrange("(t p) h -> p t h", p=P)).then_inc(sem["xin"], 16)
                def context(b):
                    sp.dma_start(ctxT[:, :, :], I["ctxT"][:, bass.ds(b * S, S)].rearrange("(k p) n -> p k n", p=P))\
                      .then_inc(sem["ctxin"], 16)

                def batch(b, last=False):
                    if not last:
                        hold(sp, sem["inproj"], 1 + TB * (b + 1), c["held"])
                        context(b + 1)
                    hold(sp, sem["xdc"], 1 + b + 1, c["held"])
                    sp.dma_start(D["bc"][bass.ds(b * 2 * NST, 2 * NST), :], xd[RK:XD, :]).then_inc(sem["bcout"], 16)
                    hold(sp, sem["bcout"], 1 + 16 * (b + 1), c["held"])
                    with sp.Fori(0, NST // RING) as n4:
                        for q in range(RING):
                            it = b * NST + n4 * RING + q
                            hold(sp, sem["dBu"], after("dBu", it - RING), c["held"])
                            hold(sp, sem["hc"], after("hc", it - RING), c["held"])
                            for w in range(2):
                                row = D["bc"][bass.ds(b * 2 * NST + w * NST + n4 * RING + q, 1), :]
                                sp.dma_start(bcst[:, q, w, :], row.to_broadcast([P, S])).then_inc(bcin[q], 16)

                context(0)
                with sp.Fori(0, B - 1) as b:
                    batch(b)
                batch(B - 1, last=True)

            @block.gpsimd
            def _(pool):
                pool.sem_inc(sem["hc"], AHEAD["hc"])
                with pool.Fori(0, n_zero) as i:
                    pool.dma_start(D["xs0"][bass.ds(i * 2 * P, 2 * P), :].rearrange("(p a) (c z) -> p (a c) z", a=2, z=P),
                                   bc(c["zeros"][:, :], 1, 2 * H // P)).then_inc(sem["zfill"], 16)
                pool.wait_ge(sem["ve"], 1 + 1)
                pool.tensor_tensor(rs[:, :], ve[:, :], c["minus_half"][:, 0:NT], ALU.pow).then_inc(sem["rs"], 1)
                with pool.Fori(0, B) as b:
                    with pool.Fori(0, NST // RING) as n4:
                        for q in range(RING):
                            it = b * NST + n4 * RING + q
                            pool.wait_ge(bcin[q], 1 + 32 * (b * (NST // RING) + n4 + 1))
                            pool.wait_ge(sem["scan"], after("scan", it))
                            pool.wait_ge(sem["sum"], after("sum", it - 2))
                            pool.tensor_tensor(hc[:, q % 2, :, :], hs[:, q % 2, :, :], bc(bcst[:, q, 1, :], 1, TB),
                                               ALU.mult).then_inc(sem["hc"], 1)
                pool.wait_ge(sem["zfill"], 16 * n_zero)

            @block.scalar
            def _(act):
                act.wait_ge(sem["weights"], 1 + 16 * n_weights)
                act.activation(a_neg[:, :, :], a_log[:, :, :], ACT.Exp).then_inc(sem["aexp"], 1)
                def padded(b):
                    for t in range(TB):
                        act.wait_ge(sem["inproj"], 1 + TB * b + t + 1)
                        act.wait_ge(sem["conv"], 1 + TB * b)
                        act.wait_ge(sem["pad"], 1 + 1)
                        act.activation(xpad[:, t, CONV - 1:], ps_w[:, t, :], ACT.Copy).then_inc(sem["xpadc"], 1)

                def batch(b, last=False):
                    act.wait_ge(sem["sum"], after("sum", NST * b - 1))
                    for t in range(TB):
                        act.wait_ge(sem["conv"], 1 + TB * b + t + 1)
                        act.activation(u[:, t, :], conv[:, t, :], ACT.Silu, bias=conv_b[:, t:t + 1]).then_inc(sem["u"], 1)
                    for t in range(TB):
                        act.wait_ge(sem["dtmm"], 1 + TB * b + t + 1)
                        act.activation(tmp[:, t, :], ps_w[:, t, :], ACT.Abs, bias=dt_b[:, t:t + 1]).then_inc(sem["spa"], 1)
                    for t in range(TB):
                        act.wait_ge(sem["spa"], 1 + TB * b + t + 1)
                        act.activation(tmp[:, t, :], tmp[:, t, :], ACT.Exp, scale=-1.0).then_inc(sem["spb"], 1)
                    act.wait_ge(sem["tr"], 1 + TB * b)
                    for t in range(TB):
                        act.wait_ge(sem["spc"], 1 + TB * b + t + 1)
                        act.activation(gate[:, t, :], conv[:, t, :], ACT.Ln).then_inc(sem["spd"], 1)
                    act.wait_ge(sem["aneg"], 1 + 1)
                    act.wait_ge(sem["dt"], 1 + TB * (b + 1))
                    with act.Fori(0, NST // RING) as n4:
                        for q in range(RING):
                            act.wait_ge(sem["scan"], after("scan", b * NST + n4 * RING + q - 2))
                            for t in range(TB):
                                i = act.activation(dA[:, q % 2, t, 1:], dt[:, t, 1:], ACT.Exp,
                                                   scale=a_neg[:, n4 * RING + q, t:t + 1])
                            i.then_inc(sem["dA"], 1)
                    act.wait_ge(sem["norm"], 1 + 2 * (b + 1))
                    for t in range(TB):
                        act.activation(gate[:, t, :], x[:, b * TB + t, :], ACT.Silu, scale=norm[:, 0, t:t + 1],
                                       bias=norm[:, 1, t:t + 1]).then_inc(sem["gate"], 1)
                    if not last:
                        padded(b + 1)

                padded(0)
                with act.Fori(0, B - 1) as b:
                    batch(b)
                batch(B - 1, last=True)

            @block.vector
            def _(dve):
                dve.sem_inc(sem["dBu"], AHEAD["dBu"])
                dve.sem_inc(sem["scan"], AHEAD["scan"])
                dve.memset(xpad[:, :, 0:CONV - 1], 0.0).then_inc(sem["pad"], 1)
                dve.memset(dA[:, :, :, 0:1], 0.0).then_inc(sem["diag"], 1)
                dve.wait_ge(sem["aexp"], 1 + 1)
                dve.tensor_scalar(a_neg[:, :, :], a_neg[:, :, :], -1.0, None, ALU.mult).then_inc(sem["aneg"], 1)
                for t in range(TB):
                    dve.tensor_scalar(d_diag[:, t, :], c["ident"][:, :], d_col[:, t:t + 1], None, ALU.mult)\
                       .then_inc(sem["diag"], 1)
                dve.wait_ge(sem["xin"], 1 + 16)
                for j in range(NT):
                    dve.bn_stats(st[:, j, :], x[:, j, :]).then_inc(sem["stats"], 1)
                dve.wait_ge(sem["stats"], 1 + NT)
                for j in range(NT):
                    dve.bn_aggr(mv[:, j, :], st[:, j, :]).then_inc(sem["stats"], 1)
                dve.wait_ge(sem["stats"], 1 + 2 * NT)
                dve.tensor_scalar(ve[:, :], mv[:, :, 1], LN_EPS, None, ALU.add).then_inc(sem["ve"], 1)
                dve.wait_ge(sem["rs"], 1 + 1)
                dve.scalar_tensor_tensor(out=nb[:, :], in0=mv[:, :, 0], scalar=-1.0, in1=rs[:, :],
                                         op0=ALU.mult, op1=ALU.mult).then_inc(sem["nb"], 1)
                dve.wait_ge(sem["nb"], 1 + 1)
                dve.wait_ge(sem["diag"], 1 + 1)
                def convolve(b):
                    for t in range(TB):
                        dve.wait_ge(sem["xpadc"], 1 + TB * b + t + 1)
                        dve.tensor_scalar(conv[:, t, :], xpad[:, t, 0:S], conv_w[:, t, 0:1], None, ALU.mult)\
                           .then_inc(sem["spe"], 1)
                        for j in range(1, CONV):
                            dve.wait_ge(sem["spe"], 1 + (TB * b + t) * (CONV - 1) + j)
                            dve.scalar_tensor_tensor(out=conv[:, t, :], in0=xpad[:, t, j:j + S],
                                                     scalar=conv_w[:, t, j:j + 1], in1=conv[:, t, :],
                                                     op0=ALU.mult, op1=ALU.add)\
                               .then_inc(sem["spe"] if j < CONV - 1 else sem["conv"], 1)

                def batch(b, last=False):
                    dve.tensor_copy(norm[:, 0, :], rs[:, bass.ds(b * TB, TB)]).then_inc(sem["norm"], 1)
                    dve.tensor_copy(norm[:, 1, :], nb[:, bass.ds(b * TB, TB)]).then_inc(sem["norm"], 1)
                    dve.wait_ge(sem["xproj"], 1 + b + 1)
                    dve.tensor_copy(xd[:, :], ps_w[0:XD, 0, :]).then_inc(sem["xdc"], 1)
                    for t in range(TB):
                        dve.wait_ge(sem["spa"], 1 + TB * b + t + 1)
                        dve.tensor_scalar(dt[:, t, :], ps_w[:, t, :], dt_b[:, t:t + 1], 0.0, ALU.add, ALU.max)\
                           .then_inc(sem["spm"], 1)
                    dve.wait_ge(sem["u"], 1 + TB * (b + 1))
                    for t in range(TB):
                        dve.wait_ge(sem["spb"], 1 + TB * b + t + 1)
                        dve.tensor_scalar(conv[:, t, :], tmp[:, t, :], 1.0, None, ALU.add).then_inc(sem["spc"], 1)
                    for t in range(TB):
                        dve.wait_ge(sem["spc"], 1 + TB * b + t + 1)
                        dve.scalar_tensor_tensor(out=tmp[:, t, :], in0=conv[:, t, :], scalar=-1.0, in1=tmp[:, t, :],
                                                 op0=ALU.add, op1=ALU.subtract).then_inc(sem["corr"], 1)
                    for t in range(TB):
                        dve.wait_ge(sem["spd"], 1 + TB * b + t + 1)
                        dve.wait_ge(sem["corr"], 1 + TB * b + t + 1)
                        dve.tensor_tensor(tmp[:, t, :], gate[:, t, :], tmp[:, t, :], ALU.subtract).then_inc(sem["dtc"], 1)
                    for t in range(TB):
                        dve.wait_ge(sem["dtc"], 1 + TB * b + t + 1)
                        dve.tensor_tensor(dt[:, t, :], dt[:, t, :], tmp[:, t, :], ALU.add).then_inc(sem["dt"], 1)
                    for t in range(TB):
                        dve.wait_ge(sem["dt"], 1 + TB * b + t + 1)
                        dve.tensor_tensor(du[:, t, :], dt[:, t, :], u[:, t, :], ALU.mult).then_inc(sem["du"], 1)
                    dve.wait_ge(sem["du"], 1 + TB * (b + 1))
                    dve.sem_inc(c["held"], 1)
                    flat = "p t s -> p (t s)"
                    with dve.Fori(0, NST // RING) as n4:
                        for q in range(RING):
                            it = b * NST + n4 * RING + q
                            dve.wait_ge(bcin[q], 1 + 32 * (b * (NST // RING) + n4 + 1))
                            dve.wait_ge(sem["scan"], after("scan", it - 2))
                            dve.tensor_tensor(dBu[:, q % 2, :, :], du[:, :, :], bc(bcst[:, q, 0, :], 1, TB), ALU.mult)\
                               .then_inc(sem["dBu"], 1)
                            dve.wait_ge(sem["dBu"], after("dBu", it))
                            dve.wait_ge(sem["dA"], 1 + it + 1)
                            dve.wait_ge(sem["hc"], after("hc", it - 2))
                            dve.tensor_tensor_scan(hs[:, q % 2, :, :].rearrange(flat), dA[:, q % 2, :, :].rearrange(flat),
                                                   dBu[:, q % 2, :, :].rearrange(flat), 0.0, ALU.mult, ALU.add)\
                               .then_inc(sem["scan"], 1)
                    if not last:
                        dve.wait_ge(sem["spd"], 1 + TB * (b + 1))
                        convolve(b + 1)
                    dve.wait_ge(sem["sum"], after("sum", NST * (b + 1) - 1))
                    for t in range(TB):
                        dve.wait_ge(sem["gate"], 1 + TB * b + t + 1)
                        dve.tensor_tensor(gate[:, t, :], ps_y[:, t, :], gate[:, t, :], ALU.mult).then_inc(sem["yz"], 1)
                    for t in range(TB):
                        dve.wait_ge(sem["tr"], 1 + TB * b + t + 1)
                        xt = x[:, b * TB + t, :]
                        dve.tensor_tensor(xt, ps_y[:, t, :], xt, ALU.add).then_inc(sem["xadd"], 1)

                convolve(0)
                with dve.Fori(0, B - 1) as b:
                    batch(b)
                batch(B - 1, last=True)

            @block.tensor
            def _(pe):
                pe.sem_inc(sem["sum"], AHEAD["sum"])
                pe.wait_ge(sem["weights"], 1 + 16 * n_weights)
                pe.wait_ge(sem["diag"], 1 + 1 + TB)
                def project(b):
                    pe.wait_ge(sem["ctxin"], 1 + 16 * (b + 1))
                    pe.wait_ge(sem["spm"], 1 + TB * b)
                    for t in range(TB):
                        for k in range(KC):
                            i = pe.matmul(ps_w[:, t, :], w_in[:, k, t * P:(t + 1) * P], ctxT[:, k, :],
                                          start=k == 0, stop=k == KC - 1)
                        i.then_inc(sem["inproj"], 1)

                def batch(b, last=False):
                    pe.wait_ge(sem["u"], 1 + TB * (b + 1))
                    pe.wait_ge(sem["bcout"], 1 + 16 * b)
                    pe.wait_ge(sem["xpadc"], 1 + TB * (b + 1))
                    for k in range(KH):
                        i = pe.matmul(ps_w[0:XD, 0, :], w_xp[:, k, :], u[:, k, :], start=k == 0, stop=k == KH - 1)
                    i.then_inc(sem["xproj"], 1)
                    pe.wait_ge(sem["xdc"], 1 + b + 1)
                    for t in range(TB):
                        pe.matmul(ps_w[:, t, :], w_dt[:, t * P:(t + 1) * P], xd[0:RK, :], start=True, stop=True)\
                          .then_inc(sem["dtmm"], 1)
                    pe.wait_ge(sem["xadd"], 1 + TB * b)
                    for t in range(TB):
                        pe.matmul(ps_y[:, t, :], d_diag[:, t, :], u[:, t, :], start=True, stop=False,
                                  skip_group_check=True)
                    if not last:
                        project(b + 1)
                    with pe.Fori(0, NST // RING) as n4:
                        for q in range(RING):
                            pe.wait_ge(sem["hc"], after("hc", b * NST + n4 * RING + q))
                            for t in range(TB):
                                i = pe.matmul(ps_y[:, t, :], c["ident"][:, :], hc[:, q % 2, t, :], start=False,
                                              stop=False, skip_group_check=True)
                            i.then_inc(sem["sum"], 1)
                    pe.wait_ge(sem["yz"], 1 + TB * (b + 1))
                    for lt in range(TB):
                        for t in range(TB):
                            i = pe.transpose(ps_y[:, lt, t * P:(t + 1) * P], gate[:, t, lt * P:(lt + 1) * P],
                                             c["ident"][:, :])
                        i.then_inc(sem["tr"], 1)

                project(0)
                with pe.Fori(0, B - 1) as b:
                    batch(b)
                batch(B - 1, last=True)


def select(dve, pause, step, vals, m8, k, W, seg, gt, eq, cnt, cum):
    flat = "p t e -> p (t e)"
    pause()
    for j in range(NT):
        step(dve.max(m8[:, j, :], vals[:, j, :]), wait=j == NT - 1)
    kth = bc(m8[:, :, k - 1], 2, W)
    step(dve.tensor_tensor(gt, vals, kth, ALU.is_gt), wait=False)
    step(dve.tensor_tensor(eq, vals, kth, ALU.is_equal))
    step(dve.tensor_reduce(cnt, gt, AX_X, ALU.add), wait=False)
    step(dve.tensor_tensor_scan(cum.rearrange(flat), seg, eq.rearrange(flat), 0.0, ALU.mult, ALU.add))
    step(dve.tensor_tensor(cum, cum, bc(cnt, 2, W), ALU.add))
    step(dve.scalar_tensor_tensor(out=eq.rearrange(flat), in0=cum.rearrange(flat), scalar=float(k),
                                  in1=eq.rearrange(flat), op0=ALU.is_le, op1=ALU.mult))
    step(dve.tensor_tensor(gt, gt, eq, ALU.add))


def route_stage(nc, c, I, D, x, L, route):
    K, FS = (K0, FS0) if L == 0 else (K1, FS1)
    FC = FS // P
    NR = E + 1 if L == 0 else E
    R = f"r{L}_"
    slots = D["xs0"] if L == 0 else D["xs1"]
    nslot = NSLOT0 if L == 0 else NSLOT1
    scat, gath, wsel = route["scat"], route["gath"], route["wsel"]
    with ExitStack() as ctx:
        pl = Pools(nc, ctx)
        ctx.callback(pl.clear)
        sb = lambda n, shape, dt=F32: pl.sb(R + n, shape, dt)
        wr = sb("wr", [P, KH, NR])
        wg = sb("wg", [P, KH, FS])
        wu = sb("wu", [P, KH, FS])
        wd = sb("wd", [P, FC, H])
        xn = sb("xn", [P, NT, H])
        xnT = sb("xnT", [P, KH, T])
        h = sb("h", [P, max(FC, 2 * TB), S])
        xnb = h[:, 0:TB, :]
        xnTb = h[:, TB:2 * TB, :]
        sg = sb("sg", [P, 2, S])
        st = sb("st", [P, TB, 6])
        mv = sb("mv", [P, TB, 2])
        ve = sb("ve", [P, TB])
        rs = sb("rs", [P, TB])
        if L == 0:
            late = h[:, FC - 3:FC, :].rearrange("p f s -> p (f s)")
            lgs = late[:, 0:NT * NR].rearrange("p (t e) -> p t e", e=NR)
            eq = late[:, NT * NR:NT * (NR + E)].rearrange("p (t e) -> p t e", e=E)
            m8 = late[:, NT * (NR + E):NT * (NR + E + 8)].rearrange("p (t e) -> p t e", e=8)
        else:
            eq = sb("eq", [P, NT, E])
            m8 = sb("m8", [P, NT, 8])
        mx = sb("mx", [P, NT])
        sc = sb("sc", [P, NT, E])
        sel = sb("sel", [P, NT, E])
        few = sb("few", [P, 2, TB, E])
        hit = sb("hit", [P, TB, K, E])
        cum = hit[:, :, :, :].rearrange("p t k e -> p (t k) e")[:, 0:NT, :]
        pos = sb("pos", [P, NT, E])
        cnt = sb("cnt", [P, NT])
        k8 = sb("k8", [P, TB, 8])
        selb = sb("selb", [P, NT, E], BF16)
        earlier = sb("earlier", [P, NT, E], BF16)
        allb = sb("allb", [P, E], BF16)
        base = sb("base", [P, E])
        gate = sb("gate", [P, NT])
        tk = sb("tk", [P, TB, K])
        if L == 1:
            bias = sb("bias", [P, E])
            sb_ = sb("sb", [P, NT, E])
            pr = sb("pr", [P, 4, NT * GR])
            gs = sb("gs", [P, NT, GR])
            gm = sb("gm", [P, NT, GR])
            geq = sb("geq", [P, NT, GR])
            gcum = sb("gcum", [P, NT, GR])
            ones_e = sb("ones_e", [P, E])
            past = sb("past", [P, E])
            ti = sb("ti", [P, E], I32)
            tf = sb("tf", [P, E])
            tcum = sb("tcum", [P, E])
            te = sb("te", [P, 2])
            tei = sb("tei", [P, 2], I32)
        ps_t = pl.ps(R + "ps_t", [P, 2, S])
        ps_r = pl.ps(R + "ps_r", [P, 512])
        ps_p = pl.ps(R + "ps_p", [P, 512])
        ps_g = pl.ps(R + "ps_g", [P, 2, S])
        ps_u = pl.ps(R + "ps_u", [P, 2, S])
        lg = ps_r[:, 0:TB * NR].rearrange("p (t e) -> p t e", e=NR)
        sem = {n: pl.sem(R + n) for n in (
            "win", "wrin", "stats", "ve", "rs", "xnb", "tr", "xnTb", "xnT", "logits", "lg", "centred", "score", "gate",
            "chain", "sel", "pos", "idx", "g", "u", "sg", "h", "down", "xadd", "eid", "eidout")}
        sem["scat"] = pl.sem0(R + "scat")
        tiled = "(k p) n -> p k n"
        n_in = 3
        n_r = 2 if L == 1 else 1

        pl.start_at_one()
        with nc.Block() as block:

            @block.sync
            def _(sp):
                sp.dma_start(wr[:, :, :], I[f"wr{L}"].rearrange(tiled, p=P)).then_inc(sem["wrin"], 16)
                if L == 1:
                    sp.dma_start(bias[:, :], I["rbias"].to_broadcast([P, E])).then_inc(sem["wrin"], 16)
                sp.dma_start(wg[:, :, :], I[f"wsg{L}"].rearrange(tiled, p=P)).then_inc(sem["win"], 16)
                sp.dma_start(wu[:, :, :], I[f"wsu{L}"].rearrange(tiled, p=P)).then_inc(sem["win"], 16)
                sp.dma_start(wd[:, :, :], I[f"wsd{L}"].rearrange(tiled, p=P)).then_inc(sem["win"], 16)
                if L == 1:
                    sp.wait_ge(sem["eid"], 1 + 1)
                    sp.dma_start(D["expert"].rearrange("(p a) o -> p (a o)", a=2), tei[:, :]).then_inc(sem["eidout"], 16)
                    sp.wait_ge(sem["eidout"], 1 + 16)

            @block.gpsimd
            def _(pool):
                with pool.Fori(0, B) as b:
                    pool.wait_ge(sem["ve"], 1 + b + 1)
                    pool.tensor_tensor(rs[:, :], ve[:, :], c["minus_half"][:, 0:TB], ALU.pow).then_inc(sem["rs"], 1)
                for t in range(NT):
                    pool.wait_ge(sem["idx"], 1 + t // TB + 1)
                    for k in range(K):
                        pool.indirect_dma_start(slots[:, :], bass.IndirectOffsetOnAxis(scat[:, t, k:k + 1], 0),
                                                xn[:, t, :], None, bounds_check=nslot - 1, oob_is_err=False)\
                            .then_inc(sem["scat"], 16)
                pool.wait_ge(sem["scat"], 16 * NT * K)

            @block.scalar
            def _(act):
                with act.Fori(0, B) as b:
                    act.wait_ge(sem["xnT"], 1 + b)
                    act.wait_ge(sem["logits"], 1 + b)
                    for k in range(KH):
                        act.wait_ge(sem["tr"], 1 + KH * b + k + 1)
                        act.activation(xnTb[:, k, :], ps_t[:, k % 2, :], ACT.Copy).then_inc(sem["xnTb"], 1)
                    act.wait_ge(sem["logits"], 1 + b + 1)
                    if L == 0:
                        act.activation(lgs[:, bass.ds(b * TB, TB), :], lg, ACT.Copy).then_inc(sem["lg"], 1)
                    else:
                        act.activation(sc[:, bass.ds(b * TB, TB), :], lg, ACT.Sigmoid).then_inc(sem["lg"], 1)
                if L == 0:
                    act.wait_ge(sem["lg"], 1 + B)
                    act.activation(gate[:, :], lgs[:, :, E], ACT.Sigmoid).then_inc(sem["gate"], 1)
                    act.wait_ge(sem["centred"], 1 + 1)
                    act.activation(sc[:, :, :], sc[:, :, :], ACT.Exp).then_inc(sem["score"], 1)
                with act.Fori(0, B) as b:
                    for f in range(FC):
                        n = FC * b + f
                        act.wait_ge(sem["g"], 1 + n + 1)
                        if f >= 2:
                            act.wait_ge(sem["h"], 1 + n - 1)
                        else:
                            act.wait_ge(sem["h"], 1 + FC * b)
                        act.activation(sg[:, f % 2, :], ps_g[:, f % 2, :], ACT.Silu).then_inc(sem["sg"], 1)

            @block.vector
            def _(dve):
                done = [0, 0]

                def step(ins, wait=True):
                    ins.then_inc(sem["chain"], 1)
                    done[1] += 1
                    if wait:
                        dve.wait_ge(sem["chain"], 1 + done[0] + done[1])
                    return ins

                def pause():
                    dve.sem_inc(c["held"], 1)

                with dve.Fori(0, B) as b:
                    for j in range(TB):
                        dve.bn_stats(st[:, j, :], x[:, b * TB + j, :]).then_inc(sem["stats"], 1)
                    hold(dve, sem["stats"], 1 + 2 * TB * b + TB, c["held"])
                    for j in range(TB):
                        dve.bn_aggr(mv[:, j, :], st[:, j, :]).then_inc(sem["stats"], 1)
                    dve.wait_ge(sem["stats"], 1 + 2 * TB * (b + 1))
                    dve.tensor_scalar(ve[:, :], mv[:, :, 1], LN_EPS, None, ALU.add).then_inc(sem["ve"], 1)
                    dve.wait_ge(sem["rs"], 1 + b + 1)
                    dve.wait_ge(sem["tr"], 1 + KH * b)
                    for j in range(TB):
                        for dst in (xnb[:, j, :], xn[:, b * TB + j, :]):
                            i = dve.tensor_scalar(dst, x[:, b * TB + j, :], mv[:, j, 0:1], rs[:, j:j + 1],
                                                  ALU.subtract, ALU.mult)
                    i.then_inc(sem["xnb"], 1)
                    dve.wait_ge(sem["xnTb"], 1 + KH * (b + 1))
                    dve.tensor_copy(xnT[:, :, bass.ds(b * S, S)], xnTb).then_inc(sem["xnT"], 1)

                def product(b, f):
                    n = FC * b + f
                    dve.wait_ge(sem["sg"], 1 + n + 1)
                    dve.wait_ge(sem["u"], 1 + n + 1)
                    if f == 0:
                        dve.wait_ge(sem["down"], 1 + TB * b)
                    dve.tensor_tensor(h[:, f, :], ps_u[:, f % 2, :], sg[:, f % 2, :], ALU.mult)\
                       .then_inc(sem["h"], 1)

                def slots_of(b, base1, between=None):
                    bt = bass.ds(b * TB, TB)
                    slot, weight, kept = few[:, 0, :, :], few[:, 1, :, :], hit[:, :, 0, :]
                    step(dve.tensor_tensor(slot, pos[:, bt, :], bc(base1[:, :], 1, TB), ALU.add))
                    if L == 0:
                        step(dve.scalar_tensor_tensor(out=kept, in0=pos[:, bt, :], scalar=float(CAP),
                                                      in1=sel[:, bt, :], op0=ALU.is_lt, op1=ALU.mult))
                        step(dve.tensor_tensor(weight, sc[:, bt, :], kept, ALU.mult), wait=False)
                        step(dve.tensor_tensor(slot, slot, kept, ALU.mult))
                    else:
                        step(dve.tensor_copy(weight, sc[:, bt, :]), wait=False)
                        step(dve.tensor_tensor(slot, slot, sel[:, bt, :], ALU.mult))
                    pause()
                    for j in range(TB):
                        step(dve.max(k8[:, j, :], slot[:, j, :]), wait=j == TB - 1)
                    if between:
                        between()
                    for j in range(TB):
                        step(dve.tensor_tensor(hit[:, j, :, :], bc(slot[:, j, :], 1, K), bc(k8[:, j, 0:K], 2, E),
                                               ALU.is_equal), wait=j == TB - 1)
                    for j in range(TB):
                        step(dve.tensor_tensor(hit[:, j, :, :], hit[:, j, :, :], bc(weight[:, j, :], 1, K), ALU.mult),
                             wait=j == TB - 1)
                    ks = k8[:, :, 0:K]
                    step(dve.tensor_reduce(wsel[:, bt, 0:K], hit[:, :, :, :], AX_X, ALU.add), wait=False)
                    step(dve.tensor_scalar(tk[:, :, :], ks, 1.0, float(SKIP), ALU.is_lt, ALU.mult))
                    step(dve.tensor_tensor(tk[:, :, :], tk[:, :, :], ks, ALU.add))
                    step(dve.tensor_scalar(scat[:, bt, 0:K], tk[:, :, :], -1.0, None, ALU.add), wait=False)
                    dve.tensor_scalar(gath[:, bt, 0:K], ks, -1.0, 0.0, ALU.add, ALU.max).then_inc(sem["idx"], 1)

                def add_shared(b):
                    for j in range(TB):
                        dve.wait_ge(sem["down"], 1 + TB * b + j + 1)
                        xt = x[:, b * TB + j, :]
                        if L == 0:
                            dve.scalar_tensor_tensor(out=xt, in0=ps_t[:, j % 2, :], scalar=gate[:, bass.ds(b * TB + j, 1)],
                                                     in1=xt, op0=ALU.mult, op1=ALU.add).then_inc(sem["xadd"], 1)
                        else:
                            dve.tensor_tensor(xt, ps_t[:, j % 2, :], xt, ALU.add).then_inc(sem["xadd"], 1)

                dve.wait_ge(sem["lg"], 1 + B)
                dve.wait_ge(sem["xnT"], 1 + B)
                if L == 0:
                    step(dve.tensor_reduce(mx[:, :], lgs[:, :, 0:E], AX_X, ALU.max))
                    dve.tensor_tensor(sc[:, :, :], lgs[:, :, 0:E], bc(mx[:, :], 2, E), ALU.subtract)\
                       .then_inc(sem["centred"], 1)
                    dve.wait_ge(sem["score"], 1 + 1)
                    chosen_from = sc
                    product(0, 0)
                else:
                    dve.wait_ge(sem["wrin"], 1 + 32)
                    step(dve.tensor_tensor(sb_[:, :, :], sc[:, :, :], bc(bias[:, :], 1, NT), ALU.add))
                    four = sb_[:, :, :].rearrange("p t (g i) -> p (t g) i", i=GR // 2)
                    mx01, mn01, mx23, mn23 = (pr[:, i, :] for i in range(4))
                    step(dve.tensor_tensor(mx01, four[:, :, 0], four[:, :, 1], ALU.max), wait=False)
                    step(dve.tensor_tensor(mn01, four[:, :, 0], four[:, :, 1], ALU.min), wait=False)
                    step(dve.tensor_tensor(mx23, four[:, :, 2], four[:, :, 3], ALU.max), wait=False)
                    step(dve.tensor_tensor(mn23, four[:, :, 2], four[:, :, 3], ALU.min))
                    gflat = gs[:, :, :].rearrange("p t g -> p (t g)")
                    step(dve.tensor_tensor(mn01, mn01, mn23, ALU.max))
                    step(dve.tensor_tensor(mn23, mx01, mx23, ALU.min), wait=False)
                    step(dve.tensor_tensor(gflat, mx01, mx23, ALU.max))
                    step(dve.tensor_tensor(mn01, mn01, mn23, ALU.max))
                    step(dve.tensor_tensor(gflat, gflat, mn01, ALU.add))
                    select(dve, pause, step, gs[:, :, :], m8[:, :, :], GSEL, GR, c["half_seg8"][:, :],
                           gm[:, :, :], geq[:, :, :], cnt[:, :], gcum[:, :, :])
                    product(0, 0)
                    step(dve.tensor_tensor(four, four, bc(gm[:, :, :].rearrange("p t g -> p (t g)"), 2, GR // 2),
                                           ALU.mult))
                    chosen_from = sb_
                select(dve, pause, step, chosen_from[:, :, :], m8[:, :, :], K, E, c["seg"][:, :],
                       sel[:, :, :], eq[:, :, :], cnt[:, :], cum[:, :, :])
                product(0, 1)
                chosen, so_far = (v[:, :, :].rearrange("p t e -> p (t e)") for v in (cum, eq))
                by_expert = lambda v: v.rearrange("p (e t) -> p t e", t=NT)
                step(dve.tensor_copy(selb[:, :, :], sel[:, :, :]), wait=False)
                step(dve.tensor_copy(by_expert(chosen), sel[:, :, :]))
                step(dve.tensor_tensor_scan(so_far, c["seg_t"][:, :], chosen, 0.0, ALU.mult, ALU.add))
                step(dve.tensor_copy(allb[:, :], by_expert(so_far)[:, NT - 1, :]), wait=False)
                dve.tensor_tensor(earlier[:, :, :], by_expert(so_far), sel[:, :, :], ALU.subtract).then_inc(sem["sel"], 1)
                step(dve.tensor_tensor(sc[:, :, :], sc[:, :, :], sel[:, :, :], ALU.mult))
                step(dve.tensor_reduce(cnt[:, :], sc[:, :, :], AX_X, ALU.add))
                step(dve.reciprocal(mx[:, :], cnt[:, :]))
                if L == 1:
                    step(dve.tensor_scalar(mx[:, :], mx[:, :], ROUTED, None, ALU.mult))
                step(dve.tensor_tensor(sc[:, :, :], sc[:, :, :], bc(mx[:, :], 2, E), ALU.mult))
                dve.wait_ge(sem["pos"], 1 + 1)
                step(dve.tensor_copy(pos[:, :, :].rearrange("p t e -> p (t e)"), ps_p[:, :]))
                if L == 0:
                    base1 = c["slot0"]
                else:
                    step(dve.memset(ones_e[:, :], 1.0), wait=False)
                    step(dve.tensor_scalar(tf[:, :], ps_r[:, 0:E], float(P - 1), None, ALU.add))
                    step(dve.tensor_copy(ti[:, :], tf[:, :]))
                    step(dve.tensor_scalar(ti[:, :], ti[:, :], 7, None, ALU.arith_shift_right))
                    step(dve.tensor_copy(tf[:, :], ti[:, :]))
                    step(dve.tensor_tensor_scan(tcum[:, :], ones_e[:, :], tf[:, :], 0.0, ALU.mult, ALU.add))
                    step(dve.tensor_copy(route["ends"][0:1, 1:], tcum[0:1, :]), wait=False)
                    step(dve.memset(route["ends"][0:1, 0:1], 0), wait=False)
                    step(dve.tensor_tensor(base[:, :], tcum[:, :], tf[:, :], ALU.subtract))
                    step(dve.tensor_scalar(base[:, :], base[:, :], float(P), 1.0, ALU.mult, ALU.add))
                    for a in range(2):
                        step(dve.tensor_scalar(past[:, :], tcum[:, :], c["tile_no"][:, a:a + 1], None, ALU.is_le))
                        step(dve.tensor_reduce(te[:, a:a + 1], past[:, :], AX_X, ALU.add))
                    step(dve.tensor_scalar(te[:, :], te[:, :], float(E - 1), None, ALU.min))
                    dve.tensor_copy(tei[:, :], te[:, :]).then_inc(sem["eid"], 1)
                    base1 = base
                slots_of(0, base1, lambda: product(0, 2))
                for f in range(3, FC):
                    product(0, f)
                if L == 0:
                    dve.wait_ge(sem["gate"], 1 + 1)
                add_shared(0)
                first = done[1]
                F_STEPS = 24
                with dve.Fori(1, B) as b:
                    done[0], done[1] = first + (b - 1) * F_STEPS, 0
                    for f in range(2):
                        product(b, f)
                    slots_of(b, base1, lambda: product(b, 2))
                    assert done[1] <= F_STEPS, done
                    if done[1] < F_STEPS:
                        dve.sem_inc(sem["chain"], F_STEPS - done[1])
                    for f in range(3, FC):
                        product(b, f)
                    add_shared(b)

            @block.tensor
            def _(pe):
                pe.wait_ge(sem["wrin"], 1 + 16 * n_r)
                with pe.Fori(0, B) as b:
                    pe.wait_ge(sem["xnb"], 1 + b + 1)
                    for k in range(KH):
                        pe.wait_ge(sem["xnTb"], 1 + KH * b + max(k - 1, 0))
                        for j in range(TB):
                            i = pe.transpose(ps_t[:, k % 2, j * P:(j + 1) * P], xnb[:, j, k * P:(k + 1) * P],
                                             c["ident"][:, :])
                        i.then_inc(sem["tr"], 1)
                    pe.wait_ge(sem["xnTb"], 1 + KH * (b + 1))
                    pe.wait_ge(sem["lg"], 1 + b)
                    for j in range(TB):
                        for k in range(KH):
                            i = pe.matmul(lg[:, j, :], xnTb[:, k, j * P:(j + 1) * P], wr[:, k, :], start=k == 0, stop=k == KH - 1)
                    i.then_inc(sem["logits"], 1)
                pe.wait_ge(sem["win"], 1 + 16 * n_in)
                pe.wait_ge(sem["xnT"], 1 + B)

                def chunk(b, f):
                    n = FC * b + f
                    for src, ps, w, taken in (("g", ps_g, wg, "sg"), ("u", ps_u, wu, "h")):
                        pe.wait_ge(sem[taken], 1 + (n - 1 if f >= 2 else FC * b))
                        for k in range(KH):
                            i = pe.matmul(ps[:, f % 2, :], w[:, k, f * P:(f + 1) * P], xnT[:, k, bass.ds(b * S, S)],
                                          start=k == 0, stop=k == KH - 1)
                        i.then_inc(sem[src], 1)

                def positions():
                    pe.wait_ge(sem["sel"], 1 + 1)
                    pe.wait_ge(sem["lg"], 1 + B)
                    flat = "p t e -> p (t e)"
                    pe.matmul(ps_p[:, :], c["before_bf"][:, :], selb[:, :, :].rearrange(flat), start=True, stop=False)
                    i = pe.matmul(ps_p[:, :], c["ones_bf"][:, :], earlier[:, :, :].rearrange(flat), start=False, stop=True)
                    if L == 1:
                        i = pe.matmul(ps_r[:, 0:E], c["ones_bf"][:, :], allb[:, :], start=True, stop=True)
                    i.then_inc(sem["pos"], 1)

                def down(b):
                    pe.wait_ge(sem["h"], 1 + FC * (b + 1))
                    for j in range(TB):
                        pe.wait_ge(sem["xadd"], 1 + (TB * b + j - 1 if j >= 2 else TB * b))
                        for f in range(FC):
                            i = pe.matmul(ps_t[:, j % 2, :], h[:, f, j * P:(j + 1) * P], wd[:, f, :],
                                          start=f == 0, stop=f == FC - 1)
                        i.then_inc(sem["down"], 1)

                for f in range(FC):
                    chunk(0, f)
                    if f == 2:
                        positions()
                down(0)
                with pe.Fori(1, B) as b:
                    for f in range(FC):
                        chunk(b, f)
                    down(b)


def expert_stage0(nc, c, I, D):
    FR = F0 - 2 * P
    with ExitStack() as ctx:
        pl = Pools(nc, ctx)
        ctx.callback(pl.clear)
        RING = 4
        TILES = E // 2
        ROUNDS = TILES // RING
        assert 2 * CAP == P and TILES % RING == 0
        wg = pl.sb("e0_wg", [P, RING, 2, KH, F0])
        wu = pl.sb("e0_wu", [P, RING, 2, KH, F0])
        wd = pl.sb("e0_wd", [P, RING, 2, 3, H])
        xs = pl.sb("e0_xs", [P, RING, H])
        xsT = pl.sb("e0_xsT", [P, 2, KH, P])
        sg = pl.sb("e0_sg", [P, 2, F0])
        h = pl.sb("e0_h", [P, 2, F0])
        hT = pl.sb("e0_hT", [P, 2, 3, P])
        yo = pl.sb("e0_yo", [P, RING, H])
        ps_x = pl.ps("e0_psx", [P, 512])
        ps_g = pl.ps("e0_psg", [P, 2, 512])
        ps_u = pl.ps("e0_psu", [P, 2, 512])
        ps_h = pl.ps("e0_psh", [P, 512])
        ps_o = pl.ps("e0_pso", [P, 2, 512])
        sem = {n: pl.sem("e0_" + n) for n in ("in0", "in1", "in2", "in3", "tr", "xsT", "g", "u", "sg", "h", "htr",
                                              "hT", "down", "yo", "stored")}
        sem["out"] = pl.sem0("e0_out")
        landed = [sem[f"in{q}"] for q in range(RING)]
        LOADS = 7
        chunks = [(f, P if f < 2 else FR) for f in range(3)]

        pl.start_at_one()
        with nc.Block() as block:

            @block.sync
            def _(sp):
                def fetch(t, q):
                    sp.dma_start(xs[:, q, :], D["xs0"][bass.ds(t * P, P), :]).then_inc(landed[q], 16)
                    for w, name in ((wg, "wg0"), (wu, "wu0")):
                        sp.dma_start(w[:, q, :, :, :].rearrange("p e k f -> p e (k f)"), I[name][bass.ds(t * 2, 2), :, :]
                                     .rearrange("e (p k) f -> p e (k f)", k=KH)).then_inc(landed[q], 16)
                    for z in range(2):
                        sp.dma_start(wd[:, q, z, 0:2, :], I["wd0"][bass.ds(t * 2 + z, 1), 0:2 * P, :]
                                     .rearrange("o (c p) n -> p (o c) n", p=P)).then_inc(landed[q], 16)
                        sp.dma_start(wd[0:FR, q, z, 2, :], I["wd0"][bass.ds(t * 2 + z, 1), 2 * P:F0, :]
                                     .rearrange("o p n -> p (o n)")).then_inc(landed[q], 16)

                for q in range(RING):
                    fetch(q, q)
                with sp.Fori(1, ROUNDS) as i:
                    for q in range(RING):
                        hold(sp, sem["down"], 1 + i * RING + q - RING + 1, c["held"])
                        fetch(i * RING + q, q)

            @block.gpsimd
            def _(pool):
                with pool.Fori(0, ROUNDS) as i:
                    for q in range(RING):
                        t = i * RING + q
                        hold(pool, sem["yo"], 1 + t + 1, c["held"])
                        pool.dma_start(D["y0"][bass.ds(t * P, P), :], yo[:, q, :]).then_inc(sem["out"], 16)
                        hold(pool, sem["out"], 16 * (t + 1), c["held"])
                        pool.sem_inc(sem["stored"], 1)

            @block.scalar
            def _(act):
                def gate(t, q):
                    act.wait_ge(sem["g"], 1 + t + 1)
                    act.wait_ge(sem["h"], 1 + t)
                    act.activation(sg[:, q % 2, :], ps_g[:, q % 2, 0:F0], ACT.Silu).then_inc(sem["sg"], 1)

                def empty(t, q, first=False):
                    act.wait_ge(sem["down"], 1 + t + 1)
                    if not first:
                        act.wait_ge(sem["stored"], 1 + t - RING + 1)
                    act.activation(yo[:, q % RING, :], ps_o[:, q % 2, :], ACT.Copy).then_inc(sem["yo"], 1)

                for t in range(2 * RING):
                    gate(t, t)
                    if t > 0:
                        empty(t - 1, t - 1, first=t - 1 < RING)
                with act.Fori(2, ROUNDS) as i:
                    for q in range(RING):
                        gate(i * RING + q, q)
                        empty(i * RING + q - 1, q + RING - 1)
                empty(TILES - 1, RING - 1)

            @block.vector
            def _(dve):
                def turned_rows(q, t_before):
                    dve.wait_ge(sem["tr"], 1 + t_before + 2)
                    if not (isinstance(t_before, int) and t_before < 1):
                        dve.wait_ge(sem["u"], 1 + t_before)
                    dve.tensor_copy(xsT[:, q % 2, :, :], ps_x[:, :].rearrange("p (k s) -> p k s", s=P))\
                       .then_inc(sem["xsT"], 1)

                def turned_hidden(t, q):
                    dve.wait_ge(sem["htr"], 1 + t + 1)
                    dve.tensor_copy(hT[:, q % 2, 0:2, :], ps_h[:, 0:2 * P].rearrange("p (c s) -> p c s", s=P))
                    dve.tensor_copy(hT[0:FR, q % 2, 2, :], ps_h[0:FR, 2 * P:3 * P]).then_inc(sem["hT"], 1)

                def product(t, q):
                    dve.wait_ge(sem["sg"], 1 + t + 1)
                    dve.wait_ge(sem["u"], 1 + t + 1)
                    dve.tensor_tensor(h[:, q % 2, :], ps_u[:, q % 2, 0:F0], sg[:, q % 2, :], ALU.mult).then_inc(sem["h"], 1)

                def a_round(i, first=False, last=False):
                    for q in range(RING):
                        t = i * RING + q
                        if not (last and q == RING - 1):
                            turned_rows(q + 1, t)
                        if not (first and q == 0):
                            turned_hidden(t - 1, q + RING - 1)
                        product(t, q)

                turned_rows(0, -1)
                a_round(0, first=True)
                with dve.Fori(1, ROUNDS - 1) as i:
                    a_round(i)
                a_round(ROUNDS - 1, last=True)
                turned_hidden(TILES - 1, RING - 1)

            @block.tensor
            def _(pe):
                half = lambda z: slice(z * CAP, (z + 1) * CAP)

                def turn_rows(q, turn):
                    pe.wait_ge(landed[q % RING], 1 + 16 * LOADS * (turn + 1))
                    for k in range(KH):
                        i = pe.transpose(ps_x[:, k * P:(k + 1) * P], xs[:, q % RING, k:H:KH], c["ident"][:, :])
                    i.then_inc(sem["tr"], 1)

                def up(t, q):
                    pe.wait_ge(sem["xsT"], 1 + t + 1)
                    for ps, w, name in ((ps_g, wg, "g"), (ps_u, wu, "u")):
                        for k in range(KH):
                            for z in range(2):
                                i = pe.matmul(ps[half(z), q % 2, 0:F0], xsT[:, q % 2, k, half(z)], w[:, q % RING, z, k, :],
                                              start=k == 0, stop=k == KH - 1, tile_position=(0, z * CAP),
                                              skip_group_check=True)
                        i.then_inc(sem[name], 1)

                def turn_hidden(t, q):
                    pe.wait_ge(sem["h"], 1 + t + 1)
                    for f, m in chunks:
                        i = pe.transpose(ps_h[0:m, f * P:(f + 1) * P], h[:, q % 2, f * P:f * P + m], c["ident"][:, :])
                    i.then_inc(sem["htr"], 1)

                def down(t, q, first=False):
                    pe.wait_ge(sem["hT"], 1 + t + 1)
                    if not first:
                        pe.wait_ge(sem["yo"], 1 + t - 1)
                    for f, m in chunks:
                        for z in range(2):
                            i = pe.matmul(ps_o[half(z), q % 2, :], hT[0:m, q % 2, f, half(z)], wd[0:m, q % RING, z, f, :],
                                          start=f == 0, stop=f == 2, tile_position=(0, z * CAP), skip_group_check=True)
                    i.then_inc(sem["down"], 1)

                def a_round(i, first=False, last=False):
                    for q in range(RING):
                        t = i * RING + q
                        if not (last and q == RING - 1):
                            pe.wait_ge(sem["xsT"], 1 + t + 1)
                            turn_rows(q + 1, i + (q + 1) // RING)
                        if not (first and q == 0):
                            turn_hidden(t - 1, q + RING - 1)
                        up(t, q)
                        if not (first and q == 0):
                            down(t - 1, q + RING - 1, first and q == 1)

                turn_rows(0, 0)
                a_round(0, first=True)
                with pe.Fori(1, ROUNDS - 1) as i:
                    a_round(i)
                a_round(ROUNDS - 1, last=True)
                turn_hidden(TILES - 1, RING - 1)
                down(TILES - 1, RING - 1)


def expert_stage1(nc, c, I, D, ends):
    with ExitStack() as ctx:
        pl = Pools(nc, ctx)
        ctx.callback(pl.clear)
        NW = F1 // P
        RING = 4
        assert NTILE1 % RING == 0 and E % RING == 0
        wgu = pl.sb("e1_wgu", [P, RING, KH, 2 * F1])
        wd = pl.sb("e1_wd", [P, RING, NW, H])
        xs = pl.sb("e1_xs", [P, RING, H])
        xsT = pl.sb("e1_xsT", [P, 2, KH, P])
        sg = pl.sb("e1_sg", [P, 2, F1])
        h = pl.sb("e1_h", [P, 2, F1])
        hT = pl.sb("e1_hT", [P, 2, NW, P])
        yo = pl.sb("e1_yo", [P, RING, H])
        ids = pl.sb("e1_ids", [1, NTILE1], I32)
        ps_x = pl.ps("e1_psx", [P, 2, 512])
        ps_g = pl.ps("e1_psg", [P, 2, 512])
        ps_h = pl.ps("e1_psh", [P, 2, 512])
        ps_o = pl.ps("e1_pso", [P, 2, 512])
        sem = {n: pl.sem("e1_" + n) for n in ("ids", "w0", "w1", "w2", "w3", "ready", "tr", "xsT", "gu", "sg", "h",
                                              "htr", "hT", "down", "yo", "stored")}
        landed = [sem[f"w{s}"] for s in range(RING)]
        rows_in = [pl.sem0(f"e1_rows{q}") for q in range(RING)]
        sem["out"] = pl.sem0("e1_out")
        ROUNDS = NTILE1 // RING

        pl.start_at_one()
        with nc.Block() as block:

            @block.sync
            def _(sp):
                sp.dma_start(ids[0:1, :], D["expert"][0:NTILE1, :].rearrange("n o -> o n")).then_inc(sem["ids"], 16)

                def fetch(e, s):
                    for a, name in ((0, "wg1"), (1, "wu1")):
                        sp.dma_start(wgu[:, s, :, a * F1:(a + 1) * F1], I[name][bass.ds(e, 1), :, :]
                                     .rearrange("o (p k) f -> p (o k) f", k=KH)).then_inc(landed[s], 16)
                    sp.dma_start(wd[:, s, :, :], I["wd1"][bass.ds(e, 1), :, :]
                                 .rearrange("o (p c) n -> p (o c) n", c=NW)).then_inc(landed[s], 16)

                def announce(s, turn):
                    hold(sp, landed[s], 1 + 48 * (turn + 1), c["held"])
                    sp.sem_inc(sem["ready"], 1)

                def refill(e, q):
                    last = sp.value_load(ends[0:1, bass.ds(e, 1)], min_val=0, max_val=NTILE1)
                    hold(sp, sem["down"], 1 + last, c["held"])
                    fetch(e + RING - 1, (q + RING - 1) % RING)

                for e in range(RING - 1):
                    fetch(e, e)
                with sp.Fori(0, E // RING - 1) as i:
                    for q in range(RING):
                        announce(q, i)
                        refill(i * RING + q, q)
                for q in range(RING):
                    announce(q, E // RING - 1)
                    if q == 0:
                        refill(E - RING, 0)

            @block.gpsimd
            def _(pool):
                def load(t, q):
                    pool.dma_start(xs[:, q, :], D["xs1"][bass.ds(t * P, P), :]).then_inc(rows_in[q], 16)

                def store(t, q):
                    hold(pool, sem["yo"], 1 + t + 1, c["held"])
                    pool.dma_start(D["y1"][bass.ds(t * P, P), :], yo[:, q, :]).then_inc(sem["out"], 16)

                def tell(t):
                    hold(pool, sem["out"], 16 * (t + 1), c["held"])
                    pool.sem_inc(sem["stored"], 1)

                for q in range(RING):
                    load(q, q)
                with pool.Fori(0, ROUNDS - 1) as i:
                    for q in range(RING):
                        t = i * RING + q
                        hold(pool, sem["tr"], 1 + t + 1, c["held"])
                        load(t + RING, q)
                        store(t, q)
                        tell(t)
                for q in range(RING):
                    t = NTILE1 - RING + q
                    store(t, q)
                    tell(t)

            @block.scalar
            def _(act):
                def gate(t, q):
                    act.wait_ge(sem["gu"], 1 + t + 1)
                    act.wait_ge(sem["h"], 1 + t)
                    act.activation(sg[:, q % 2, :], ps_g[:, q % 2, 0:F1], ACT.Silu).then_inc(sem["sg"], 1)

                def empty(t, q, first=False):
                    act.wait_ge(sem["down"], 1 + t + 1)
                    if not first:
                        act.wait_ge(sem["stored"], 1 + t - RING + 1)
                    act.activation(yo[:, q % RING, :], ps_o[:, q % 2, :], ACT.Copy).then_inc(sem["yo"], 1)

                for t in range(RING):
                    gate(t, t)
                    if t > 0:
                        empty(t - 1, t - 1, first=True)
                gate(RING, 0)
                empty(RING - 1, RING - 1, first=True)
                for q in range(1, RING):
                    gate(RING + q, q)
                    empty(RING + q - 1, q - 1)
                with act.Fori(2, ROUNDS) as i:
                    for q in range(RING):
                        gate(i * RING + q, q)
                        empty(i * RING + q - 1, q + RING - 1)
                empty(NTILE1 - 1, RING - 1)

            @block.vector
            def _(dve):
                def turned_rows(t, q):
                    dve.wait_ge(sem["tr"], 1 + t + 1)
                    dve.wait_ge(sem["gu"], 1 + t - 1)
                    dve.tensor_copy(xsT[:, q % 2, :, :], ps_x[:, q % 2, :].rearrange("p (k s) -> p k s", s=P))\
                       .then_inc(sem["xsT"], 1)

                def turned_hidden(t, q):
                    dve.wait_ge(sem["htr"], 1 + t + 1)
                    dve.tensor_copy(hT[:, q % 2, :, :], ps_h[:, q % 2, 0:NW * P].rearrange("p (c s) -> p c s", s=P))\
                       .then_inc(sem["hT"], 1)

                def product(t, q):
                    dve.wait_ge(sem["sg"], 1 + t + 1)
                    dve.tensor_tensor(h[:, q % 2, :], ps_g[:, q % 2, F1:], sg[:, q % 2, :], ALU.mult).then_inc(sem["h"], 1)

                def a_round(i, first=False, last=False):
                    for q in range(RING):
                        t = i * RING + q
                        if not (last and q == RING - 1):
                            turned_rows(t + 1, q + 1)
                        if not (first and q == 0):
                            turned_hidden(t - 1, q + RING - 1)
                        product(t, q)

                dve.wait_ge(sem["tr"], 1 + 1)
                dve.tensor_copy(xsT[:, 0, :, :], ps_x[:, 0, :].rearrange("p (k s) -> p k s", s=P)).then_inc(sem["xsT"], 1)
                a_round(0, first=True)
                with dve.Fori(1, ROUNDS - 1) as i:
                    a_round(i)
                a_round(ROUNDS - 1, last=True)
                turned_hidden(NTILE1 - 1, RING - 1)

            @block.tensor
            def _(pe):
                def turn_rows(q, landed_count):
                    pe.wait_ge(rows_in[q % RING], landed_count)
                    for k in range(KH):
                        j = pe.transpose(ps_x[:, q % 2, k * P:(k + 1) * P], xs[:, q % RING, k:H:KH], c["ident"][:, :])
                    j.then_inc(sem["tr"], 1)

                def up(t, q):
                    e = pe.value_load(ids[0:1, bass.ds(t, 1)], min_val=0, max_val=E - 1)
                    hold(pe, sem["ready"], 1 + e + 1, c["held"])
                    pe.wait_ge(sem["xsT"], 1 + t + 1)
                    for k in range(KH):
                        j = pe.matmul(ps_g[:, q % 2, :], xsT[:, q % 2, k, :], wgu[:, bass.ds(e % RING, 1), k, :],
                                      start=k == 0, stop=k == KH - 1)
                    j.then_inc(sem["gu"], 1)

                def turn_hidden(t, q):
                    pe.wait_ge(sem["h"], 1 + t + 1)
                    for a in range(NW):
                        j = pe.transpose(ps_h[:, q % 2, a * P:(a + 1) * P], h[:, q % 2, a:F1:NW], c["ident"][:, :])
                    j.then_inc(sem["htr"], 1)

                def down(t, q, first=False):
                    e = pe.value_load(ids[0:1, bass.ds(t, 1)], min_val=0, max_val=E - 1)
                    pe.wait_ge(sem["hT"], 1 + t + 1)
                    if not first:
                        pe.wait_ge(sem["yo"], 1 + t - 1)
                    for a in range(NW):
                        j = pe.matmul(ps_o[:, q % 2, :], hT[:, q % 2, a, :], wd[:, bass.ds(e % RING, 1), a, :],
                                      start=a == 0, stop=a == NW - 1)
                    j.then_inc(sem["down"], 1)

                def a_round(i, first=False, last=False):
                    for q in range(RING):
                        t = i * RING + q
                        if not (last and q == RING - 1):
                            pe.wait_ge(sem["xsT"], 1 + t)
                            turn_rows(q + 1, 16 * (i + 1 + (q + 1) // RING))
                        if not (first and q == 0):
                            turn_hidden(t - 1, q + RING - 1)
                        up(t, q)
                        if not (first and q == 0):
                            down(t - 1, q + RING - 1, first and q == 1)

                pe.wait_ge(sem["ids"], 1 + 16)
                turn_rows(0, 16)
                a_round(0, first=True)
                with pe.Fori(1, ROUNDS - 1) as i:
                    a_round(i)
                a_round(ROUNDS - 1, last=True)
                turn_hidden(NTILE1 - 1, RING - 1)
                down(NTILE1 - 1, RING - 1)


def combine_stage(nc, c, I, D, x, L, route, out=None):
    K = K0 if L == 0 else K1
    NB = 8
    y = D["y0"] if L == 0 else D["y1"]
    per = NB // K
    with ExitStack() as ctx:
        pl = Pools(nc, ctx)
        ctx.callback(pl.clear)
        rows = pl.sb(f"c{L}_rows", [P, NB, H])
        got = [pl.sem0(f"c{L}_got{i}") for i in range(NB)]
        used = pl.sem(f"c{L}_used")
        stored = pl.sem(f"c{L}_stored")
        pl.start_at_one()
        with nc.Block() as block:

            @block.sync
            def _(sp):
                if out is not None:
                    with sp.Fori(0, NT) as t:
                        hold(sp, used, 1 + K * (t + 1), c["held"])
                        sp.dma_start(out[bass.ds(t * P, P), :], x[:, bass.ds(t, 1), :].rearrange("p a h -> p (a h)"))\
                          .then_inc(stored, 16)
                    sp.wait_ge(stored, 1 + 16 * NT)

            @block.gpsimd
            def _(pool):
                for t in range(NT):
                    for k in range(K):
                        n = t * K + k
                        if n >= NB:
                            pool.wait_ge(used, 1 + n - NB + 1)
                        pool.indirect_dma_start(rows[:, n % NB, :], None, y[:, :],
                                                bass.IndirectOffsetOnAxis(route["gath"][:, t, k:k + 1], 0))\
                            .then_inc(got[n % NB], 16)

            @block.vector
            def _(dve):
                with dve.Fori(0, NT // per) as r:
                    for n in range(NB):
                        t, k = n // K, n % K
                        dve.wait_ge(got[n], 16 * (r + 1))
                        dve.wait_ge(used, 1 + r * NB + n)
                        xt = x[:, r * per + t, :]
                        dve.scalar_tensor_tensor(out=xt, in0=rows[:, n, :],
                                                 scalar=route["wsel"][:, bass.ds(r * per + t, 1), k],
                                                 in1=xt, op0=ALU.mult, op1=ALU.add).then_inc(used, 1)


def attention_stage(nc, c, I, D, x):
    ND = HG * DCA
    NI = 2 * TB + 1
    KI, DI, QI = 0, TB, TB + 1
    NG_STEPS = TB * HG
    N = NG * NG_STEPS
    SB, PB = 4, 4
    BT, BO = 4, 6
    LAG = 3
    T_KT, T_DKT, T_V, T_DV, T_QT = NI, NI + NG, NI + NG + 1, NI + NG + 1 + TB, NI + NG + 2 + TB
    TAKEN = T_QT + NG
    with ExitStack() as ctx:
        pl = Pools(nc, ctx)
        ctx.callback(pl.clear)
        sb = lambda n, shape, dt=F32: pl.sb("a_" + n, shape, dt)
        wq = sb("wq", [P, KH, H])
        wkv = sb("wkv", [P, KC, 2, H])
        wkvd = sb("wkvd", [P, KC, 2, H])
        wo = sb("wo", [P, KH, H])
        bq = sb("bq", [P, H])
        bkv = sb("bkv", [P, 2, H])
        bkvd = sb("bkvd", [P, 2, H])
        bo = sb("bo", [P, H])
        hw = sb("hw", [P, 6])
        xnb = sb("xnb", [P, TB, H])
        xnT = sb("xnT", [P, KH, S])
        ctxT = sb("ctxT", [P, KC, S])
        ctxd = sb("ctxd", [P, KC, P // DCA, DCA])
        mask_r = sb("mask_r", [ND, HG, HD])
        mask_c = sb("mask_c", [P, HG, DCA])
        st = sb("st", [P, NT, 6])
        mv = sb("mv", [P, NT, 2])
        ve = sb("ve", [P, NT])
        rs = sb("rs", [P, NT])
        hd = sb("hd", [P, NI, NH, HD])
        hsq = sb("hsq", [P, 2, NH, HD])
        mu = sb("mu", [P, NI, NH])
        hv = sb("hv", [P, NI, NH])
        v = sb("v", [P, TB, H])
        dv = sb("dv", [ND, NG, HG, HD])
        qT = sb("qT", [P, NG, S])
        kT = sb("kT", [P, NG, S])
        kd = sb("kd", [P, NG, HG, DCA])
        sd = sb("sd", [P, TB, NG, ND])
        md = sb("md", [P, TB * NH])
        pdT = sb("pdT", [ND, NG, S])
        p = sb("p", [P, PB, S])
        pt = sb("pt", [P, 2, TB, P])
        nm = sb("nm", [P, N])
        sm = sb("sm", [P, N])
        rm = sb("rm", [P, N])
        oT = sb("oT", [P, NG, S])
        ps = pl.ps("a_ps", [P, 8, 512])
        sem = {n: pl.sem("a_" + n) for n in (
            "win", "ctx", "ctxd", "const", "stats", "ve", "rs", "xnb", "xtr", "xnT", "item", "chain", "cent", "sq",
            "var", "sqrt", "hn", "val", "ktr", "qtr", "taken", "sd", "sdc", "pdexp", "pd", "pdT", "pdTc",
            "zfill", "s", "max", "exp", "inv", "prob", "ptr", "pt", "pv", "oT", "bias", "om", "xadd")}
        n_in = 8 + HG
        f3 = "p a b -> p (a b)"

        pl.start_at_one()
        with nc.Block() as block:

            @block.sync
            def _(sp):
                sp.dma_start(wq[:, :, :], I["wq"].rearrange("(k p) n -> p k n", p=P)).then_inc(sem["win"], 16)
                sp.dma_start(wo[:, :, :], I["wo"].rearrange("(k p) n -> p k n", p=P)).then_inc(sem["win"], 16)
                for dst, name in ((wkv, "wkv"), (wkvd, "wkvd")):
                    sp.dma_start(dst[:, :, :, :].rearrange("p k z n -> p k (z n)"),
                                 I[name].rearrange("(k p) n -> p k n", p=P)).then_inc(sem["win"], 16)
                for dst, name in ((bq[:, :], "bq"), (bkv[:, :, :].rearrange(f3), "bkv"),
                                  (bkvd[:, :, :].rearrange(f3), "bkvd"), (bo[:, :], "bo")):
                    sp.dma_start(dst, I[name].to_broadcast([P, I[name].shape[1]])).then_inc(sem["win"], 16)
                for i in range(HG):
                    sp.dma_start(hw[i * HD:(i + 1) * HD, :], I["headnorm"]).then_inc(sem["win"], 16)
                zero_rows = 2 * P
                assert NSLOT1 % (B * zero_rows) == 0
                with sp.Fori(0, B) as b:
                    hold(sp, sem["val"], 1 + (TB + 1) * b, c["held"])
                    sp.dma_start(ctxT[:, :, :], I["ctxT"][:, bass.ds(b * S, S)].rearrange("(k p) n -> p k n", p=P))\
                      .then_inc(sem["ctx"], 16)
                    with sp.Fori(0, NSLOT1 // (B * zero_rows)) as i:
                        sp.dma_start(D["xs1"][bass.ds((b * (NSLOT1 // (B * zero_rows)) + i) * zero_rows, zero_rows), :]
                                     .rearrange("(p a) (c z) -> p (a c) z", a=2, z=P),
                                     bc(c["zeros"][:, :], 1, 2 * H // P)).then_inc(sem["zfill"], 16)
                sp.wait_ge(sem["zfill"], 1 + 16 * (NSLOT1 // zero_rows))

            @block.gpsimd
            def _(pool):
                pool.memset(mask_r[:, :, :], 1.0).then_inc(sem["const"], 1)
                pool.memset(mask_c[:, :, :], 1.0).then_inc(sem["const"], 1)
                pool.memset(p[:, :, :], 0.0).then_inc(sem["const"], 1)
                pool.wait_ge(sem["const"], 1 + 3)
                n = 3
                for m, width, rows in ((mask_r, HD, DCA), (mask_c, DCA, HD)):
                    pool.affine_select(out=m[:, :, :], in_=m[:, :, :], compare_op=ALU.is_ge, fill=0.0, base=0,
                                       pattern=[[-rows, HG], [0, width]], channel_multiplier=1).then_inc(sem["const"], 1)
                    n += 1
                    pool.wait_ge(sem["const"], 1 + n)
                    pool.affine_select(out=m[:, :, :], in_=m[:, :, :], compare_op=ALU.is_ge, fill=0.0, base=rows - 1,
                                       pattern=[[rows, HG], [0, width]], channel_multiplier=-1).then_inc(sem["const"], 1)
                    n += 1
                pool.wait_ge(sem["ve"], 1 + 1)
                pool.tensor_tensor(rs[:, :], ve[:, :], c["minus_half"][:, 0:NT], ALU.pow).then_inc(sem["rs"], 1)
                with pool.Fori(0, B) as b:
                    pool.wait_ge(sem["ctx"], 1 + 16 * (b + 1))
                    pool.sem_inc(c["held"], 1)
                    for i in range(P // DCA):
                        j = pool.tensor_copy(ctxd[:, :, i, :], ctxT[:, :, S2:])
                    j.then_inc(sem["ctxd"], 1)
                    pool.wait_ge(sem["xnb"], 1 + b + 1)
                    xb = x[:, bass.ds(b * TB, TB), :]
                    pool.tensor_tensor(xb, xb, bc(bo[:, :], 1, TB), ALU.add).then_inc(sem["bias"], 1)

            @block.scalar
            def _(act):
                act.wait_ge(sem["const"], 1 + 7)
                with act.Fori(0, B) as b:

                    def turn_x():
                        for k in range(KH):
                            act.wait_ge(sem["xtr"], 1 + KH * b + k + 1)
                            act.wait_ge(sem["om"], 1 + TB * b)
                            act.activation(xnT[:, k, :], ps[:, 5 + k % 3, :], ACT.Copy).then_inc(sem["xnT"], 1)

                    for i in range(NI + 1):
                        if i < NI:
                            act.wait_ge(sem["cent"], 1 + NI * b + i + 1)
                            act.activation(hsq[:, i % 2, :, :], hd[:, i, :, :], ACT.Square).then_inc(sem["sq"], 1)
                        if i >= 1:
                            act.wait_ge(sem["var"], 1 + NI * b + i)
                            act.activation(hv[:, i - 1, :], hv[:, i - 1, :], ACT.Sqrt).then_inc(sem["sqrt"], 1)
                        if i == 1:
                            turn_x()
                    act.wait_ge(sem["sdc"], 1 + b + 1)
                    act.activation(sd[:, :, :, :], sd[:, :, :, :], ACT.Exp).then_inc(sem["pdexp"], 1)

                    def exponentials(n):
                        act.wait_ge(sem["max"], 1 + N * b + n + 1)
                        act.activation(p[:, n % PB, 0:S2], ps[:, n % SB, 0:S2], ACT.Exp, bias=nm[:, n:n + 1],
                                       accum_out=sm[:, n:n + 1]).then_inc(sem["exp"], 1)

                    def turned(n):
                        act.wait_ge(sem["ptr"], 1 + N * b + n + 1)
                        if n >= 2:
                            act.wait_ge(sem["pv"], 1 + N * b + n - 1)
                        act.activation(pt[:, n % 2, :, :], ps[:, BT + n % 2, :].rearrange("p (j s) -> p j s", s=P),
                                       ACT.Copy).then_inc(sem["pt"], 1)

                    exponentials(0)
                    for g in range(NG):
                        act.wait_ge(sem["pdT"], 1 + NG * b + g + 1)
                        act.activation(pdT[:, g, :], ps[0:ND, BT + g % 2, :], ACT.Copy).then_inc(sem["pdTc"], 1)
                    for n in range(1, N + LAG):
                        if n >= LAG:
                            turned(n - LAG)
                        if n < N:
                            exponentials(n)

            @block.vector
            def _(dve):
                done = [0, 0]

                def step(ins, wait=True):
                    ins.then_inc(sem["chain"], 1)
                    done[1] += 1
                    if wait:
                        dve.wait_ge(sem["chain"], 1 + done[0] + done[1])

                dve.wait_ge(sem["win"], 1 + 16 * n_in)
                dve.tensor_scalar(hw[:, 0:2], hw[:, 0:2], SCALE, None, ALU.mult).then_inc(sem["hn"], 1)
                dve.wait_ge(sem["hn"], 1 + 1)
                for j in range(NT):
                    dve.bn_stats(st[:, j, :], x[:, j, :]).then_inc(sem["stats"], 1)
                dve.wait_ge(sem["stats"], 1 + NT)
                for j in range(NT):
                    dve.bn_aggr(mv[:, j, :], st[:, j, :]).then_inc(sem["stats"], 1)
                dve.wait_ge(sem["stats"], 1 + 2 * NT)
                dve.tensor_scalar(ve[:, :], mv[:, :, 1], LN_EPS, None, ALU.add).then_inc(sem["ve"], 1)
                dve.wait_ge(sem["rs"], 1 + 1)
                CHAIN = 64
                with dve.Fori(0, B) as b:
                    done[0], done[1] = b * CHAIN, 0
                    for j in range(TB):
                        t = b * TB + j
                        i = dve.tensor_scalar(xnb[:, j, :], x[:, t, :], mv[:, bass.ds(t, 1), 0], rs[:, bass.ds(t, 1)],
                                              ALU.subtract, ALU.mult)
                    i.then_inc(sem["xnb"], 1)

                    bank = [0, 1, 2, 3, 4, 0, 1, 2, 3]
                    biases = [bkv[:, 0, :]] * TB + [bkvd[:, 0, :]] + [bq[:, :]] * TB

                    def centre(i):
                        dve.wait_ge(sem["item"], 1 + NI * b + i + 1)
                        dve.tensor_tensor(hd[:, i, :, :].rearrange(f3), ps[:, bank[i], :], biases[i], ALU.add)\
                           .then_inc(sem["taken"], 1)
                        dve.wait_ge(sem["taken"], 1 + TAKEN * b + i + 1)
                        step(dve.tensor_reduce(mu[:, i, :], hd[:, i, :, :], AX_X, ALU.add))
                        step(dve.tensor_scalar(mu[:, i, :], mu[:, i, :], 1.0 / HD, None, ALU.mult))
                        dve.tensor_tensor(hd[:, i, :, :], hd[:, i, :, :], bc(mu[:, i, :], 2, HD), ALU.subtract)\
                           .then_inc(sem["cent"], 1)

                    def variance(i):
                        dve.wait_ge(sem["sq"], 1 + NI * b + i + 1)
                        step(dve.tensor_reduce(hv[:, i, :], hsq[:, i % 2, :, :], AX_X, ALU.add))
                        dve.tensor_scalar(hv[:, i, :], hv[:, i, :], 1.0 / HD, HEAD_EPS, ALU.mult, ALU.add)\
                           .then_inc(sem["var"], 1)

                    def scale(i):
                        dve.wait_ge(sem["sqrt"], 1 + NI * b + i + 1)
                        step(dve.reciprocal(mu[:, i, :], hv[:, i, :]))
                        dve.tensor_tensor(hd[:, i, :, :], hd[:, i, :, :], bc(mu[:, i, :], 2, HD), ALU.mult)\
                           .then_inc(sem["hn"], 1)

                    for i in range(NI + 2):
                        if i < NI:
                            centre(i)
                        if 1 <= i < NI + 1:
                            variance(i - 1)
                        if i >= 2:
                            scale(i - 2)
                    for g in range(NG):
                        dve.wait_ge(sem["ktr"], 1 + (NG + 1) * b + g + 1)
                        dve.tensor_scalar(kT[:, g, 0:S2], ps[:, g, 0:S2], hw[:, 2:3], hw[:, 3:4], ALU.mult, ALU.add)\
                           .then_inc(sem["taken"], 1)
                    dve.wait_ge(sem["ktr"], 1 + (NG + 1) * (b + 1))
                    step(dve.tensor_scalar(kd[:, :, :, :].rearrange("p g h s -> p (g h s)"), ps[:, 4, 0:NG * ND],
                                           hw[:, 4:5], hw[:, 5:6], ALU.mult, ALU.add))
                    dve.tensor_tensor(kd[:, :, :, :], kd[:, :, :, :], bc(mask_c[:, :, :], 1, NG), ALU.mult)\
                       .then_inc(sem["taken"], 1)
                    for j in range(TB):
                        dve.wait_ge(sem["val"], 1 + (TB + 1) * b + j + 1)
                        dve.tensor_tensor(v[:, j, :], ps[:, (5, 6, 7, 0)[j], :], bkv[:, 1, :], ALU.add)\
                           .then_inc(sem["taken"], 1)
                    dve.wait_ge(sem["val"], 1 + (TB + 1) * (b + 1))
                    step(dve.tensor_tensor(dv[:, :, :, :].rearrange("p g h d -> p (g h d)"), ps[0:ND, 1, :],
                                           bkvd[0:ND, 1, :], ALU.add))
                    dve.tensor_tensor(dv[:, :, :, :], dv[:, :, :, :], bc(mask_r[:, :, :], 1, NG), ALU.mult)\
                       .then_inc(sem["taken"], 1)
                    for g in range(NG):
                        dve.wait_ge(sem["qtr"], 1 + NG * b + g + 1)
                        dve.tensor_scalar(qT[:, g, :], ps[:, 2 + g, :], hw[:, 0:1], hw[:, 1:2], ALU.mult, ALU.add)\
                           .then_inc(sem["taken"], 1)
                    sdf = sd[:, :, :, :].rearrange("p j g (h s) -> p (j g h) s", s=DCA)
                    sdp = ps[:, BO:BO + 2, :].rearrange("p a (r s) -> p (a r) s", s=DCA)
                    dve.wait_ge(sem["sd"], 1 + b + 1)
                    step(dve.tensor_reduce(md[:, :], sdp, AX_X, ALU.max))
                    dve.tensor_tensor(sdf, sdp, bc(md[:, :], 2, DCA), ALU.subtract).then_inc(sem["sdc"], 1)

                    def maximum(n):
                        dve.wait_ge(sem["s"], 1 + N * b + n + 1)
                        dve.tensor_reduce(nm[:, n:n + 1], ps[:, n % SB, 0:S2], AX_X, ALU.max, negate=True)\
                           .then_inc(sem["max"], 1)

                    def invert(n):
                        dve.wait_ge(sem["exp"], 1 + N * b + n + 1)
                        dve.reciprocal(rm[:, n:n + 1], sm[:, n:n + 1]).then_inc(sem["inv"], 1)

                    def normalise(n):
                        dve.wait_ge(sem["inv"], 1 + N * b + n + 1)
                        dve.tensor_scalar(p[:, n % PB, 0:S2], p[:, n % PB, 0:S2], rm[:, n:n + 1], None, ALU.mult)\
                           .then_inc(sem["prob"], 1)

                    maximum(0)
                    dve.wait_ge(sem["pdexp"], 1 + b + 1)
                    step(dve.tensor_reduce(md[:, :], sdf, AX_X, ALU.add))
                    step(dve.reciprocal(md[:, :], md[:, :]))
                    dve.tensor_tensor(sdf, sdf, bc(md[:, :], 2, DCA), ALU.mult).then_inc(sem["pd"], 1)
                    for n in range(1, N + LAG + 2):
                        if n <= N:
                            invert(n - 1)
                        if n < N:
                            maximum(n)
                        if n <= N:
                            normalise(n - 1)
                        if n > LAG + 1 and (n - LAG - 1) % NG_STEPS == 0:
                            g = (n - LAG - 1) // NG_STEPS - 1
                            dve.wait_ge(sem["pv"], 1 + N * b + (g + 1) * NG_STEPS)
                            dve.tensor_copy(oT[:, g, :], ps[:, BO + g % 2, :]).then_inc(sem["oT"], 1)
                    assert done[1] <= CHAIN
                    dve.sem_inc(sem["chain"], CHAIN - done[1])
                    dve.wait_ge(sem["bias"], 1 + b + 1)
                    for j in range(TB):
                        dve.wait_ge(sem["om"], 1 + TB * b + j + 1)
                        xt = x[:, b * TB + j, :]
                        dve.tensor_tensor(xt, ps[:, 4 + j, :], xt, ALU.add).then_inc(sem["xadd"], 1)

            @block.tensor
            def _(pe):
                pe.wait_ge(sem["win"], 1 + 16 * n_in)
                ident = c["ident"]
                with pe.Fori(0, B) as b:

                    def taken(n):
                        pe.wait_ge(sem["taken"], 1 + TAKEN * b + n + 1)

                    def project(bank, src, w, signal):
                        for k in range(len(w)):
                            i = pe.matmul(ps[:, bank, :], src[k], w[k], start=k == 0, stop=k == len(w) - 1)
                        i.then_inc(sem[signal], 1)

                    pe.wait_ge(sem["ctx"], 1 + 16 * (b + 1))
                    pe.wait_ge(sem["exp"], 1 + N * b)
                    tok = lambda j: [ctxT[:, k, j * P:(j + 1) * P] for k in range(KC)]
                    dtok = [ctxd[:, k, :, :].rearrange("p h s -> p (h s)") for k in range(KC)]
                    for j in range(TB):
                        project(j, tok(j), [wkv[:, k, 0, :] for k in range(KC)], "item")
                    pe.wait_ge(sem["ctxd"], 1 + b + 1)
                    pe.wait_ge(sem["xadd"], 1 + TB * b)
                    project(4, dtok, [wkvd[:, k, 0, :] for k in range(KC)], "item")
                    pe.wait_ge(sem["xnb"], 1 + b + 1)
                    for k in range(KH):
                        if k == 3:
                            pe.wait_ge(sem["xnT"], 1 + KH * b + 1)
                        for j in range(TB):
                            i = pe.transpose(ps[:, 5 + k % 3, j * P:(j + 1) * P], xnb[:, j, k * P:(k + 1) * P], ident[:, :])
                        i.then_inc(sem["xtr"], 1)
                    pe.wait_ge(sem["xnT"], 1 + KH * (b + 1))
                    for j in range(TB):
                        taken(j)
                        project(j, [xnT[:, k, j * P:(j + 1) * P] for k in range(KH)], [wq[:, k, :] for k in range(KH)], "item")
                    pe.wait_ge(sem["hn"], 1 + NI * b + 1 + DI)
                    for g in range(NG):
                        taken(QI + g)
                        for j in range(TB):
                            i = pe.transpose(ps[:, g, j * P:(j + 1) * P],
                                             hd[:, KI + j, g * HG:(g + 1) * HG, :].rearrange(f3), ident[:, :])
                        i.then_inc(sem["ktr"], 1)
                    hold(pe, sem["hn"], 1 + NI * b + 1 + QI, c["held"])
                    for g in range(NG):
                        i = pe.transpose(ps[:, 4, g * ND:(g + 1) * ND],
                                         hd[0:ND, DI, g * HG:(g + 1) * HG, :].rearrange(f3), ident[0:ND, 0:ND])
                    i.then_inc(sem["ktr"], 1)
                    for j in range(TB):
                        if j == 3:
                            taken(T_KT)
                        project((5, 6, 7, 0)[j], tok(j), [wkv[:, k, 1, :] for k in range(KC)], "val")
                    taken(T_KT + 1)
                    project(1, dtok, [wkvd[:, k, 1, :] for k in range(KC)], "val")
                    pe.wait_ge(sem["hn"], 1 + NI * b + 1 + NI)
                    for g in range(NG):
                        taken((T_KT + 2, T_KT + 3, T_DKT, T_V)[g])
                        for j in range(TB):
                            i = pe.transpose(ps[:, 2 + g, j * P:(j + 1) * P],
                                             hd[:, QI + j, g * HG:(g + 1) * HG, :].rearrange(f3), ident[:, :])
                        i.then_inc(sem["qtr"], 1)
                    taken(T_QT + 3)
                    for j in range(TB):
                        for g in range(NG):
                            a = (j % 2 * NG + g) * ND
                            i = pe.matmul(ps[:, BO + j // 2, a:a + ND], qT[:, g, j * P:(j + 1) * P],
                                          kd[:, g, :, :].rearrange("p h s -> p (h s)"), start=True, stop=True)
                    i.then_inc(sem["sd"], 1)

                    def where(n):
                        return n // NG_STEPS, n // HG % TB, n % HG

                    def scores(n):
                        g, j, hh = where(n)
                        if n >= SB:
                            pe.wait_ge(sem["exp"], 1 + N * b + n - SB + 1)
                        strip = slice(hh * HD, (hh + 1) * HD)
                        pe.matmul(ps[:, n % SB, 0:S2], qT[strip, g, j * P:(j + 1) * P], kT[strip, g, 0:S2],
                                  start=True, stop=True).then_inc(sem["s"], 1)

                    def turn(n):
                        pe.wait_ge(sem["prob"], 1 + N * b + n + 1)
                        if n >= 2:
                            pe.wait_ge(sem["pt"], 1 + N * b + n - 1)
                        for a in range(TB):
                            i = pe.transpose(ps[:, BT + n % 2, a * P:(a + 1) * P], p[:, n % PB, a * P:(a + 1) * P], ident[:, :])
                        i.then_inc(sem["ptr"], 1)

                    def dca(g):
                        if g >= 2:
                            pe.wait_ge(sem["oT"], 1 + NG * b + g - 1)
                        pe.matmul(ps[:, BO + g % 2, :], dv[:, g, :, :].rearrange(f3), pdT[:, g, :],
                                  start=True, stop=False, skip_group_check=True)

                    def weigh(n):
                        g, j, hh = where(n)
                        if n % NG_STEPS == 0:
                            dca(g)
                        pe.wait_ge(sem["pt"], 1 + N * b + n + 1)
                        for a in range(TB):
                            col = (g * HG + hh) * HD
                            i = pe.matmul(ps[hh * HD:(hh + 1) * HD, BO + g % 2, j * P:(j + 1) * P], v[:, a, col:col + HD],
                                          pt[:, n % 2, a, :], start=False, stop=a == TB - 1, skip_group_check=True,
                                          tile_position=(0, hh * HD))
                        i.then_inc(sem["pv"], 1)

                    for n in range(LAG):
                        scores(n)
                    for g in range(NG):
                        if g >= 2:
                            hold(pe, sem["pdTc"], 1 + NG * b + g - 1, c["held"])
                        else:
                            hold(pe, sem["pd"], 1 + b + 1, c["held"])
                        for j in range(TB):
                            i = pe.transpose(ps[0:ND, BT + g % 2, j * P:(j + 1) * P], sd[:, j, g, :], ident[:, :])
                        i.then_inc(sem["pdT"], 1)
                    pe.wait_ge(sem["pdTc"], 1 + NG * (b + 1))
                    for n in range(LAG, N + LAG + 1):
                        if n < N:
                            scores(n)
                        if n - LAG < N:
                            turn(n - LAG)
                        if n > LAG:
                            weigh(n - LAG - 1)
                    pe.wait_ge(sem["pt"], 1 + N * (b + 1))
                    for j in range(TB):
                        if j == 0:
                            pe.wait_ge(sem["oT"], 1 + NG * (b + 1))
                        project(4 + j, [oT[:, g, j * P:(j + 1) * P] for g in range(NG)], [wo[:, g, :] for g in range(NG)], "om")


def program(nc, I, out, upto=9):
    with ExitStack() as ctx:
        pl = Pools(nc, ctx)
        D = {"bc": nc.dram_tensor("bc_rows", (B * 2 * NST, S), F32).ap(),
             "xs0": nc.dram_tensor("slots_in0", (NSLOT0, H), F32).ap(),
             "xs1": nc.dram_tensor("slots_in1", (NSLOT1, H), F32).ap(),
             "y0": nc.dram_tensor("slots_out0", (NSLOT0, H), F32).ap(),
             "y1": nc.dram_tensor("slots_out1", (NSLOT1, H), F32).ap(),
             "expert": nc.dram_tensor("tile_expert", (2 * P, 1), I32).ap()}
        c = {}
        x = pl.sb("x_resid", [P, NT, H])
        constants(nc, pl, c)
        mamba_stage(nc, pl, c, I, D, x)
        def routes(L, K):
            return {"scat": pl.sb(f"scat{L}", [P, NT, K], I32), "gath": pl.sb(f"gath{L}", [P, NT, K], I32),
                    "wsel": pl.sb(f"wsel{L}", [P, NT, K])}

        if upto >= 2:
            route0 = routes(0, K0)
            route_stage(nc, c, I, D, x, 0, route0)
        if upto >= 3:
            expert_stage0(nc, c, I, D)
            combine_stage(nc, c, I, D, x, 0, route0)
        if upto >= 4:
            attention_stage(nc, c, I, D, x)
        if upto >= 5:
            route1 = routes(1, K1)
            route1["ends"] = pl.sb("ends", [1, 1 + E], I32)
            route_stage(nc, c, I, D, x, 1, route1)
        if upto >= 6:
            expert_stage1(nc, c, I, D, route1["ends"])
            combine_stage(nc, c, I, D, x, 1, route1, out)
            return
        stored = pl.sem("stored")
        with nc.Block() as block:

            @block.sync
            def _(sp):
                sp.dma_start(out.rearrange("(t p) h -> p t h", p=P), x[:, :, :]).then_inc(stored, 16)
                sp.wait_ge(stored, 16)


def layouts(a):
    f = np.ascontiguousarray
    col = lambda v: f(v.reshape(TB, P).T)
    i = {"x": f(a["x"].reshape(T, H)), "ctxT": f(a["ctx_1024"].reshape(T, DM).T),
         "in_projT": f(a["L0_xattn_in_proj_w"].T), "x_projT": f(a["L0_xattn_x_proj_w"].T),
         "dt_projT": f(a["L0_xattn_dt_proj_w"].T), "conv_w": f(a["L0_xattn_conv_w"].reshape(H, CONV)),
         "conv_b": col(a["L0_xattn_conv_b"]), "dt_b": col(a["L0_xattn_dt_proj_b"]), "d_col": col(a["L0_xattn_D"]),
         "a_log": f(a["L0_xattn_A_log"].reshape(TB, P, NST).transpose(1, 2, 0).reshape(P, NST * TB))}
    i["wr0"] = f(np.concatenate([a["L0_ffn_Wr"], a["L0_ffn_Wse"]], 1))
    i["wsg0"], i["wsu0"], i["wsd0"] = (f(a["L0_ffn_" + n]) for n in ("Wsg", "Wsu", "Wsd"))
    i["wg0"], i["wu0"], i["wd0"] = (f(a["L0_ffn_" + n]) for n in ("Wg", "Wu", "Wd"))
    i["wr1"] = f(a["L1_ffn_router_w"])
    i["rbias"] = f(a["L1_ffn_router_bias"].reshape(1, E))
    i["wsg1"], i["wsu1"], i["wsd1"] = (f(a["L1_ffn_" + n]) for n in ("sw_gate", "sw_up", "sw_down"))
    i["wg1"], i["wu1"], i["wd1"] = (f(a["L1_ffn_" + n]) for n in ("w_gate", "w_up", "w_down"))
    i["wq"], i["wo"] = f(a["L1_xattn_Wq"]), f(a["L1_xattn_Wo"])
    by_head = lambda w: f(w.reshape(-1, NH, 2, HD).transpose(0, 2, 1, 3).reshape(-1, 2 * H))
    i["wkv"] = by_head(np.concatenate([a["L1_xattn_Wk"], a["L1_xattn_Wv"]], 1))
    i["bkv"] = by_head(np.concatenate([a["L1_xattn_bk"], a["L1_xattn_bv"]]))
    i["wkvd"] = f(a["L1_xattn_Wkv_dca"])
    i["bkvd"] = f(a["L1_xattn_bkv_dca"].reshape(1, 2 * H))
    i["bq"], i["bo"] = f(a["L1_xattn_bq"].reshape(1, H)), f(a["L1_xattn_bo"].reshape(1, H))
    i["headnorm"] = f(np.stack([a["L1_xattn_" + n] for n in ("qn_w", "qn_b", "kn_w", "kn_b", "kn_dca_w", "kn_dca_b")], 1))
    return i


def kernel(**inputs):
    import concourse.bacc as bacc
    from concourse.bass_utils import run_bass_kernel_spmd

    nc = bacc.Bacc("TRN2", target_bir_lowering=False, num_devices=1)
    host = layouts({k: np.asarray(v) for k, v in inputs.items()})
    I = {k: nc.dram_tensor("in_" + k, v.shape, mybir.dt.from_np(v.dtype), kind="ExternalInput").ap()
         for k, v in host.items()}
    out = nc.dram_tensor("out_x", (T, H), F32, kind="ExternalOutput").ap()
    program(nc, I, out)
    r = run_bass_kernel_spmd(nc, [{"in_" + k: v for k, v in host.items()}], core_ids=[0])
    return r.results[0]["out_x"].reshape(B, S, H)
```
